# Optimizing a Trainium2 kernel written in Bass

```python
import numpy as np
import jax
import jax.numpy as jnp

def _softmax(x, axis=-1):
    return jax.nn.softmax(x, axis=axis)

def _gelu(x):
    return jax.nn.gelu(x, approximate=True)

def _silu(x):
    return jax.nn.silu(x)

def _sigmoid(x):
    return jax.nn.sigmoid(x)

def _layernorm(x, axis=-1, eps=1e-05):
    m = jnp.mean(x, axis=axis, keepdims=True)
    v = jnp.var(x, axis=axis, keepdims=True)
    return (x - m) / jnp.sqrt(v + eps)

def _scatter_add(tgt, idx, src, axis=0):
    return tgt.at[idx].add(src)

def _segment_sum(src, seg, n):
    return jax.ops.segment_sum(src, seg, n)
kernel_name = 'mk_lm_tower_d2_tok_ids256_r4_1a3ced'

def setup_inputs(seed: int=0):
    np.random.seed(seed)
    _w = jnp.asarray

    def _rec_inputs():
        import jax
        import jax.numpy as jnp
        _rk = jax.random.key(seed)
        x = jax.random.randint(jax.random.fold_in(_rk, 1), (8, 512), 0, 64, jnp.int32)
        return x
    x = _rec_inputs()

    def _L0_tok_setup():
        import jax, jax.numpy as jnp
        import numpy as np
        BASE = 257
        HASH_MOD = 1024
        WINDOWS = (2, 4, 8, 16)
        MATCH_OFFSETS = (1, 2, 4, 8)
        CHUNK = 32
        EPS_LN = 1e-05

        def _shift_right(x, k):
            B, T = x.shape
            return jnp.concatenate([jnp.zeros((B, k), x.dtype), x[:, :T - k]], axis=1)

        def _rolling_hashes(chars):
            c = chars.astype(jnp.int32)
            hs = []
            for w in WINDOWS:
                acc = jnp.zeros_like(c)
                p = 1
                for j in range(w):
                    acc = acc + _shift_right(c, j) * p
                    p = p * BASE % HASH_MOD
                hs.append(acc % HASH_MOD)
            return jnp.stack(hs, axis=2)

        def _match_features(chars):
            feats = []
            for k in MATCH_OFFSETS:
                m = (chars == _shift_right(chars, k)).astype(jnp.float32)
                m = m.at[:, :k].set(0.0)
                feats.append(m)
            return jnp.stack(feats, axis=-1)

        def _layer_norm(x, g, b):
            mu = jnp.mean(x, axis=-1, keepdims=True)
            var = jnp.mean((x - mu) ** 2, axis=-1, keepdims=True)
            return (x - mu) * jax.lax.rsqrt(var + EPS_LN) * g + b

        def _forward(chars, emb_byte, hash_tables, Wq, bq, conv_w, conv_b, Win, b_in, Wg, bg, Wi, bi, Wo, bo, ln_g, ln_b, mlp_w, mlp_b, Wout, bout):
            B, T = chars.shape
            byte_emb = emb_byte[chars]
            hidx = _rolling_hashes(chars)
            scale_embeds = jnp.stack([hash_tables[s][hidx[:, :, s]] for s in range(len(WINDOWS))], axis=2)
            E = scale_embeds.shape[-1]
            q = byte_emb @ Wq + bq
            scores = jnp.einsum('bte,btse->bts', q, scale_embeds) / jnp.sqrt(jnp.float32(E))
            w = jax.nn.softmax(scores, axis=-1)
            hash_feat = jnp.einsum('bts,btse->bte', w, scale_embeds)
            C = hash_feat.shape[-1]
            kk = conv_w.shape[-1]
            ht = jnp.moveaxis(hash_feat, 1, 2)
            ht = jnp.pad(ht, ((0, 0), (0, 0), (kk - 1, 0)))
            ht = jax.lax.conv_general_dilated(ht, conv_w, window_strides=(1,), padding='VALID', dimension_numbers=('NCH', 'OIH', 'NCH'), feature_group_count=C)
            hash_feat = jax.nn.silu(jnp.moveaxis(ht + conv_b[None, :, None], 2, 1))
            mf = _match_features(chars)
            feat = jnp.concatenate([byte_emb, hash_feat, mf], axis=-1)
            h = jax.nn.silu(feat @ Win + b_in)
            gates = jax.nn.sigmoid(h @ Wg + bg)
            drive = (1.0 - gates) * (h @ Wi + bi)
            S = gates.shape[-1]
            nC = T // CHUNK
            g = gates.reshape(B, nC, CHUNK, S).transpose(1, 0, 2, 3)
            d = drive.reshape(B, nC, CHUNK, S).transpose(1, 0, 2, 3)

            def step(hc, ab):
                a, b = ab
                log_a = jnp.log(jnp.maximum(a, 1e-06))
                cum_a = jnp.exp(jnp.cumsum(log_a, axis=1))
                inv = 1.0 / jnp.maximum(cum_a, 1e-08)
                cum_wb = jnp.cumsum(b * inv, axis=1)
                out = cum_a * (hc[:, None, :] + cum_wb)
                return (out[:, -1], out)
            _, states = jax.lax.scan(step, jnp.zeros((B, S), h.dtype), (g, d))
            states = states.transpose(1, 0, 2, 3).reshape(B, T, S)
            h = _layer_norm(h + states @ Wo + bo, ln_g, ln_b)
            for l in range(mlp_w.shape[0]):
                h = h + jax.nn.silu(h @ mlp_w[l] + mlp_b[l])
            return h @ Wout + bout
        key = jax.random.key(seed)
        ks = jax.random.split(key, 12)
        B, T, V = (8, 2048, 64)
        EB, E, H, SS, KC, NM, NR = (64, 64, 128, 32, 4, 4, 3)
        feat = EB + E + NM

        def lin(k, i, o):
            return (jax.random.normal(k, (i, o), jnp.float32) / np.sqrt(i)).astype(jnp.float32)
        return {'chars': jax.random.randint(ks[0], (B, T), 0, V), 'emb_byte': jax.random.normal(ks[1], (V, EB), jnp.float32) * 0.02, 'hash_tables': jax.random.normal(ks[2], (len(WINDOWS), HASH_MOD, E), jnp.float32) * 0.02, 'Wq': lin(ks[3], EB, E), 'bq': jnp.zeros((E,), jnp.float32), 'conv_w': jax.random.normal(ks[4], (E, 1, KC), jnp.float32) * 0.2, 'conv_b': jnp.zeros((E,), jnp.float32), 'Win': lin(ks[5], feat, H), 'b_in': jnp.zeros((H,), jnp.float32), 'Wg': lin(ks[6], H, SS), 'bg': jnp.zeros((SS,), jnp.float32), 'Wi': lin(ks[7], H, SS), 'bi': jnp.zeros((SS,), jnp.float32), 'Wo': lin(ks[8], SS, H), 'bo': jnp.zeros((H,), jnp.float32), 'ln_g': jnp.ones((H,), jnp.float32), 'ln_b': jnp.zeros((H,), jnp.float32), 'mlp_w': jax.random.normal(ks[9], (NR, H, H), jnp.float32) / np.sqrt(H), 'mlp_b': jnp.zeros((NR, H), jnp.float32), 'Wout': lin(ks[10], H, V), 'bout': jnp.zeros((V,), jnp.float32)}
    _L0_tok_all = _L0_tok_setup()
    _L0_tok_in = {k: v for k, v in _L0_tok_all.items() if k in ('emb_byte', 'hash_tables', 'Wq', 'bq', 'conv_w', 'conv_b', 'Win', 'b_in', 'Wg', 'bg', 'Wi', 'bi', 'Wo', 'bo', 'ln_g', 'ln_b', 'mlp_w', 'mlp_b', 'Wout', 'bout')}
    del _L0_tok_all

    def _L0_attn_setup():
        import jax, jax.numpy as jnp
        import numpy as np
        import math
        B, T, D = (4, 256, 64)
        H = 4
        DH = D // H
        SHIFTS = (0, 4, 8, 12)
        WINDOW = 64
        key = jax.random.key(seed)
        ks = jax.random.split(key, 9)
        sc = 1.0 / math.sqrt(D)
        return {'x': jax.random.normal(ks[0], (B, T, D), jnp.float32), 'Wq': jax.random.normal(ks[1], (D, D), jnp.float32) * sc, 'bq': jnp.zeros((D,), jnp.float32), 'Wk': jax.random.normal(ks[2], (D, D), jnp.float32) * sc, 'bk': jnp.zeros((D,), jnp.float32), 'Wv': jax.random.normal(ks[3], (D, D), jnp.float32) * sc, 'bv': jnp.zeros((D,), jnp.float32), 'Wo': jax.random.normal(ks[4], (D, D), jnp.float32) * sc, 'bo': jnp.zeros((D,), jnp.float32), 'shift_logits': jnp.zeros((H, len(SHIFTS)), jnp.float32), 'alibi_slope': jnp.ones((H,), jnp.float32) * 0.01}
    _L0_attn_all = _L0_attn_setup()
    _L0_attn_in = {k: v for k, v in _L0_attn_all.items() if k in ('Wq', 'bq', 'Wk', 'bk', 'Wv', 'bv', 'Wo', 'bo', 'shift_logits', 'alibi_slope')}
    del _L0_attn_all

    def _L0_ffn_setup():
        import jax, jax.numpy as jnp
        import numpy as np
        C = 64
        HID = 256
        E = 8
        TEMP = 1.0
        key = jax.random.key(seed)
        ks = jax.random.split(key, 7)
        x = jax.random.normal(ks[0], (8, 4096, C), dtype=jnp.float32)
        W1 = jax.random.normal(ks[1], (C, HID), dtype=jnp.float32) * 0.02
        b1 = jnp.zeros((HID,), dtype=jnp.float32)
        Wg = jax.random.normal(ks[2], (HID, E), dtype=jnp.float32) * 0.02
        bg = jnp.zeros((E,), dtype=jnp.float32)
        Wd = jax.random.normal(ks[3], (E, HID, C), dtype=jnp.float32) * 0.02
        bd = jnp.zeros((E, C), dtype=jnp.float32)
        return {'x': x, 'W1': W1, 'b1': b1, 'Wg': Wg, 'bg': bg, 'Wd': Wd, 'bd': bd}
    _L0_ffn_all = _L0_ffn_setup()
    _L0_ffn_in = {k: v for k, v in _L0_ffn_all.items() if k in ('W1', 'b1', 'Wg', 'bg', 'Wd', 'bd')}
    del _L0_ffn_all

    def _L1_attn_setup():
        import jax, jax.numpy as jnp
        import numpy as np
        B, N, D, H = (4, 256, 64, 8)
        key = jax.random.key(seed)
        k1, k2, k3 = jax.random.split(key, 3)
        x = jax.random.normal(k1, (B, N, D), dtype=jnp.float32)
        Wqkv = jax.random.normal(k2, (D, 3 * D * H), dtype=jnp.float32) * 0.02
        bqkv = jnp.zeros((3 * D * H,), dtype=jnp.float32)
        W0 = jax.random.normal(k3, (D * H, D), dtype=jnp.float32) * 0.02
        b0 = jnp.zeros((D,), dtype=jnp.float32)
        return {'x': x, 'Wqkv': Wqkv, 'bqkv': bqkv, 'W0': W0, 'b0': b0}
    _L1_attn_all = _L1_attn_setup()
    _L1_attn_in = {k: v for k, v in _L1_attn_all.items() if k in ('Wqkv', 'bqkv', 'W0', 'b0')}
    del _L1_attn_all

    def _L1_ffn_setup():
        import jax, jax.numpy as jnp
        import numpy as np
        DIM = 64
        HEADS = 8
        NUM_KEYS = 64
        NUM_KV = NUM_KEYS ** 2
        PK_TOPK = 16
        FINAL_TOPK = 16
        DIM_KEY = DIM // 2
        P = 2

        def _pk(x, Wq_pk, pk_keys):
            b, n, _ = x.shape
            q = (x @ Wq_pk).reshape(b, n, P, HEADS, DIM_KEY).transpose(2, 0, 1, 3, 4)
            sim = jnp.einsum('pbnhd,pkhd->pbnhk', q, pk_keys)
            scores, idx = jax.lax.top_k(sim, PK_TOPK)
            idx0 = idx[0]
            idx1 = idx[1] * NUM_KEYS
            index = (idx0[..., :, None] + idx1[..., None, :]).reshape(b, n, HEADS, PK_TOPK * PK_TOPK)
            score = (scores[0][..., :, None] + scores[1][..., None, :]).reshape(b, n, HEADS, PK_TOPK * PK_TOPK)
            final_scores, pk_idx = jax.lax.top_k(score, FINAL_TOPK)
            final_indices = jnp.take_along_axis(index, pk_idx, axis=-1)
            final_scores = jax.nn.softmax(final_scores, axis=-1)
            return (final_scores, final_indices)
        key = jax.random.key(seed)
        ks = jax.random.split(key, 7)
        b, n = (2, 256)
        std = 0.02
        x = jax.random.normal(ks[0], (b, n, DIM), dtype=jnp.float32)
        Wq_pk = jax.random.normal(ks[1], (DIM, P * HEADS * DIM_KEY), dtype=jnp.float32) * std
        pk_keys = jax.random.normal(ks[2], (P, NUM_KEYS, HEADS, DIM_KEY), dtype=jnp.float32) * std
        Wq = jax.random.normal(ks[3], (DIM, HEADS * DIM), dtype=jnp.float32) * std
        keys_table = jax.random.normal(ks[4], (NUM_KV * HEADS, DIM), dtype=jnp.float32) * std
        values_table = jax.random.normal(ks[5], (NUM_KV * HEADS, DIM), dtype=jnp.float32) * std
        Wo = jax.random.normal(ks[6], (DIM * HEADS, DIM), dtype=jnp.float32) * std
        return {'x': x, 'Wq_pk': Wq_pk, 'pk_keys': pk_keys, 'Wq': Wq, 'keys_table': keys_table, 'values_table': values_table, 'Wo': Wo}
    _L1_ffn_all = _L1_ffn_setup()
    _L1_ffn_in = {k: v for k, v in _L1_ffn_all.items() if k in ('Wq_pk', 'pk_keys', 'Wq', 'keys_table', 'values_table', 'Wo')}
    del _L1_ffn_all
    return {'x': x, 'L0_tok_emb_byte': _L0_tok_in['emb_byte'], 'L0_tok_hash_tables': _L0_tok_in['hash_tables'], 'L0_tok_Wq': _L0_tok_in['Wq'], 'L0_tok_bq': _L0_tok_in['bq'], 'L0_tok_conv_w': _L0_tok_in['conv_w'], 'L0_tok_conv_b': _L0_tok_in['conv_b'], 'L0_tok_Win': _L0_tok_in['Win'], 'L0_tok_b_in': _L0_tok_in['b_in'], 'L0_tok_Wg': _L0_tok_in['Wg'], 'L0_tok_bg': _L0_tok_in['bg'], 'L0_tok_Wi': _L0_tok_in['Wi'], 'L0_tok_bi': _L0_tok_in['bi'], 'L0_tok_Wo': _L0_tok_in['Wo'], 'L0_tok_bo': _L0_tok_in['bo'], 'L0_tok_ln_g': _L0_tok_in['ln_g'], 'L0_tok_ln_b': _L0_tok_in['ln_b'], 'L0_tok_mlp_w': _L0_tok_in['mlp_w'], 'L0_tok_mlp_b': _L0_tok_in['mlp_b'], 'L0_tok_Wout': _L0_tok_in['Wout'], 'L0_tok_bout': _L0_tok_in['bout'], 'L0_attn_Wq': _L0_attn_in['Wq'], 'L0_attn_bq': _L0_attn_in['bq'], 'L0_attn_Wk': _L0_attn_in['Wk'], 'L0_attn_bk': _L0_attn_in['bk'], 'L0_attn_Wv': _L0_attn_in['Wv'], 'L0_attn_bv': _L0_attn_in['bv'], 'L0_attn_Wo': _L0_attn_in['Wo'], 'L0_attn_bo': _L0_attn_in['bo'], 'L0_attn_shift_logits': _L0_attn_in['shift_logits'], 'L0_attn_alibi_slope': _L0_attn_in['alibi_slope'], 'L0_ffn_W1': _L0_ffn_in['W1'], 'L0_ffn_b1': _L0_ffn_in['b1'], 'L0_ffn_Wg': _L0_ffn_in['Wg'], 'L0_ffn_bg': _L0_ffn_in['bg'], 'L0_ffn_Wd': _L0_ffn_in['Wd'], 'L0_ffn_bd': _L0_ffn_in['bd'], 'L1_attn_Wqkv': _L1_attn_in['Wqkv'], 'L1_attn_bqkv': _L1_attn_in['bqkv'], 'L1_attn_W0': _L1_attn_in['W0'], 'L1_attn_b0': _L1_attn_in['b0'], 'L1_ffn_Wq_pk': _L1_ffn_in['Wq_pk'], 'L1_ffn_pk_keys': _L1_ffn_in['pk_keys'], 'L1_ffn_Wq': _L1_ffn_in['Wq'], 'L1_ffn_keys_table': _L1_ffn_in['keys_table'], 'L1_ffn_values_table': _L1_ffn_in['values_table'], 'L1_ffn_Wo': _L1_ffn_in['Wo']}

def reference(x, L0_tok_emb_byte, L0_tok_hash_tables, L0_tok_Wq, L0_tok_bq, L0_tok_conv_w, L0_tok_conv_b, L0_tok_Win, L0_tok_b_in, L0_tok_Wg, L0_tok_bg, L0_tok_Wi, L0_tok_bi, L0_tok_Wo, L0_tok_bo, L0_tok_ln_g, L0_tok_ln_b, L0_tok_mlp_w, L0_tok_mlp_b, L0_tok_Wout, L0_tok_bout, L0_attn_Wq, L0_attn_bq, L0_attn_Wk, L0_attn_bk, L0_attn_Wv, L0_attn_bv, L0_attn_Wo, L0_attn_bo, L0_attn_shift_logits, L0_attn_alibi_slope, L0_ffn_W1, L0_ffn_b1, L0_ffn_Wg, L0_ffn_bg, L0_ffn_Wd, L0_ffn_bd, L1_attn_Wqkv, L1_attn_bqkv, L1_attn_W0, L1_attn_b0, L1_ffn_Wq_pk, L1_ffn_pk_keys, L1_ffn_Wq, L1_ffn_keys_table, L1_ffn_values_table, L1_ffn_Wo):
    import jax
    import jax.numpy as jnp

    def _L0_tok_ref(chars, emb_byte, hash_tables, Wq, bq, conv_w, conv_b, Win, b_in, Wg, bg, Wi, bi, Wo, bo, ln_g, ln_b, mlp_w, mlp_b, Wout, bout):
        import jax, jax.numpy as jnp
        import numpy as np
        BASE = 257
        HASH_MOD = 1024
        WINDOWS = (2, 4, 8, 16)
        MATCH_OFFSETS = (1, 2, 4, 8)
        CHUNK = 32
        EPS_LN = 1e-05

        def _shift_right(x, k):
            B, T = x.shape
            return jnp.concatenate([jnp.zeros((B, k), x.dtype), x[:, :T - k]], axis=1)

        def _rolling_hashes(chars):
            c = chars.astype(jnp.int32)
            hs = []
            for w in WINDOWS:
                acc = jnp.zeros_like(c)
                p = 1
                for j in range(w):
                    acc = acc + _shift_right(c, j) * p
                    p = p * BASE % HASH_MOD
                hs.append(acc % HASH_MOD)
            return jnp.stack(hs, axis=2)

        def _match_features(chars):
            feats = []
            for k in MATCH_OFFSETS:
                m = (chars == _shift_right(chars, k)).astype(jnp.float32)
                m = m.at[:, :k].set(0.0)
                feats.append(m)
            return jnp.stack(feats, axis=-1)

        def _layer_norm(x, g, b):
            mu = jnp.mean(x, axis=-1, keepdims=True)
            var = jnp.mean((x - mu) ** 2, axis=-1, keepdims=True)
            return (x - mu) * jax.lax.rsqrt(var + EPS_LN) * g + b

        def _forward(chars, emb_byte, hash_tables, Wq, bq, conv_w, conv_b, Win, b_in, Wg, bg, Wi, bi, Wo, bo, ln_g, ln_b, mlp_w, mlp_b, Wout, bout):
            B, T = chars.shape
            byte_emb = emb_byte[chars]
            hidx = _rolling_hashes(chars)
            scale_embeds = jnp.stack([hash_tables[s][hidx[:, :, s]] for s in range(len(WINDOWS))], axis=2)
            E = scale_embeds.shape[-1]
            q = byte_emb @ Wq + bq
            scores = jnp.einsum('bte,btse->bts', q, scale_embeds) / jnp.sqrt(jnp.float32(E))
            w = jax.nn.softmax(scores, axis=-1)
            hash_feat = jnp.einsum('bts,btse->bte', w, scale_embeds)
            C = hash_feat.shape[-1]
            kk = conv_w.shape[-1]
            ht = jnp.moveaxis(hash_feat, 1, 2)
            ht = jnp.pad(ht, ((0, 0), (0, 0), (kk - 1, 0)))
            ht = jax.lax.conv_general_dilated(ht, conv_w, window_strides=(1,), padding='VALID', dimension_numbers=('NCH', 'OIH', 'NCH'), feature_group_count=C)
            hash_feat = jax.nn.silu(jnp.moveaxis(ht + conv_b[None, :, None], 2, 1))
            mf = _match_features(chars)
            feat = jnp.concatenate([byte_emb, hash_feat, mf], axis=-1)
            h = jax.nn.silu(feat @ Win + b_in)
            gates = jax.nn.sigmoid(h @ Wg + bg)
            drive = (1.0 - gates) * (h @ Wi + bi)
            S = gates.shape[-1]
            nC = T // CHUNK
            g = gates.reshape(B, nC, CHUNK, S).transpose(1, 0, 2, 3)
            d = drive.reshape(B, nC, CHUNK, S).transpose(1, 0, 2, 3)

            def step(hc, ab):
                a, b = ab
                log_a = jnp.log(jnp.maximum(a, 1e-06))
                cum_a = jnp.exp(jnp.cumsum(log_a, axis=1))
                inv = 1.0 / jnp.maximum(cum_a, 1e-08)
                cum_wb = jnp.cumsum(b * inv, axis=1)
                out = cum_a * (hc[:, None, :] + cum_wb)
                return (out[:, -1], out)
            _, states = jax.lax.scan(step, jnp.zeros((B, S), h.dtype), (g, d))
            states = states.transpose(1, 0, 2, 3).reshape(B, T, S)
            h = _layer_norm(h + states @ Wo + bo, ln_g, ln_b)
            for l in range(mlp_w.shape[0]):
                h = h + jax.nn.silu(h @ mlp_w[l] + mlp_b[l])
            return h @ Wout + bout
        return _forward(chars, emb_byte, hash_tables, Wq, bq, conv_w, conv_b, Win, b_in, Wg, bg, Wi, bi, Wo, bo, ln_g, ln_b, mlp_w, mlp_b, Wout, bout)

    def _L0_attn_ref(x, Wq, bq, Wk, bk, Wv, bv, Wo, bo, shift_logits, alibi_slope):
        import jax, jax.numpy as jnp
        import numpy as np
        import math
        B, T, D = (4, 256, 64)
        H = 4
        DH = D // H
        SHIFTS = (0, 4, 8, 12)
        WINDOW = 64
        Bt, Tt, Dd = x.shape

        def split(y):
            return y.reshape(Bt, Tt, H, DH).transpose(0, 2, 1, 3)
        q = split(x @ Wq.T + bq)
        k0 = split(x @ Wk.T + bk)
        v0 = split(x @ Wv.T + bv)

        def shift_time(t, s):
            if s == 0:
                return t
            return jnp.pad(t[:, :, :Tt - s, :], ((0, 0), (0, 0), (s, 0), (0, 0)))
        K = jnp.stack([shift_time(k0, s) for s in SHIFTS], axis=2)
        V = jnp.stack([shift_time(v0, s) for s in SHIFTS], axis=2)
        qn = q / math.sqrt(DH)
        att = jnp.einsum('bhtd,bhskd->bhstk', qn, K)
        pos = jnp.arange(Tt)
        rel = pos[None, :] - pos[:, None]
        dist = jnp.clip(rel, 0, None).astype(att.dtype)
        alibi = -alibi_slope[:, None, None] * dist
        if WINDOW is not None and WINDOW < Tt:
            keep = (rel >= 0) & (rel < WINDOW)
            mask = jnp.where(keep, 0.0, -10000.0).astype(att.dtype)
            att = att + mask[None, None, None]
        att = att + alibi[None, :, None]
        pi = jax.nn.softmax(shift_logits, axis=-1)
        att = att + jnp.log(pi + 1e-08)[None, :, :, None, None]
        att = jax.scipy.special.logsumexp(att, axis=2)
        p = jax.nn.softmax(att, axis=-1)
        ctx = jnp.einsum('bhtk,bhskd->bhtd', p, V)
        out = ctx.transpose(0, 2, 1, 3).reshape(Bt, Tt, H * DH)
        return out @ Wo.T + bo

    def _L0_ffn_ref(x, W1, b1, Wg, bg, Wd, bd):
        import jax, jax.numpy as jnp
        import numpy as np
        C = 64
        HID = 256
        E = 8
        TEMP = 1.0
        orig_shape = x.shape
        xf = x.reshape(-1, orig_shape[-1])
        H = jax.nn.gelu(xf @ W1 + b1, approximate=False)
        probs = jax.nn.softmax((H @ Wg + bg) / TEMP, axis=-1)
        assign = jnp.argmax(probs, axis=-1)
        out = jnp.zeros_like(xf)
        for e in range(Wd.shape[0]):
            y = H @ Wd[e] + bd[e]
            sel = (assign == e)[:, None]
            out = out + jnp.where(sel, probs[:, e:e + 1] * y, 0.0)
        return out.reshape(orig_shape)

    def _L1_attn_ref(x, Wqkv, bqkv, W0, b0):
        import jax, jax.numpy as jnp
        import numpy as np
        B, N, D, H = (4, 256, 64, 8)
        b, n, d = x.shape
        h = Wqkv.shape[1] // (3 * d)
        qkv = x @ Wqkv + bqkv
        q, k, v = jnp.reshape(qkv, (3, b, n, d, h))
        score = jnp.einsum('bnqh,btqh->bnth', q, k) * d ** (-0.5)
        attn = jax.nn.softmax(score, axis=1)
        av = jnp.einsum('bnnh,bnqh->bnqh', attn, v)
        out = av.reshape(b, n, d * h) @ W0 + b0
        return out

    def _L1_ffn_ref(x, Wq_pk, pk_keys, Wq, keys_table, values_table, Wo):
        import jax, jax.numpy as jnp
        import numpy as np
        DIM = 64
        HEADS = 8
        NUM_KEYS = 64
        NUM_KV = NUM_KEYS ** 2
        PK_TOPK = 16
        FINAL_TOPK = 16
        DIM_KEY = DIM // 2
        P = 2

        def _pk(x, Wq_pk, pk_keys):
            b, n, _ = x.shape
            q = (x @ Wq_pk).reshape(b, n, P, HEADS, DIM_KEY).transpose(2, 0, 1, 3, 4)
            sim = jnp.einsum('pbnhd,pkhd->pbnhk', q, pk_keys)
            scores, idx = jax.lax.top_k(sim, PK_TOPK)
            idx0 = idx[0]
            idx1 = idx[1] * NUM_KEYS
            index = (idx0[..., :, None] + idx1[..., None, :]).reshape(b, n, HEADS, PK_TOPK * PK_TOPK)
            score = (scores[0][..., :, None] + scores[1][..., None, :]).reshape(b, n, HEADS, PK_TOPK * PK_TOPK)
            final_scores, pk_idx = jax.lax.top_k(score, FINAL_TOPK)
            final_indices = jnp.take_along_axis(index, pk_idx, axis=-1)
            final_scores = jax.nn.softmax(final_scores, axis=-1)
            return (final_scores, final_indices)
        b, n, d = x.shape
        q = (x @ Wq).reshape(b, n, HEADS, DIM) * DIM ** (-0.5)
        kv_scores, indices = _pk(x, Wq_pk, pk_keys)
        offsets = jnp.arange(HEADS, dtype=indices.dtype) * NUM_KV
        ind = indices + offsets[None, None, :, None]
        k = jnp.einsum('bnhk,bnhkd->bnhd', kv_scores, keys_table[ind])
        v = jnp.einsum('bnhk,bnhkd->bnhd', kv_scores, values_table[ind])
        sim = jnp.einsum('bihd,bjhd->bhij', q, k)
        neg = -jnp.finfo(sim.dtype).max
        causal = jnp.tril(jnp.ones((n, n), dtype=bool))
        sim = jnp.where(causal, sim, neg)
        attn = jax.nn.softmax(sim, axis=-1)
        out = jnp.einsum('bhij,bjhd->bhid', attn, v)
        out = out.transpose(0, 2, 1, 3).reshape(b, n, HEADS * DIM)
        return out @ Wo
    h = _L0_tok_ref(x, L0_tok_emb_byte, L0_tok_hash_tables, L0_tok_Wq, L0_tok_bq, L0_tok_conv_w, L0_tok_conv_b, L0_tok_Win, L0_tok_b_in, L0_tok_Wg, L0_tok_bg, L0_tok_Wi, L0_tok_bi, L0_tok_Wo, L0_tok_bo, L0_tok_ln_g, L0_tok_ln_b, L0_tok_mlp_w, L0_tok_mlp_b, L0_tok_Wout, L0_tok_bout)
    h = h + _L0_attn_ref(_layernorm(h, axis=-1), L0_attn_Wq, L0_attn_bq, L0_attn_Wk, L0_attn_bk, L0_attn_Wv, L0_attn_bv, L0_attn_Wo, L0_attn_bo, L0_attn_shift_logits, L0_attn_alibi_slope)
    h = h + _L0_ffn_ref(_layernorm(h, axis=-1), L0_ffn_W1, L0_ffn_b1, L0_ffn_Wg, L0_ffn_bg, L0_ffn_Wd, L0_ffn_bd)
    h = h + _L1_attn_ref(_layernorm(h, axis=-1), L1_attn_Wqkv, L1_attn_bqkv, L1_attn_W0, L1_attn_b0)
    h = h + _L1_ffn_ref(_layernorm(h, axis=-1), L1_ffn_Wq_pk, L1_ffn_pk_keys, L1_ffn_Wq, L1_ffn_keys_table, L1_ffn_values_table, L1_ffn_Wo)
    return h

_drawn_inputs = setup_inputs


def setup_inputs(seed=0):
    import zlib

    import numpy as np

    out = dict(_drawn_inputs(seed))
    spreads = {'L0_tok_bq': (0.0, 0.8),
     'L0_tok_conv_b': (0.0, 0.1),
     'L0_tok_b_in': (0.0, 0.1),
     'L0_tok_bg': (0.0, 0.1),
     'L0_tok_bi': (0.0, 0.1),
     'L0_tok_bo': (0.0, 0.1),
     'L0_tok_ln_g': (1.0, 0.2),
     'L0_tok_ln_b': (0.0, 0.1),
     'L0_tok_mlp_b': (0.0, 0.1),
     'L0_tok_bout': (0.0, 0.1),
     'L0_attn_bq': (0.0, 0.8),
     'L0_attn_bk': (0.0, 2.0),
     'L0_attn_bv': (0.0, 0.1),
     'L0_attn_bo': (0.0, 0.366),
     'L0_attn_shift_logits': (0.0, 2.0),
     'L0_attn_alibi_slope': (0.009999999776482582, 0.6),
     'L0_ffn_b1': (0.0, 0.8),
     'L0_ffn_bg': (0.0, 0.8),
     'L0_ffn_bd': (0.0, 0.8),
     'L1_attn_bqkv': (0.0, 2.0),
     'L1_attn_b0': (0.0, 0.379)}
    factors = {'L0_tok_hash_tables': 8.0,
     'L0_tok_Wq': 27.069,
     'L0_tok_conv_w': 8.0,
     'L0_attn_Wq': 8.0,
     'L0_attn_Wk': 6.584,
     'L0_ffn_W1': 8.0,
     'L0_ffn_Wg': 8.0,
     'L0_ffn_Wd': 8.0,
     'L1_attn_Wqkv': 64.0,
     'L1_attn_W0': 64.0,
     'L1_ffn_Wq_pk': 8.0,
     'L1_ffn_pk_keys': 8.0,
     'L1_ffn_Wq': 200.0,
     'L1_ffn_keys_table': 200.0,
     'L1_ffn_values_table': 8.0,
     'L1_ffn_Wo': 8.0}
    for name, (base, spread) in spreads.items():
        noise = np.random.default_rng([zlib.crc32(name.encode()), seed]).standard_normal(out[name].shape)
        drawn = base * np.exp(spread * noise) if base else spread * noise
        out[name] = jnp.asarray(drawn.astype(out[name].dtype))
    for name, factor in factors.items():
        out[name] = (out[name] * factor).astype(out[name].dtype)
    return out
```

```python
from contextlib import ExitStack

import concourse.bass as bass
from concourse import mybir

F32 = mybir.dt.float32
BF16 = mybir.dt.bfloat16
I32 = mybir.dt.int32
U32 = mybir.dt.uint32
ALU = mybir.AluOpType
ACT = mybir.ActivationFunctionType
AX = mybir.AxisListType

P = 128
D = 64
B, T = 8, 512
NTOK = B * T
TT = T // P
EPS = 1e-5


class Steps:

    def __init__(self, eng, sem):
        self.eng, self.sem, self.n = eng, sem, 0

    def did(self, ins):
        ins.then_inc(self.sem, 1)
        self.n += 1
        return self.n

    def wait(self, n=None):
        self.eng.wait_ge(self.sem, self.n if n is None else n)

    def restart(self):
        self.wait()
        self.eng.sem_clear(self.sem)
        self.n = 0


def held(eng, sem, value, passed):
    eng.wait_ge(sem, value)
    eng.sem_inc(passed, 1)


def bc(ap, axis, n):
    a = ap.unsqueeze(axis)
    shape = list(a.shape)
    shape[axis] = n
    return a.broadcast_to(shape)


def ln_moments(dve, s, x, stats, moments):
    for t in range(TT):
        s.did(dve.bn_stats(stats[:, t, :], x[:, t, :]))
    s.wait()
    for t in range(TT):
        s.did(dve.bn_aggr(moments[:, t, :], stats[:, t, :]))
    s.wait()


def ln_apply(dve, s, xn, x, moments, std):
    s.did(dve.reciprocal(std[:, :], std[:, :]))
    s.wait()
    for t in range(TT):
        ins = dve.tensor_scalar(xn[:, t, :], x[:, t, :], moments[:, t, 0:1], std[:, t:t + 1], ALU.subtract, ALU.mult)
        if t < TT - 1:
            s.did(ins)
    return ins


def clear_semaphores(nc, sems):
    with nc.Block() as block:
        @block.sync
        def _(sp):
            for one in sems:
                sp.sem_clear(one)
E_TOK, H_TOK, S_TOK, KC, NM, NR = 64, 128, 32, 4, 4, 3
VOCAB, BASE, HASH_MOD = 64, 257, 1024
WINDOWS, MATCH_OFFSETS = (2, 4, 8, 16), (1, 2, 4, 8)
NW, WMAX, CHUNK = len(WINDOWS), 16, 32
NCH = T // CHUNK


def pad_chars(nc, x, xpad):
    with ExitStack() as ctx:
        fill = ctx.enter_context(nc.sbuf_tensor("pad_fill", [B, WMAX], I32))
        filled = ctx.enter_context(nc.semaphore("pad_filled"))
        written = ctx.enter_context(nc.semaphore("pad_written"))
        copied = ctx.enter_context(nc.semaphore("pad_copied"))
        with nc.Block() as block:
            @block.vector
            def _(dve):
                dve.memset(fill[:, :], -1).then_inc(filled, 1)

            @block.sync
            def _(sp):
                sp.dma_start(xpad[:, WMAX:WMAX + T], x).then_inc(copied, 16)
                sp.wait_ge(filled, 1)
                sp.dma_start(xpad[:, 0:WMAX], fill[:, :]).then_inc(written, 16)
                sp.wait_ge(copied, 16)
                sp.wait_ge(written, 16)

        clear_semaphores(nc, [filled, written, copied])


def tower_tok(nc, w, x, xpad, h_out):
    with ExitStack() as ctx:
        def sb(name, shape, dt=F32):
            return ctx.enter_context(nc.sbuf_tensor("tok_" + name, shape, dt))

        def ps(name, shape):
            return ctx.enter_context(nc.psum_tensor("tok_" + name, shape, F32))

        sems = []

        def sem(name):
            sems.append(ctx.enter_context(nc.semaphore("tok_" + name)))
            return sems[-1]

        embT = sb("embT", [E_TOK, VOCAB])
        wq = sb("wq", [E_TOK, E_TOK])
        bq = sb("bq", [1, E_TOK])
        conv_w = sb("conv_w", [E_TOK, KC])
        conv_b = sb("conv_b", [E_TOK, 1])
        win_byte = sb("win_byte", [E_TOK, H_TOK])
        win_hash = sb("win_hash", [E_TOK, H_TOK])
        win_match = sb("win_match", [NM, H_TOK])
        b_in = sb("b_in", [H_TOK, 1])
        wg = sb("wg", [H_TOK, S_TOK])
        bg = sb("bg", [S_TOK, 1])
        wi = sb("wi", [H_TOK, S_TOK])
        bi = sb("bi", [S_TOK, 1])
        woT = sb("woT", [H_TOK, S_TOK])
        bo = sb("bo", [H_TOK, 1])
        ln_g = sb("ln_g", [H_TOK, 1])
        ln_b = sb("ln_b", [H_TOK, 1])
        mlp_w = sb("mlp_w", [H_TOK, NR, H_TOK])
        mlp_b = sb("mlp_b", [H_TOK, NR])
        wout = sb("wout", [H_TOK, D])
        bout = sb("bout", [1, D])
        q_table = sb("q_table", [VOCAB, E_TOK])
        in_table = sb("in_table", [VOCAB, H_TOK])
        wo_centred = sb("wo_centred", [S_TOK, H_TOK])
        bo_centred = sb("bo_centred", [H_TOK, 1])
        ident = sb("ident", [P, P])
        centre = sb("centre", [P, P])
        mean_all = sb("mean_all", [P, P])
        ones_row = sb("ones_row", [1, P])
        eps = sb("eps", [P, 1])
        vocab_id_i = sb("vocab_id_i", [VOCAB, 1], I32)
        vocab_id = sb("vocab_id", [VOCAB, 1])
        in_chunk = sb("in_chunk", [S_TOK, T])
        chunk_start = sb("chunk_start", [S_TOK, T])
        powers = sb("powers", [P, WMAX])
        table_base = sb("table_base", [P, NW], I32)
        windows = sb("windows", [P, B * TT, WMAX], I32)
        windows_f = sb("windows_f", [P, B * TT, WMAX])
        hash_sum = sb("hash_sum", [P, B * TT, NW])
        hash_idx = sb("hash_idx", [P, B * TT, NW], I32)
        loaded, gp_made, dve_made, pe_made = sem("loaded"), sem("gp_made"), sem("dve_made"), sem("pe_made")
        windows_loaded = sem("windows_loaded")
        psw = ps("psw", [P, 512])
        WEIGHTS = [(embT, w["emb_byteT"]), (wq, w["Wq"]), (bq, w["bq"].unsqueeze(0)),
                   (conv_w, w["conv_w"].rearrange("c a k -> c (a k)")), (conv_b, w["conv_b"].unsqueeze(1)),
                   (win_byte, w["Win"][0:E_TOK, :]), (win_hash, w["Win"][E_TOK:2 * E_TOK, :]),
                   (win_match, w["Win"][2 * E_TOK:2 * E_TOK + NM, :]), (b_in, w["b_in"].unsqueeze(1)),
                   (wg, w["Wg"]), (bg, w["bg"].unsqueeze(1)), (wi, w["Wi"]), (bi, w["bi"].unsqueeze(1)),
                   (woT, w["WoT"]), (bo, w["bo"].unsqueeze(1)), (ln_g, w["ln_g"].unsqueeze(1)),
                   (ln_b, w["ln_b"].unsqueeze(1)), (wout, w["Wout"]), (bout, w["bout"].unsqueeze(0)),
                   (mlp_b, w["mlp_bT"])]

        with nc.Block() as block:
            @block.sync
            def _(sp):
                for b in range(B):
                    src = bass.AP(xpad.tensor, xpad.offset + b * (WMAX + T) + 1, [[1, P], [P, TT], [1, WMAX]])
                    sp.dma_start(windows[:, b * TT:(b + 1) * TT, :], src).then_inc(windows_loaded, 16)
                for dst, src in WEIGHTS:
                    sp.dma_start(dst[:, :], src).then_inc(loaded, 16)
                sp.dma_start(mlp_w[:, :, :], w["mlp_w"].rearrange("l i o -> i l o")).then_inc(loaded, 16)

            @block.gpsimd
            def _(pool):
                pool.iota(vocab_id_i[:, :], [[0, 1]], base=0, channel_multiplier=1).then_inc(gp_made, 1)
                pool.iota(table_base[:, :], [[HASH_MOD, NW]], base=0, channel_multiplier=0).then_inc(gp_made, 1)
                pool.memset(ident[:, :], 0.0).then_inc(gp_made, 1)
                pool.wait_ge(gp_made, 3)
                pool.affine_select(out=ident[:, :], in_=ident[:, :], compare_op=ALU.not_equal, fill=1.0, base=0,
                                   pattern=[[-1, P]], channel_multiplier=1).then_inc(gp_made, 1)

            @block.vector
            def _(dve):
                s = Steps(dve, dve_made)
                s.did(dve.memset(mean_all[:, :], 1.0 / H_TOK))
                s.did(dve.memset(ones_row[:, :], 1.0))
                s.did(dve.memset(eps[:, :], EPS))
                s.did(dve.memset(in_chunk[:, :], 1.0))
                s.did(dve.memset(chunk_start[:, :], 0.0))
                power = 1
                for j in range(WMAX):
                    s.did(dve.memset(powers[:, WMAX - 1 - j:WMAX - j], float(power)))
                    power = power * BASE % HASH_MOD
                s.wait()
                s.did(dve.memset(in_chunk[:, 0:T:CHUNK], 0.0))
                s.did(dve.memset(chunk_start[:, 0:T:CHUNK], 1.0))
                dve.wait_ge(gp_made, 4)
                s.did(dve.tensor_copy(vocab_id[:, :], vocab_id_i[:, :]))
                s.did(dve.tensor_tensor(centre[:, :], ident[:, :], mean_all[:, :], ALU.subtract))
                dve.wait_ge(windows_loaded, 16 * B)
                s.did(dve.tensor_scalar(windows_f[:, :, :], windows[:, :, :], 0.0, None, ALU.max))
                s.wait()
                s.did(dve.tensor_tensor(windows_f[:, :, :], windows_f[:, :, :], bc(powers[:, :], 1, B * TT), ALU.mult))
                s.wait()
                for n, width in enumerate(WINDOWS):
                    s.did(dve.tensor_reduce(hash_sum[:, :, n], windows_f[:, :, WMAX - width:WMAX], AX.X, ALU.add))
                s.wait()
                s.did(dve.tensor_copy(hash_idx[:, :, :], hash_sum[:, :, :]))
                s.wait()
                s.did(dve.tensor_scalar(hash_idx[:, :, :], hash_idx[:, :, :], HASH_MOD - 1, None, ALU.bitwise_and))
                s.wait()
                s.did(dve.tensor_tensor(hash_idx[:, :, :], hash_idx[:, :, :], bc(table_base[:, :], 1, B * TT), ALU.add))
                dve.wait_ge(pe_made, 1)
                s.did(dve.tensor_copy(q_table[:, :], psw[0:VOCAB, 0:E_TOK]))
                s.did(dve.tensor_copy(in_table[:, :], psw[0:VOCAB, 64:192]))
                s.did(dve.tensor_copy(wo_centred[:, :], psw[0:S_TOK, 192:320]))
                s.did(dve.tensor_copy(bo_centred[:, :], psw[:, 320:321]))
                s.wait()

            @block.tensor
            def _(pe):
                pe.wait_ge(loaded, 16 * (len(WEIGHTS) + 1))
                pe.wait_ge(dve_made, 5 + WMAX + 4)
                pe.matmul(psw[0:VOCAB, 0:E_TOK], embT[:, :], wq[:, :], start=True, stop=False)
                pe.matmul(psw[0:VOCAB, 0:E_TOK], ones_row[:, 0:VOCAB], bq[:, :], start=False, stop=True)
                pe.matmul(psw[0:VOCAB, 64:192], embT[:, :], win_byte[:, :], start=True, stop=True)
                pe.matmul(psw[0:S_TOK, 192:320], woT[:, :], centre[:, :], start=True, stop=True)
                pe.matmul(psw[:, 320:321], centre[:, :], bo[:, :], start=True, stop=True).then_inc(pe_made, 1)

        R = range(2)
        chars = sb("chars", [VOCAB, 2, T], I32)
        shifted = sb("shifted", [NM, 2, T], I32)
        own = sb("own", [NM, 2, T], I32)
        idx_now = sb("idx_now", [P, 2, TT * NW], I32)
        rows = [sb(f"rows{b}", [P, TT, NW, E_TOK]) for b in R]
        onehot = [sb(f"onehot{b}", [VOCAB, T]) for b in R]
        match = [sb(f"match{b}", [NM, T]) for b in R]
        prod = [sb(f"prod{b}", [P, TT, NW, E_TOK]) for b in R]
        score = [sb(f"score{b}", [P, TT, NW]) for b in R]
        score_e = [sb(f"score_e{b}", [P, TT, NW]) for b in R]
        smax = [sb(f"smax{b}", [P, TT]) for b in R]
        ssum = [sb(f"ssum{b}", [P, TT]) for b in R]
        feat = [sb(f"feat{b}", [P, TT, E_TOK]) for b in R]
        featT = [sb(f"featT{b}", [E_TOK, KC - 1 + T]) for b in R]
        conv = [[sb(f"conv{b}_{k}", [E_TOK, T]) for k in R] for b in R]
        hash_act = [sb(f"hash_act{b}", [E_TOK, T]) for b in R]
        h1 = [sb(f"h1_{b}", [H_TOK, T]) for b in R]
        gate = [sb(f"gate{b}", [S_TOK, T]) for b in R]
        one_minus = [sb(f"one_minus{b}", [S_TOK, T]) for b in R]
        drive = [sb(f"drive{b}", [S_TOK, T]) for b in R]
        gate_in = [sb(f"gate_in{b}", [S_TOK, T]) for b in R]
        gate_start = [sb(f"gate_start{b}", [S_TOK, T]) for b in R]
        cum_a = [sb(f"cum_a{b}", [S_TOK, T]) for b in R]
        cum_wb = [sb(f"cum_wb{b}", [S_TOK, T]) for b in R]
        carry = [sb(f"carry{b}", [S_TOK, 1 + NCH]) for b in R]
        states = [sb(f"states{b}", [S_TOK, T]) for b in R]
        cen = [sb(f"cen{b}", [H_TOK, T]) for b in R]
        sq = [sb(f"sq{b}", [H_TOK, T]) for b in R]
        hid = [sb(f"hid{b}", [H_TOK, T]) for b in R]
        hid_act = [sb(f"hid_act{b}", [H_TOK, T]) for b in R]
        h_tok = [sb(f"h_tok{b}", [P, TT, D]) for b in R]
        ps_q = [ps(f"ps_q{b}", [P, TT, E_TOK]) for b in R]
        ps_h = [ps(f"ps_h{b}", [P, 512]) for b in R]
        ps_s = [ps(f"ps_s{b}", [P, 512]) for b in R]

        chars_in = [sem(f"chars_in{b}") for b in R]
        rows_in = [nc.alloc_semaphore(f"tok_rows_in{b}") for b in R]
        stored = [sem(f"stored{b}") for b in R]
        names = ("idx_ready chars_used rows_used q_ready scores_centred exps_ready feat_ready featT_ready conv_ready "
                 "hash_ready onehot_ready in_ready h1_ready gates_ready gates_act drive_pre drive_ready states_ready "
                 "centred_ready squares_ready var_ready std_ready hid_ready mlp_lin mlp_ready mlp_act out_ready h_ready")
        S = {n: sem(n) for n in names.split()}
        dve_steps, pool_passed, dve_passed, pe_passed = sem("dve_steps"), sem("pool_passed"), sem("dve_passed"), sem("pe_passed")

        with nc.Block() as block:
            @block.sync
            def _(sp):
                sp.sem_inc(S["chars_used"], 2)
                with sp.Fori(0, B // 2) as i:
                    for b in R:
                        sp.wait_ge(S["chars_used"], 2 * i + b + 1)
                        row = 2 * i + b
                        seq = x[bass.ds(row, 1), :]
                        sp.dma_start(chars[:, b, :], seq.partition_broadcast(VOCAB).rearrange("p a t -> p (a t)")).then_inc(chars_in[b], 16)
                        sp.dma_start(own[:, b, :], seq.partition_broadcast(NM).rearrange("p a t -> p (a t)")).then_inc(chars_in[b], 16)
                        for n, k in enumerate(MATCH_OFFSETS):
                            sp.dma_start(shifted[n:n + 1, b, :], xpad[bass.ds(row, 1), WMAX - k:WMAX - k + T]).then_inc(chars_in[b], 16)
                    for b in R:
                        sp.wait_ge(S["h_ready"], 2 * i + b + 1)
                        dst = h_out[bass.ds((2 * i + b) * T, T), :].rearrange("(t p) d -> p t d", p=P)
                        sp.dma_start(dst, h_tok[b][:, :, :]).then_inc(stored[b], 16)
                for b in R:
                    sp.wait_ge(stored[b], 16 * B // 2)

            @block.gpsimd
            def _(pool):
                pool.sem_inc(S["rows_used"], 2)
                with pool.Fori(0, B // 2) as i:
                    for b in R:
                        pool.wait_ge(S["rows_used"], 2 * i + b + 1)
                        held(pool, S["idx_ready"], 2 * i + b + 1, pool_passed)
                        for t in range(TT):
                            for n in range(NW):
                                pool.indirect_dma_start(
                                    rows[b][:, t, n, :], None, w["hash_rows"],
                                    bass.IndirectOffsetOnAxis(idx_now[:, b, t * NW + n:t * NW + n + 1], 0),
                                ).then_inc(rows_in[b], 16)

            @block.vector
            def _(dve):
                s = Steps(dve, dve_steps)
                for b in R:
                    s.did(dve.memset(featT[b][:, 0:KC - 1], 0.0))
                    s.did(dve.memset(carry[b][:, 0:1], 0.0))
                s.wait()
                with dve.Fori(0, B // 2) as i:
                    n = [2 * i + 1, 2 * i + 2]
                    s.restart()
                    mark = [0, 0]
                    for b in R:
                        held(dve, S["rows_used"], n[b], dve_passed)
                        dve.tensor_copy(idx_now[:, b, :], hash_idx[:, bass.ds((2 * i + b) * TT, TT), :].rearrange("p t n -> p (t n)")).then_inc(S["idx_ready"], 1)
                    for b in R:
                        dve.wait_ge(chars_in[b], 16 * 6 * (i + 1))
                        dve.tensor_scalar(onehot[b][:, :], chars[:, b, :], vocab_id[:, 0:1], None, ALU.is_equal).then_inc(S["onehot_ready"], 1)
                        s.did(dve.tensor_tensor(match[b][:, :], shifted[:, b, :], own[:, b, :], ALU.is_equal))
                        s.wait()
                        dve.sem_inc(S["chars_used"], 1)
                    for b in R:
                        dve.wait_ge(S["q_ready"], n[b])
                        dve.wait_ge(rows_in[b], 16 * TT * NW * (i + 1))
                        s.did(dve.tensor_tensor(prod[b][:, :, :, :], rows[b][:, :, :, :], bc(ps_q[b][:, :, :], 2, NW), ALU.mult))
                        s.wait()
                        s.did(dve.tensor_reduce(score[b][:, :, :], prod[b][:, :, :, :], AX.X, ALU.add))
                        s.wait()
                        s.did(dve.tensor_reduce(smax[b][:, :], score[b][:, :, :], AX.X, ALU.max))
                        s.wait()
                        dve.tensor_tensor(score[b][:, :, :], score[b][:, :, :], bc(smax[b][:, :], 2, NW), ALU.subtract).then_inc(S["scores_centred"], 1)
                    for b in R:
                        dve.wait_ge(S["exps_ready"], n[b])
                        s.did(dve.tensor_reduce(ssum[b][:, :], score_e[b][:, :, :], AX.X, ALU.add))
                        s.wait()
                        s.did(dve.reciprocal(ssum[b][:, :], ssum[b][:, :]))
                        s.wait()
                        s.did(dve.tensor_tensor(score_e[b][:, :, :], score_e[b][:, :, :], bc(ssum[b][:, :], 2, NW), ALU.mult))
                        s.wait()
                        s.did(dve.tensor_tensor(prod[b][:, :, :, :], rows[b][:, :, :, :], bc(score_e[b][:, :, :], 3, E_TOK), ALU.mult))
                        s.wait()
                        dve.sem_inc(S["rows_used"], 1)
                        dve.tensor_reduce(feat[b][:, :, :], prod[b][:, :, :, :].rearrange("p t s e -> p t e s"), AX.X, ALU.add).then_inc(S["feat_ready"], 1)
                    for b in R:
                        dve.wait_ge(S["featT_ready"], n[b])
                        s.did(dve.tensor_copy(featT[b][:, KC - 1:], ps_s[b][0:E_TOK, :]))
                        s.wait()
                        s.did(dve.tensor_scalar(conv[b][0][:, :], featT[b][:, 0:T], conv_w[:, 0:1], None, ALU.mult))
                        for k in range(1, KC):
                            s.wait()
                            ins = dve.scalar_tensor_tensor(conv[b][k % 2][:, :], featT[b][:, k:k + T], conv_w[:, k:k + 1], conv[b][(k + 1) % 2][:, :], ALU.mult, ALU.add)
                            if k < KC - 1:
                                s.did(ins)
                        ins.then_inc(S["conv_ready"], 1)
                    for b in R:
                        dve.wait_ge(S["gates_act"], n[b])
                        s.did(dve.tensor_scalar(one_minus[b][:, :], gate[b][:, :], -1.0, 1.0, ALU.mult, ALU.add))
                        s.did(dve.tensor_scalar(gate[b][:, :], gate[b][:, :], 1e-6, None, ALU.max))
                        s.wait()
                        s.did(dve.tensor_tensor(drive[b][:, :], drive[b][:, :], one_minus[b][:, :], ALU.mult))
                        s.did(dve.tensor_tensor(gate_in[b][:, :], gate[b][:, :], in_chunk[:, :], ALU.mult))
                        s.did(dve.tensor_tensor(gate_start[b][:, :], gate[b][:, :], chunk_start[:, :], ALU.mult))
                        s.wait()
                        s.did(dve.tensor_tensor_scan(cum_a[b][:, :], gate_in[b][:, :], gate_start[b][:, :], 0.0, ALU.mult, ALU.add))
                        s.wait()
                        s.did(dve.tensor_scalar(gate_in[b][:, :], cum_a[b][:, :], 1e-8, None, ALU.max))
                        s.wait()
                        s.did(dve.reciprocal(gate_in[b][:, :], gate_in[b][:, :]))
                        s.wait()
                        s.did(dve.tensor_tensor(drive[b][:, :], drive[b][:, :], gate_in[b][:, :], ALU.mult))
                        s.wait()
                        s.did(dve.tensor_tensor_scan(cum_wb[b][:, :], in_chunk[:, :], drive[b][:, :], 0.0, ALU.mult, ALU.add))
                        s.wait()
                        s.did(dve.tensor_tensor_scan(carry[b][:, 1:], cum_wb[b][:, CHUNK - 1:T:CHUNK], cum_a[b][:, CHUNK - 1:T:CHUNK], 0.0, ALU.add, ALU.mult))
                        s.wait()
                        s.did(dve.tensor_tensor(cum_wb[b][:, :].rearrange("p (c k) -> p c k", k=CHUNK), cum_wb[b][:, :].rearrange("p (c k) -> p c k", k=CHUNK), bc(carry[b][:, 0:NCH], 2, CHUNK), ALU.add))
                        s.wait()
                        dve.tensor_tensor(states[b][:, :], cum_wb[b][:, :], cum_a[b][:, :], ALU.mult).then_inc(S["states_ready"], 1)
                    for b in R:
                        dve.wait_ge(S["std_ready"], n[b])
                        s.did(dve.reciprocal(sq[b][:, :], sq[b][:, :]))
                        s.wait()
                        s.did(dve.tensor_tensor(cen[b][:, :], cen[b][:, :], sq[b][:, :], ALU.mult))
                        s.wait()
                        dve.tensor_scalar(hid[b][:, :], cen[b][:, :], ln_g[:, 0:1], ln_b[:, 0:1], ALU.mult, ALU.add).then_inc(S["hid_ready"], 1)
                    for l in range(NR):
                        for b in R:
                            dve.wait_ge(S["mlp_act"], 2 * NR * i + 2 * l + b + 1)
                            dve.tensor_tensor(hid[b][:, :], hid[b][:, :], hid_act[b][:, :], ALU.add).then_inc(S["mlp_ready"], 1)
                    for b in R:
                        dve.wait_ge(S["out_ready"], n[b])
                        s.did(dve.tensor_copy(h_tok[b][:, :, :], ps_q[b][:, :, :]))
                        s.wait()
                        dve.sem_inc(S["h_ready"], 1)
                s.wait()

            @block.scalar
            def _(act):
                with act.Fori(0, B // 2) as i:
                    n = [2 * i + 1, 2 * i + 2]
                    for b in R:
                        act.wait_ge(S["scores_centred"], n[b])
                        act.activation(score_e[b][:, :, :], score[b][:, :, :], ACT.Exp, scale=float(E_TOK) ** -0.5).then_inc(S["exps_ready"], 1)
                    for b in R:
                        act.wait_ge(S["conv_ready"], n[b])
                        act.activation(hash_act[b][:, :], conv[b][(KC - 1) % 2][:, :], ACT.Silu, bias=conv_b[:, 0:1]).then_inc(S["hash_ready"], 1)
                    for b in R:
                        act.wait_ge(S["in_ready"], n[b])
                        act.activation(h1[b][:, :], ps_h[b][:, :], ACT.Silu, bias=b_in[:, 0:1]).then_inc(S["h1_ready"], 1)
                    for b in R:
                        act.wait_ge(S["gates_ready"], n[b])
                        act.activation(drive[b][:, :], ps_h[b][0:S_TOK, :], ACT.Identity, bias=bi[:, 0:1])
                        act.activation(gate[b][:, :], ps_s[b][0:S_TOK, :], ACT.Sigmoid, bias=bg[:, 0:1]).then_inc(S["gates_act"], 1)
                    for b in R:
                        act.wait_ge(S["centred_ready"], n[b])
                        act.activation(cen[b][:, :], ps_h[b][:, :], ACT.Identity, bias=bo_centred[:, 0:1])
                        act.activation(sq[b][:, :], ps_h[b][:, :], ACT.Square, bias=bo_centred[:, 0:1]).then_inc(S["squares_ready"], 1)
                    for b in R:
                        act.wait_ge(S["var_ready"], n[b])
                        act.activation(sq[b][:, :], ps_s[b][:, :], ACT.Sqrt, bias=eps[:, 0:1]).then_inc(S["std_ready"], 1)
                    for l in range(NR):
                        for b in R:
                            act.wait_ge(S["mlp_lin"], 2 * NR * i + 2 * l + b + 1)
                            act.activation(hid_act[b][:, :], ps_h[b][:, :], ACT.Silu, bias=mlp_b[:, l:l + 1]).then_inc(S["mlp_act"], 1)

            @block.tensor
            def _(pe):
                with pe.Fori(0, B // 2) as i:
                    n = [2 * i + 1, 2 * i + 2]
                    for b in R:
                        pe.wait_ge(S["onehot_ready"], n[b])
                        for t in range(TT):
                            mm = pe.matmul(ps_q[b][:, t, :], onehot[b][:, t * P:(t + 1) * P], q_table[:, :], start=True, stop=True)
                        mm.then_inc(S["q_ready"], 1)
                    for b in R:
                        held(pe, S["feat_ready"], n[b], pe_passed)
                        for t in range(TT):
                            mm = pe.transpose(ps_s[b][0:E_TOK, t * P:(t + 1) * P], feat[b][:, t, :], ident[:, :])
                        mm.then_inc(S["featT_ready"], 1)
                    for b in R:
                        pe.wait_ge(S["hash_ready"], n[b])
                        pe.matmul(ps_h[b][:, :], in_table[:, :], onehot[b][:, :], start=True, stop=False)
                        pe.matmul(ps_h[b][:, :], win_match[:, :], match[b][:, :], start=False, stop=False)
                        pe.matmul(ps_h[b][:, :], win_hash[:, :], hash_act[b][:, :], start=False, stop=True).then_inc(S["in_ready"], 1)
                    for b in R:
                        pe.wait_ge(S["h1_ready"], n[b])
                        pe.matmul(ps_s[b][0:S_TOK, :], wg[:, :], h1[b][:, :], start=True, stop=True)
                        pe.matmul(ps_h[b][0:S_TOK, :], wi[:, :], h1[b][:, :], start=True, stop=True).then_inc(S["gates_ready"], 1)
                    for b in R:
                        pe.wait_ge(S["states_ready"], n[b])
                        pe.matmul(ps_h[b][:, :], centre[:, :], h1[b][:, :], start=True, stop=False)
                        pe.matmul(ps_h[b][:, :], wo_centred[:, :], states[b][:, :], start=False, stop=True).then_inc(S["centred_ready"], 1)
                    for b in R:
                        pe.wait_ge(S["squares_ready"], n[b])
                        pe.matmul(ps_s[b][:, :], mean_all[:, :], sq[b][:, :], start=True, stop=True).then_inc(S["var_ready"], 1)
                    for l in range(NR):
                        for b in R:
                            if l == 0:
                                pe.wait_ge(S["hid_ready"], n[b])
                            else:
                                pe.wait_ge(S["mlp_ready"], 2 * NR * i + 2 * (l - 1) + b + 1)
                            pe.matmul(ps_h[b][:, :], mlp_w[:, l, :], hid[b][:, :], start=True, stop=True).then_inc(S["mlp_lin"], 1)
                    for b in R:
                        pe.wait_ge(S["mlp_ready"], 2 * NR * i + 2 * (NR - 1) + b + 1)
                        for t in range(TT):
                            pe.matmul(ps_q[b][:, t, :], hid[b][:, t * P:(t + 1) * P], wout[:, :], start=True, stop=False)
                            mm = pe.matmul(ps_q[b][:, t, :], ones_row[:, :], bout[:, :], start=False, stop=True)
                        mm.then_inc(S["out_ready"], 1)

        clear_semaphores(nc, sems)


HEADS0, DH0 = 4, 16
SHIFTS = (0, 4, 8, 12)
NSH, PAD0, WINDOW = len(SHIFTS), max(SHIFTS), 64
FB = 2 * T - P
UNITS = TT * HEADS0
HIGH, MIDDLE, LOWER = range(3)
QPARTS = (HIGH, HIGH, HIGH, MIDDLE, MIDDLE, LOWER)
KPARTS = (HIGH, MIDDLE, LOWER, HIGH, MIDDLE, HIGH)
STACK = len(QPARTS) * DH0


def shifted_attention(nc, w, h_in, h_out):
    with ExitStack() as ctx:
        def sb(name, shape, dt=F32):
            return ctx.enter_context(nc.sbuf_tensor("at0_" + name, shape, dt))

        def ps(name, shape):
            return ctx.enter_context(nc.psum_tensor("at0_" + name, shape, F32))

        sems = []

        def sem(name):
            sems.append(ctx.enter_context(nc.semaphore("at0_" + name)))
            return sems[-1]

        wq = sb("wq", [D + 1, HEADS0, len(QPARTS), DH0])
        wk = sb("wk", [D + 1, HEADS0, len(QPARTS), DH0])
        less_high = [sb(f"less_high{m}", [STACK, 1]) for m in range(2)]
        less_middle = [sb(f"less_middle{m}", [STACK, 1]) for m in range(2)]
        wv = sb("wv", [D + 1, D])
        wo = sb("wo", [D + 1, D])
        logits = sb("logits", [P, HEADS0, NSH])
        lmax = sb("lmax", [P, HEADS0])
        log_pi = sb("log_pi", [P, HEADS0, NSH])
        slope = sb("slope", [P, HEADS0])
        tiny = sb("tiny", [P, 1])
        eps = sb("eps", [P, 1])
        ident = sb("ident", [P, P])
        dist_i = sb("dist_i", [P, FB], I32)
        dist = sb("dist", [P, FB])
        mask = sb("mask", [P, FB])
        bias = sb("bias", [P, HEADS0, FB])
        loaded, gp_made, dve_made, act_made = sem("loaded"), sem("gp_made"), sem("dve_made"), sem("act_made")

        x = sb("x", [P, TT, D])
        xn = sb("xn", [P, TT, D])
        stats = sb("stats", [P, TT, 6])
        moments = sb("moments", [P, TT, 2])
        std = sb("std", [P, TT])
        xnT = sb("xnT", [D + 1, T])
        qS = [sb(f"qS{h}", [STACK, T], BF16) for h in range(HEADS0)]
        kS = [sb(f"kS{h}", [STACK, PAD0 + T], BF16) for h in range(HEADS0)]
        high = [sb(f"high{k}", [STACK, T], BF16) for k in range(2)]
        middle = [sb(f"middle{k}", [STACK, T], BF16) for k in range(2)]
        rest = [sb(f"rest{k}", [STACK, T]) for k in range(2)]
        vT = sb("vT", [D, PAD0 + T])
        vsumT = [sb(f"vsumT{k}", [D, T]) for k in range(2)]
        vsum = sb("vsum", [P, TT, D])
        att = [sb(f"att{k}", [P, NSH, T]) for k in range(2)]
        prob = [sb(f"prob{k}", [P, NSH, T]) for k in range(3)]
        psum_p = [sb(f"psum_p{k}", [P, T]) for k in range(3)]
        probT = [sb(f"probT{k}", [P, TT, P]) for k in range(2)]
        rowmax = [sb(f"rowmax{k}", [P, NSH]) for k in range(2)]
        negmax = [sb(f"negmax{k}", [P, 1]) for k in range(2)]
        shiftb = [sb(f"shiftb{k}", [P, NSH]) for k in range(2)]
        sums = [sb(f"sums{k}", [P, NSH]) for k in range(6)]
        total = [sb(f"total{k}", [P, 1]) for k in range(6)]
        inv = [sb(f"inv{k}", [P, 1]) for k in range(6)]
        context = sb("context", [P, TT, D])
        contextT = sb("contextT", [D + 1, T])
        y = sb("y", [P, TT, D])
        ps_att = [ps(f"ps_att{s}", [P, T]) for s in range(NSH)]
        ps_T = ps("ps_T", [P, T])
        ps_pT = ps("ps_pT", [P, T])
        ps_c = ps("ps_c", [P, T])
        ps_v = ps("ps_v", [P, T])

        x_in, x_used, stored = sem("x_in"), sem("x_used"), sem("stored")
        names = ("moments_ready std_ready xn_ready xnT_ps xnT_ready part_ps high_ready rest_ready middle_ready parts_ready v_ps v_ready vsum_made "
                 "vsum_ps vsum_ready scores_ready scores_used shift_ready probs_ready probs_used summed pT_ps pT_ready "
                 "ctx_ps context_part context_ready cT_ps cT_ready y_ps y_ready")
        S = {n: sem(n) for n in names.split()}
        dve_steps, act_steps, gp_steps = sem("dve_steps"), sem("act_steps"), sem("gp_steps")
        dve_passed, pe_passed = sem("dve_passed"), sem("pe_passed")

        LOADS = 16 * (4 * len(QPARTS) + 6)

        with nc.Block() as block:
            @block.sync
            def _(sp):
                for dst, name in ((wq, "q"), (wk, "k")):
                    for n in range(len(QPARTS)):
                        sp.dma_start(dst[0:D, :, n, :], w[f"W{name}T"].rearrange("i (h d) -> i h d", h=HEADS0)).then_inc(loaded, 16)
                        sp.dma_start(dst[D:D + 1, :, n, :], w[f"b{name}"].unsqueeze(0).rearrange("a (h d) -> a h d", h=HEADS0)).then_inc(loaded, 16)
                for dst, name in ((wv, "v"), (wo, "o")):
                    sp.dma_start(dst[0:D, :], w[f"W{name}T"]).then_inc(loaded, 16)
                    sp.dma_start(dst[D:D + 1, :], w[f"b{name}"].unsqueeze(0)).then_inc(loaded, 16)
                sp.dma_start(logits[:, :, :], w["shift_logits"].partition_broadcast(P)).then_inc(loaded, 16)
                sp.dma_start(slope[:, :], w["alibi_slope"].partition_broadcast(P)).then_inc(loaded, 16)
                sp.wait_ge(loaded, LOADS)

            @block.gpsimd
            def _(pool):
                pool.iota(dist_i[:, :], [[1, FB]], base=P - T, channel_multiplier=-1).then_inc(gp_made, 1)
                pool.memset(ident[:, :], 0.0).then_inc(gp_made, 1)
                pool.wait_ge(gp_made, 2)
                pool.affine_select(out=ident[:, :], in_=ident[:, :], compare_op=ALU.not_equal, fill=1.0, base=0,
                                   pattern=[[-1, P]], channel_multiplier=1).then_inc(gp_made, 1)
                count = 3
                for parts, high_sign, middle_sign in ((QPARTS, less_high[0], less_middle[0]), (KPARTS, less_high[1], less_middle[1])):
                    for tile, least in ((high_sign, MIDDLE), (middle_sign, LOWER)):
                        pool.memset(tile[:, :], 0.0).then_inc(gp_made, 1)
                        count += 1
                        for n, part in enumerate(parts):
                            if part >= least:
                                for first, sign in ((n * DH0, -1.0), ((n + 1) * DH0, 0.0)):
                                    pool.wait_ge(gp_made, count)
                                    if first < STACK:
                                        pool.affine_select(out=tile[:, :], in_=tile[:, :], compare_op=ALU.is_gt, fill=sign, base=first,
                                                           pattern=[[0, 1]], channel_multiplier=-1).then_inc(gp_made, 1)
                                        count += 1

            @block.scalar
            def _(act):
                act.wait_ge(dve_made, 1)
                act.activation(log_pi[:, :, :], logits[:, :, :], ACT.Exp).then_inc(act_made, 1)
                act.wait_ge(dve_made, 2)
                act.activation(log_pi[:, :, :], logits[:, :, :], ACT.Ln, bias=tiny[:, 0:1]).then_inc(act_made, 1)

            @block.vector
            def _(dve):
                s = Steps(dve, dve_steps)
                s.did(dve.memset(tiny[:, :], 1e-8))
                s.did(dve.memset(eps[:, :], EPS))
                for h in range(HEADS0):
                    s.did(dve.memset(kS[h][:, 0:PAD0], 0.0))
                s.did(dve.memset(vT[:, 0:PAD0], 0.0))
                s.did(dve.memset(xnT[D:D + 1, :], 1.0))
                s.did(dve.memset(contextT[D:D + 1, :], 1.0))
                dve.wait_ge(gp_made, 3)
                s.did(dve.tensor_copy(dist[:, :], dist_i[:, :]))
                s.wait()
                s.did(dve.tensor_scalar(mask[:, :], dist[:, :], float(WINDOW), 10000.0, ALU.is_lt, ALU.mult))
                s.wait()
                s.did(dve.scalar_tensor_tensor(mask[:, :], dist[:, :], 0.0, mask[:, :], ALU.is_ge, ALU.mult))
                s.wait()
                s.did(dve.tensor_scalar(mask[:, :], mask[:, :], -10000.0, None, ALU.add))
                s.did(dve.tensor_scalar(dist[:, :], dist[:, :], 0.0, None, ALU.max))
                dve.wait_ge(loaded, LOADS)
                s.did(dve.tensor_scalar(slope[:, :], slope[:, :], -1.0, None, ALU.mult))
                s.did(dve.tensor_scalar(wq[:, :, :, :], wq[:, :, :, :], float(DH0) ** -0.5, None, ALU.mult))
                s.wait()
                for h in range(HEADS0):
                    s.did(dve.scalar_tensor_tensor(bias[:, h, :], dist[:, :], slope[:, h:h + 1], mask[:, :], ALU.mult, ALU.add))
                s.did(dve.tensor_reduce(lmax[:, :], logits[:, :, :], AX.X, ALU.max))
                s.wait()
                dve.tensor_tensor(logits[:, :, :], logits[:, :, :], bc(lmax[:, :], 2, NSH), ALU.subtract).then_inc(dve_made, 1)
                dve.wait_ge(act_made, 1)
                s.did(dve.tensor_reduce(lmax[:, :], log_pi[:, :, :], AX.X, ALU.add))
                s.wait()
                s.did(dve.reciprocal(lmax[:, :], lmax[:, :]))
                s.wait()
                dve.tensor_tensor(logits[:, :, :], log_pi[:, :, :], bc(lmax[:, :], 2, NSH), ALU.mult).then_inc(dve_made, 1)
                dve.wait_ge(act_made, 2)
                s.wait()

        with nc.Block() as block:
            @block.sync
            def _(sp):
                sp.sem_inc(x_used, 1)
                with sp.Fori(0, B) as i:
                    sp.wait_ge(x_used, i + 1)
                    sp.dma_start(x[:, :, :], h_in[bass.ds(i * T, T), :].rearrange("(t p) d -> p t d", p=P)).then_inc(x_in, 16)
                    sp.wait_ge(S["y_ready"], i + 1)
                    sp.dma_start(h_out[bass.ds(i * T, T), :].rearrange("(t p) d -> p t d", p=P), y[:, :, :]).then_inc(stored, 16)
                sp.wait_ge(stored, 16 * B)

            @block.vector
            def _(dve):
                s = Steps(dve, dve_steps)
                s.n = 0
                dve.sem_clear(dve_steps)
                with dve.Fori(0, B) as i:
                    s.restart()
                    held(dve, x_in, 16 * i + 16, dve_passed)
                    ln_moments(dve, s, x, stats, moments)
                    dve.sem_inc(S["moments_ready"], 1)
                    dve.wait_ge(S["std_ready"], i + 1)
                    ln_apply(dve, s, xn, x, moments, std).then_inc(S["xn_ready"], 1)
                    dve.wait_ge(S["xnT_ps"], i + 1)
                    dve.tensor_copy(xnT[0:D, :], ps_T[0:D, :]).then_inc(S["xnT_ready"], 1)
                    for m in range(2 * HEADS0):
                        h, which, k = m // 2, m % 2, m % 2
                        dst = kS[h][:, PAD0:] if which else qS[h][:, :]
                        c = 2 * HEADS0 * i + m + 1
                        dve.wait_ge(S["high_ready"], c)
                        dve.scalar_tensor_tensor(rest[k][:, :], high[k][:, :], less_high[which][:, 0:1], ps_att[m % NSH][0:STACK, :],
                                                 ALU.mult, ALU.add).then_inc(S["rest_ready"], 1)
                        dve.wait_ge(S["middle_ready"], c)
                        dve.scalar_tensor_tensor(dst, middle[k][:, :], less_middle[which][:, 0:1], rest[k][:, :],
                                                 ALU.mult, ALU.add).then_inc(S["parts_ready"], 1)
                    dve.wait_ge(S["v_ready"], i + 1)
                    s.did(dve.tensor_tensor(vsumT[0][:, :], vT[:, PAD0:PAD0 + T], vT[:, PAD0 - SHIFTS[1]:PAD0 - SHIFTS[1] + T], ALU.add))
                    s.did(dve.tensor_tensor(vsumT[1][:, :], vT[:, PAD0 - SHIFTS[2]:PAD0 - SHIFTS[2] + T], vT[:, PAD0 - SHIFTS[3]:PAD0 - SHIFTS[3] + T], ALU.add))
                    s.wait()
                    dve.tensor_tensor(vsumT[0][:, :], vsumT[0][:, :], vsumT[1][:, :], ALU.add).then_inc(S["vsum_made"], 1)
                    dve.wait_ge(S["vsum_ps"], i + 1)
                    dve.tensor_copy(vsum[:, :, :], ps_T[:, 0:TT * D].rearrange("p (t d) -> p t d", d=D)).then_inc(S["vsum_ready"], 1)

                    def maxima(u):
                        qt, h, k = u // HEADS0, u % HEADS0, u % 2
                        off = T - P - qt * P
                        for j in range(NSH):
                            if j == 0 and u >= 2:
                                dve.wait_ge(S["probs_ready"], UNITS * i + u - 1)
                            held(dve, S["scores_ready"], 4 * UNITS * i + 4 * u + j + 1, dve_passed)
                            dve.tensor_tensor_reduce(att[k][:, j, :], ps_att[j][:, :], bias[:, h, off:off + T], 1.0, -3.0e38,
                                                     ALU.add, ALU.max, rowmax[k][:, j:j + 1]).then_inc(S["scores_used"], 1)
                        dve.wait_ge(S["scores_used"], 4 * UNITS * i + 4 * u + 4)
                        s.did(dve.tensor_tensor(rowmax[k][:, :], rowmax[k][:, :], log_pi[:, h, :], ALU.add))
                        s.wait()
                        s.did(dve.tensor_reduce(negmax[k][:, :], rowmax[k][:, :], AX.X, ALU.max, negate=True))
                        s.wait()
                        dve.tensor_scalar(shiftb[k][:, :], log_pi[:, h, :], negmax[k][:, 0:1], None, ALU.add).then_inc(S["shift_ready"], 1)

                    def inverse(u):
                        k = u % 6
                        dve.wait_ge(S["probs_ready"], UNITS * i + u + 1)
                        s.did(dve.tensor_reduce(total[k][:, :], sums[k][:, :], AX.X, ALU.add))
                        s.wait()
                        s.did(dve.reciprocal(inv[k][:, :], total[k][:, :]))
                        s.wait()

                    def normalise(u):
                        qt, h, k = u // HEADS0, u % HEADS0, u % 6
                        dve.wait_ge(S["ctx_ps"], UNITS * i + u + 1)
                        dve.tensor_scalar(context[:, qt, h * DH0:(h + 1) * DH0], [ps_c, ps_v][u % 2][:, u * DH0:(u + 1) * DH0], inv[k][:, 0:1], None,
                                          ALU.mult).then_inc(S["context_part"], 1)

                    for step in range(UNITS + 4):
                        if step < UNITS:
                            maxima(step)
                        if 1 <= step <= UNITS:
                            inverse(step - 1)
                        if step >= 4:
                            normalise(step - 4)
                    dve.wait_ge(S["context_part"], UNITS * (i + 1))
                    dve.sem_inc(S["context_ready"], 1)
                    dve.wait_ge(S["cT_ps"], i + 1)
                    dve.tensor_copy(contextT[0:D, :], ps_T[0:D, :]).then_inc(S["cT_ready"], 1)
                    dve.wait_ge(S["y_ps"], i + 1)
                    s.did(dve.tensor_tensor(y[:, :, :], ps_v[:, 0:TT * D].rearrange("p (t d) -> p t d", d=D), x[:, :, :], ALU.add))
                    s.wait()
                    dve.sem_inc(x_used, 1)
                    dve.sem_inc(S["y_ready"], 1)
                s.wait()

            @block.scalar
            def _(act):
                with act.Fori(0, B) as i:
                    act.wait_ge(S["moments_ready"], i + 1)
                    act.activation(std[:, :], moments[:, :, 1], ACT.Sqrt, bias=eps[:, 0:1]).then_inc(S["std_ready"], 1)
                    act.wait_ge(S["v_ps"], i + 1)
                    act.activation(vT[:, PAD0:], ps_v[0:D, :], ACT.Copy).then_inc(S["v_ready"], 1)

                    def highs(m):
                        act.wait_ge(S["part_ps"], 2 * HEADS0 * i + m + 1)
                        if m >= 2:
                            act.wait_ge(S["rest_ready"], 2 * HEADS0 * i + m - 1)
                        act.activation(high[m % 2][:, :], ps_att[m % NSH][0:STACK, :], ACT.Copy).then_inc(S["high_ready"], 1)

                    def middles(m):
                        act.wait_ge(S["rest_ready"], 2 * HEADS0 * i + m + 1)
                        if m >= 2:
                            act.wait_ge(S["parts_ready"], 2 * HEADS0 * i + m - 1)
                        act.activation(middle[m % 2][:, :], rest[m % 2][:, :], ACT.Copy).then_inc(S["middle_ready"], 1)

                    for m in range(2 * HEADS0 + 1):
                        if m < 2 * HEADS0:
                            highs(m)
                        if m >= 1:
                            middles(m - 1)

                    def exponentials(u):
                        k = u % 2
                        act.wait_ge(S["shift_ready"], UNITS * i + u + 1)
                        if u >= 3:
                            act.wait_ge(S["summed"], UNITS * i + u - 2)
                        for j in range(NSH):
                            ins = act.activation(prob[u % 3][:, j, :], att[k][:, j, :], ACT.Exp, bias=shiftb[k][:, j:j + 1], accum_out=sums[u % 6][:, j:j + 1])
                        ins.then_inc(S["probs_ready"], 1)

                    def transposed(u):
                        act.wait_ge(S["pT_ps"], UNITS * i + u + 1)
                        if u >= 2:
                            act.wait_ge(S["ctx_ps"], UNITS * i + u - 1)
                        act.activation(probT[u % 2][:, :, :], ps_pT[:, :].rearrange("p (t q) -> p t q", t=TT), ACT.Copy).then_inc(S["pT_ready"], 1)

                    for step in range(UNITS + 2):
                        if step < UNITS:
                            exponentials(step)
                        if step >= 2:
                            transposed(step - 2)

            @block.gpsimd
            def _(pool):
                with pool.Fori(0, B) as i:
                    for u in range(UNITS):
                        k = u % 3
                        pool.wait_ge(S["probs_ready"], UNITS * i + u + 1)
                        pool.tensor_tensor(prob[k][:, 0:2, :], prob[k][:, 0:2, :], prob[k][:, 2:4, :], ALU.add).then_inc(S["probs_used"], 1)
                        pool.wait_ge(S["probs_used"], UNITS * i + u + 1)
                        if u >= 3:
                            pool.wait_ge(S["pT_ps"], UNITS * i + u - 2)
                        pool.tensor_tensor(psum_p[k][:, :], prob[k][:, 0, :], prob[k][:, 1, :], ALU.add).then_inc(S["summed"], 1)

            @block.tensor
            def _(pe):
                with pe.Fori(0, B) as i:
                    held(pe, S["xn_ready"], i + 1, pe_passed)
                    for t in range(TT):
                        mm = pe.transpose(ps_T[0:D, t * P:(t + 1) * P], xn[:, t, :], ident[:, :])
                    mm.then_inc(S["xnT_ps"], 1)
                    pe.wait_ge(S["xnT_ready"], i + 1)
                    pe.matmul(ps_v[0:D, :], wv[:, :], xnT[:, :], start=True, stop=True).then_inc(S["v_ps"], 1)
                    for m in range(2 * HEADS0):
                        if m >= NSH:
                            pe.wait_ge(S["rest_ready"], 2 * HEADS0 * i + m - NSH + 1)
                        pe.matmul(ps_att[m % NSH][0:STACK, :], [wq, wk][m % 2][:, m // 2, :, :].rearrange("i n d -> i (n d)"), xnT[:, :],
                                  start=True, stop=True).then_inc(S["part_ps"], 1)
                    held(pe, S["vsum_made"], i + 1, pe_passed)
                    for t in range(TT):
                        mm = pe.transpose(ps_T[:, t * D:(t + 1) * D], vsumT[0][:, t * P:(t + 1) * P], ident[0:D, 0:D])
                    mm.then_inc(S["vsum_ps"], 1)
                    pe.wait_ge(S["parts_ready"], 2 * HEADS0 * (i + 1))

                    def scores(u):
                        qt, h = u // HEADS0, u % HEADS0
                        for j, shift in enumerate(SHIFTS):
                            if u >= 1:
                                held(pe, S["scores_used"], 4 * UNITS * i + 4 * (u - 1) + j + 1, pe_passed)
                            pe.matmul(ps_att[j][:, :], qS[h][:, qt * P:(qt + 1) * P], kS[h][:, PAD0 - shift:PAD0 - shift + T],
                                      start=True, stop=True).then_inc(S["scores_ready"], 1)

                    def transposes(u):
                        pe.wait_ge(S["summed"], UNITS * i + u + 1)
                        if u >= 1:
                            pe.wait_ge(S["pT_ready"], UNITS * i + u)
                        for t in range(TT):
                            mm = pe.transpose(ps_pT[:, t * P:(t + 1) * P], psum_p[u % 3][:, t * P:(t + 1) * P], ident[:, :])
                        mm.then_inc(S["pT_ps"], 1)

                    def values(u):
                        h = u % HEADS0
                        pe.wait_ge(S["pT_ready"], UNITS * i + u + 1)
                        if u >= 2:
                            pe.wait_ge(S["context_part"], UNITS * i + u - 1)
                        if u == 0:
                            pe.wait_ge(S["vsum_ready"], i + 1)
                        for t in range(TT):
                            mm = pe.matmul([ps_c, ps_v][u % 2][:, u * DH0:(u + 1) * DH0], probT[u % 2][:, t, :], vsum[:, t, h * DH0:(h + 1) * DH0],
                                           start=(t == 0), stop=(t == TT - 1))
                        mm.then_inc(S["ctx_ps"], 1)

                    for step in range(UNITS + 3):
                        if step < UNITS:
                            scores(step)
                        if 2 <= step < UNITS + 2:
                            transposes(step - 2)
                        if step >= 3:
                            values(step - 3)
                    held(pe, S["context_ready"], i + 1, pe_passed)
                    for t in range(TT):
                        mm = pe.transpose(ps_T[0:D, t * P:(t + 1) * P], context[:, t, :], ident[:, :])
                    mm.then_inc(S["cT_ps"], 1)
                    pe.wait_ge(S["cT_ready"], i + 1)
                    for t in range(TT):
                        mm = pe.matmul(ps_v[:, t * D:(t + 1) * D], contextT[:, t * P:(t + 1) * P], wo[:, :], start=True, stop=True)
                    mm.then_inc(S["y_ps"], 1)

        clear_semaphores(nc, sems)


HID0, EXPERTS = 256, 8
HC0 = HID0 // P


def routed_ffn(nc, w, h_in, h_out):
    with ExitStack() as ctx:
        def sb(name, shape, dt=F32):
            return ctx.enter_context(nc.sbuf_tensor("ff0_" + name, shape, dt))

        def ps(name, shape):
            return ctx.enter_context(nc.psum_tensor("ff0_" + name, shape, F32))

        sems = []

        def sem(name):
            sems.append(ctx.enter_context(nc.semaphore("ff0_" + name)))
            return sems[-1]

        w1 = sb("w1", [D + 1, HID0])
        wg = sb("wg", [P, HC0, EXPERTS])
        bg = sb("bg", [1, EXPERTS])
        wd = sb("wd", [P, HC0, EXPERTS * D])
        bd = sb("bd", [1, EXPERTS * D])
        ones_row = sb("ones_row", [1, P])
        eps = sb("eps", [P, 1])
        ident = sb("ident", [P, P])
        expert_id_i = sb("expert_id_i", [P, EXPERTS], I32)
        expert_id = sb("expert_id", [P, EXPERTS])
        R = range(2)
        x = [sb(f"x{b}", [P, TT, D]) for b in R]
        xn = [sb(f"xn{b}", [P, TT, D]) for b in R]
        stats = [sb(f"stats{b}", [P, TT, 6]) for b in R]
        moments = [sb(f"moments{b}", [P, TT, 2]) for b in R]
        std = [sb(f"std{b}", [P, TT]) for b in R]
        xnT = [sb(f"xnT{b}", [D + 1, T]) for b in R]
        hidT = [sb(f"hidT{b}", [P, HC0, T]) for b in R]
        prob = [sb(f"prob{b}", [P, TT, EXPERTS]) for b in R]
        pmax = [sb(f"pmax{b}", [P, TT]) for b in R]
        psum_e = [sb(f"psum_e{b}", [P, TT]) for b in R]
        top8 = [sb(f"top8{b}", [P, TT, 8]) for b in R]
        top8_at = [sb(f"top8_at{b}", [P, TT, 8], U32) for b in R]
        best = [sb(f"best{b}", [P, TT]) for b in R]
        pick = [sb(f"pick{b}", [P, TT, EXPERTS]) for b in R]
        picked = [sb(f"picked{b}", [P, EXPERTS, D]) for b in R]
        y = [sb(f"y{b}", [P, TT, D]) for b in R]
        ps_T = ps("ps_T", [P, T])
        ps_hid = [ps(f"ps_hid{k}", [P, T]) for k in R]
        ps_g = ps("ps_g", [P, T])
        ps_y = [ps(f"ps_y{k}", [P, EXPERTS * D]) for k in range(4)]
        loaded, gp_made, x_used = sem("loaded"), sem("gp_made"), sem("x_used")
        x_in = [sem(f"x_in{b}") for b in R]
        stored = [sem(f"stored{b}") for b in R]
        names = ("moments_ready std_ready xn_ready xnT_ps xnT_ready hid_ps hid_ready gates_ps gates_centred gates_exp "
                 "y_ps y_used y_ready")
        S = {n: sem(n) for n in names.split()}
        dve_steps, dve_passed, pe_passed = sem("dve_steps"), sem("dve_passed"), sem("pe_passed")

        with nc.Block() as block:
            @block.sync
            def _(sp):
                for dst, src in ((w1[0:D, :], w["W1"]), (w1[D:D + 1, :], w["b1"].unsqueeze(0)),
                                 (wg[:, :, :], w["Wg"].rearrange("(c p) e -> p c e", p=P)), (bg[:, :], w["bg"].unsqueeze(0)),
                                 (bd[:, :], w["bd"].rearrange("e d -> (e d)").unsqueeze(0))):
                    sp.dma_start(dst, src).then_inc(loaded, 16)
                for c in range(HC0):
                    sp.dma_start(wd[:, c, :].rearrange("p (e d) -> p e d", e=EXPERTS),
                                 w["Wd"][:, c * P:(c + 1) * P, :].rearrange("e p d -> p e d")).then_inc(loaded, 16)
                sp.wait_ge(loaded, 16 * (5 + HC0))

            @block.gpsimd
            def _(pool):
                pool.iota(expert_id_i[:, :], [[1, EXPERTS]], base=0, channel_multiplier=0).then_inc(gp_made, 1)
                pool.memset(ident[:, :], 0.0).then_inc(gp_made, 1)
                pool.wait_ge(gp_made, 2)
                pool.affine_select(out=ident[:, :], in_=ident[:, :], compare_op=ALU.not_equal, fill=1.0, base=0,
                                   pattern=[[-1, P]], channel_multiplier=1).then_inc(gp_made, 1)

            @block.vector
            def _(dve):
                s = Steps(dve, dve_steps)
                s.did(dve.memset(ones_row[:, :], 1.0))
                s.did(dve.memset(eps[:, :], EPS))
                for b in R:
                    s.did(dve.memset(xnT[b][D:D + 1, :], 1.0))
                dve.wait_ge(gp_made, 3)
                s.did(dve.tensor_copy(expert_id[:, :], expert_id_i[:, :]))
                s.wait()
                dve.sem_clear(dve_steps)

        with nc.Block() as block:
            @block.sync
            def _(sp):
                sp.sem_inc(x_used, 2)
                with sp.Fori(0, B // 2) as i:
                    for b in R:
                        sp.wait_ge(x_used, 2 * i + b + 1)
                        sp.dma_start(x[b][:, :, :], h_in[bass.ds((2 * i + b) * T, T), :].rearrange("(t p) d -> p t d", p=P)).then_inc(x_in[b], 16)
                    for b in R:
                        sp.wait_ge(S["y_ready"], 2 * i + b + 1)
                        sp.dma_start(h_out[bass.ds((2 * i + b) * T, T), :].rearrange("(t p) d -> p t d", p=P), y[b][:, :, :]).then_inc(stored[b], 16)
                for b in R:
                    sp.wait_ge(stored[b], 16 * B // 2)

            @block.vector
            def _(dve):
                s = Steps(dve, dve_steps)
                with dve.Fori(0, B // 2) as i:
                    n = [2 * i + 1, 2 * i + 2]
                    s.restart()
                    for b in R:
                        held(dve, x_in[b], 16 * i + 16, dve_passed)
                        ln_moments(dve, s, x[b], stats[b], moments[b])
                        dve.sem_inc(S["moments_ready"], 1)
                    for b in R:
                        dve.wait_ge(S["std_ready"], n[b])
                        ln_apply(dve, s, xn[b], x[b], moments[b], std[b]).then_inc(S["xn_ready"], 1)
                    for b in R:
                        dve.wait_ge(S["xnT_ps"], n[b])
                        dve.tensor_copy(xnT[b][0:D, :], ps_T[0:D, :]).then_inc(S["xnT_ready"], 1)
                    for b in R:
                        dve.wait_ge(S["gates_ps"], n[b])
                        g = ps_g[:, 0:TT * EXPERTS].rearrange("p (t e) -> p t e", e=EXPERTS)
                        s.did(dve.tensor_reduce(pmax[b][:, :], g, AX.X, ALU.max))
                        s.wait()
                        dve.tensor_tensor(prob[b][:, :, :], g, bc(pmax[b][:, :], 2, EXPERTS), ALU.subtract).then_inc(S["gates_centred"], 1)
                    for b in R:
                        dve.wait_ge(S["gates_exp"], n[b])
                        s.did(dve.tensor_reduce(psum_e[b][:, :], prob[b][:, :, :], AX.X, ALU.add))
                        s.wait()
                        s.did(dve.reciprocal(psum_e[b][:, :], psum_e[b][:, :]))
                        s.wait()
                        s.did(dve.tensor_tensor(prob[b][:, :, :], prob[b][:, :, :], bc(psum_e[b][:, :], 2, EXPERTS), ALU.mult))
                        s.wait()
                        for t in range(TT):
                            s.did(dve.max(top8[b][:, t, :], prob[b][:, t, :]))
                        s.wait()
                        for t in range(TT):
                            s.did(dve.max_index(top8_at[b][:, t, :], top8[b][:, t, :], prob[b][:, t, :]))
                        s.wait()
                        s.did(dve.tensor_copy(best[b][:, :], top8_at[b][:, :, 0]))
                        s.wait()
                        s.did(dve.tensor_tensor(pick[b][:, :, :], bc(expert_id[:, :], 1, TT), bc(best[b][:, :], 2, EXPERTS), ALU.is_equal))
                        s.wait()
                        s.did(dve.tensor_tensor(pick[b][:, :, :], pick[b][:, :, :], prob[b][:, :, :], ALU.mult))
                        s.wait()
                        for t in range(TT):
                            dve.wait_ge(S["y_ps"], 2 * TT * i + TT * b + t + 1)
                            dve.tensor_tensor(picked[t % 2][:, :, :], ps_y[t][:, :].rearrange("p (e d) -> p e d", e=EXPERTS),
                                              bc(pick[b][:, t, :], 2, D), ALU.mult).then_inc(S["y_used"], 1)
                            dve.wait_ge(S["y_used"], 2 * TT * i + TT * b + t + 1)
                            s.did(dve.tensor_reduce(y[b][:, t, :], picked[t % 2][:, :, :].rearrange("p e d -> p d e"), AX.X, ALU.add))
                            s.wait()
                        s.did(dve.tensor_tensor(y[b][:, :, :], y[b][:, :, :], x[b][:, :, :], ALU.add))
                        s.wait()
                        dve.sem_inc(x_used, 1)
                        dve.sem_inc(S["y_ready"], 1)
                s.wait()

            @block.scalar
            def _(act):
                with act.Fori(0, B // 2) as i:
                    n = [2 * i + 1, 2 * i + 2]
                    for b in R:
                        act.wait_ge(S["moments_ready"], n[b])
                        act.activation(std[b][:, :], moments[b][:, :, 1], ACT.Sqrt, bias=eps[:, 0:1]).then_inc(S["std_ready"], 1)
                    for b in R:
                        for c in range(HC0):
                            act.wait_ge(S["hid_ps"], 2 * HC0 * i + HC0 * b + c + 1)
                            act.activation(hidT[b][:, c, :], ps_hid[c][:, :], ACT.Gelu).then_inc(S["hid_ready"], 1)
                    for b in R:
                        act.wait_ge(S["gates_centred"], n[b])
                        act.activation(prob[b][:, :, :], prob[b][:, :, :], ACT.Exp).then_inc(S["gates_exp"], 1)

            @block.tensor
            def _(pe):
                with pe.Fori(0, B // 2) as i:
                    n = [2 * i + 1, 2 * i + 2]
                    for b in R:
                        if b == 1:
                            pe.wait_ge(S["xnT_ready"], n[0])
                        held(pe, S["xn_ready"], n[b], pe_passed)
                        for t in range(TT):
                            mm = pe.transpose(ps_T[0:D, t * P:(t + 1) * P], xn[b][:, t, :], ident[:, :])
                        mm.then_inc(S["xnT_ps"], 1)
                    for b in R:
                        pe.wait_ge(S["xnT_ready"], n[b])
                        for c in range(HC0):
                            if b == 1:
                                pe.wait_ge(S["hid_ready"], 2 * HC0 * i + c + 1)
                            pe.matmul(ps_hid[c][:, :], w1[:, c * P:(c + 1) * P], xnT[b][:, :], start=True, stop=True).then_inc(S["hid_ps"], 1)
                    for b in R:
                        pe.wait_ge(S["hid_ready"], 2 * HC0 * i + HC0 * (b + 1))
                        if b == 1:
                            pe.wait_ge(S["gates_centred"], n[0])
                        for t in range(TT):
                            out = ps_g[:, t * EXPERTS:(t + 1) * EXPERTS]
                            for c in range(HC0):
                                pe.matmul(out, hidT[b][:, c, t * P:(t + 1) * P], wg[:, c, :], start=(c == 0), stop=False)
                            mm = pe.matmul(out, ones_row[:, :], bg[:, :], start=False, stop=True)
                        mm.then_inc(S["gates_ps"], 1)
                        for t in range(TT):
                            if b == 1:
                                pe.wait_ge(S["y_used"], 2 * TT * i + t + 1)
                            for c in range(HC0):
                                pe.matmul(ps_y[t][:, :], hidT[b][:, c, t * P:(t + 1) * P], wd[:, c, :], start=(c == 0), stop=False)
                            pe.matmul(ps_y[t][:, :], ones_row[:, :], bd[:, :], start=False, stop=True).then_inc(S["y_ps"], 1)

        clear_semaphores(nc, sems)


HEADS1 = 8
PAIRS = HEADS1 // 2
ROWS3 = 3 * NTOK


def project_qkv(nc, w, h_in, qkvT):
    with ExitStack() as ctx:
        def sb(name, shape, dt=F32):
            return ctx.enter_context(nc.sbuf_tensor("prj_" + name, shape, dt))

        def ps(name, shape):
            return ctx.enter_context(nc.psum_tensor("prj_" + name, shape, F32))

        sems = []

        def sem(name):
            sems.append(ctx.enter_context(nc.semaphore("prj_" + name)))
            return sems[-1]

        R = range(2)
        wqkv = sb("wqkv", [D + 1, 3, PAIRS, P])
        eps = sb("eps", [P, 1])
        ident = sb("ident", [P, P])
        x = [sb(f"x{b}", [P, TT, D]) for b in R]
        xn = [sb(f"xn{b}", [P, TT, D]) for b in R]
        stats = [sb(f"stats{b}", [P, TT, 6]) for b in R]
        moments = [sb(f"moments{b}", [P, TT, 2]) for b in R]
        std = [sb(f"std{b}", [P, TT]) for b in R]
        xnT = [sb(f"xnT{b}", [D + 1, T]) for b in R]
        rows = [sb(f"rows{k}", [P, T, 3]) for k in range(4)]
        ps_T = ps("ps_T", [P, T])
        ps_r = [ps(f"ps_r{k}", [P, T]) for k in range(6)]
        loaded, gp_made, x_used = sem("loaded"), sem("gp_made"), sem("x_used")
        x_in = [sem(f"x_in{b}") for b in R]
        stored = [sem(f"stored{k}") for k in range(4)]
        names = "moments_ready std_ready xn_ready xnT_ps xnT_ready rows_ps"
        S = {n: sem(n) for n in names.split()}
        rows_dve, rows_act = sem("rows_dve"), sem("rows_act")
        dve_steps, dve_passed, pe_passed = sem("dve_steps"), sem("dve_passed"), sem("pe_passed")

        with nc.Block() as block:
            @block.sync
            def _(sp):
                sp.dma_start(wqkv[0:D, :, :, :].rearrange("i c f m -> i (c f m)"), w["Wqkv_heads"]).then_inc(loaded, 16)
                sp.dma_start(wqkv[D:D + 1, :, :, :].rearrange("i c f m -> i (c f m)"), w["bqkv_heads"].unsqueeze(0)).then_inc(loaded, 16)
                sp.wait_ge(loaded, 32)

            @block.gpsimd
            def _(pool):
                pool.memset(ident[:, :], 0.0).then_inc(gp_made, 1)
                pool.wait_ge(gp_made, 1)
                pool.affine_select(out=ident[:, :], in_=ident[:, :], compare_op=ALU.not_equal, fill=1.0, base=0,
                                   pattern=[[-1, P]], channel_multiplier=1).then_inc(gp_made, 1)

            @block.vector
            def _(dve):
                dve.memset(eps[:, :], EPS)
                for b in R:
                    dve.memset(xnT[b][D:D + 1, :], 1.0)

        with nc.Block() as block:
            @block.sync
            def _(sp):
                sp.sem_inc(x_used, 2)
                for f in range(PAIRS):
                    sp.sem_inc(stored[f], 16)
                with sp.Fori(0, B // 2) as i:
                    for b in R:
                        sp.wait_ge(x_used, 2 * i + b + 1)
                        sp.dma_start(x[b][:, :, :], h_in[bass.ds((2 * i + b) * T, T), :].rearrange("(t p) d -> p t d", p=P)).then_inc(x_in[b], 16)
                    for b in R:
                        for f in range(PAIRS):
                            sp.wait_ge(rows_act, 4 * (2 * i + b) + f + 1)
                            sp.wait_ge(rows_dve, 4 * (2 * i + b) + f + 1)
                            sp.dma_start(qkvT[f, :, bass.ds((2 * i + b) * 3 * T, 3 * T)],
                                         rows[f][:, :, :].rearrange("p t c -> p (t c)")).then_inc(stored[f], 16)
                for f in range(PAIRS):
                    sp.wait_ge(stored[f], 16 * (B + 1))

            @block.vector
            def _(dve):
                s = Steps(dve, dve_steps)
                with dve.Fori(0, B // 2) as i:
                    n = [2 * i + 1, 2 * i + 2]
                    s.restart()
                    for b in R:
                        held(dve, x_in[b], 16 * i + 16, dve_passed)
                        ln_moments(dve, s, x[b], stats[b], moments[b])
                        dve.sem_inc(S["moments_ready"], 1)
                    for b in R:
                        dve.wait_ge(S["std_ready"], n[b])
                        s.did(ln_apply(dve, s, xn[b], x[b], moments[b], std[b]))
                        s.wait()
                        dve.sem_inc(S["xn_ready"], 1)
                        dve.sem_inc(x_used, 1)
                    for b in R:
                        dve.wait_ge(S["xnT_ps"], n[b])
                        dve.tensor_copy(xnT[b][0:D, :], ps_T[0:D, :]).then_inc(S["xnT_ready"], 1)
                    for b in R:
                        for f in range(PAIRS):
                            dve.wait_ge(stored[f], 16 * (2 * i + b) + 16)
                            dve.wait_ge(S["rows_ps"], 12 * (2 * i + b) + 3 * f + 1)
                            dve.tensor_copy(rows[f][:, :, 0], ps_r[3 * (f % 2)][:, :]).then_inc(rows_dve, 1)
                s.wait()

            @block.scalar
            def _(act):
                with act.Fori(0, B // 2) as i:
                    n = [2 * i + 1, 2 * i + 2]
                    for b in R:
                        act.wait_ge(S["moments_ready"], n[b])
                        act.activation(std[b][:, :], moments[b][:, :, 1], ACT.Sqrt, bias=eps[:, 0:1]).then_inc(S["std_ready"], 1)
                    for b in R:
                        for f in range(PAIRS):
                            act.wait_ge(stored[f], 16 * (2 * i + b) + 16)
                            for c in range(1, 3):
                                act.wait_ge(S["rows_ps"], 12 * (2 * i + b) + 3 * f + c + 1)
                                ins = act.activation(rows[f][:, :, c], ps_r[3 * (f % 2) + c][:, :], ACT.Copy)
                            ins.then_inc(rows_act, 1)

            @block.tensor
            def _(pe):
                with pe.Fori(0, B // 2) as i:
                    n = [2 * i + 1, 2 * i + 2]
                    for b in R:
                        if b == 1:
                            pe.wait_ge(S["xnT_ready"], n[0])
                        held(pe, S["xn_ready"], n[b], pe_passed)
                        for t in range(TT):
                            mm = pe.transpose(ps_T[0:D, t * P:(t + 1) * P], xn[b][:, t, :], ident[:, :])
                        mm.then_inc(S["xnT_ps"], 1)
                    for b in R:
                        pe.wait_ge(S["xnT_ready"], n[b])
                        for f in range(PAIRS):
                            if b or f >= 2:
                                pe.wait_ge(rows_dve, 4 * (2 * i + b) + f - 1)
                                pe.wait_ge(rows_act, 4 * (2 * i + b) + f - 1)
                            for c in range(3):
                                pe.matmul(ps_r[3 * (f % 2) + c][:, :], wqkv[:, c, f, :], xnT[b][:, :], start=True, stop=True).then_inc(S["rows_ps"], 1)

        clear_semaphores(nc, sems)


def diagonal_attention(nc, w, qkvT, h_in, h_out):
    with ExitStack() as ctx:
        def sb(name, shape, dt=F32):
            return ctx.enter_context(nc.sbuf_tensor("dia_" + name, shape, dt))

        def ps(name, shape):
            return ctx.enter_context(nc.psum_tensor("dia_" + name, shape, F32))

        sems = []

        def sem(name):
            sems.append(ctx.enter_context(nc.semaphore("dia_" + name)))
            return sems[-1]

        R = range(2)
        SCALE = float(D) ** -0.5
        UN = TT * HEADS1
        w0 = sb("w0", [P, PAIRS, 2 * D])
        b0 = sb("b0", [P, D])
        ident = sb("ident", [P, P])
        qT = [sb(f"qT{b}", [P, PAIRS, T]) for b in R]
        kT = [sb(f"kT{b}", [P, PAIRS, T]) for b in R]
        vT = [sb(f"vT{b}", [P, PAIRS, T]) for b in R]
        x = [sb(f"x{b}", [P, TT, D]) for b in R]
        negmax = [sb(f"negmax{b}", [P, UN]) for b in R]
        bias = [sb(f"bias{b}", [P, UN]) for b in R]
        diag = [sb(f"diag{b}", [P, UN]) for b in R]
        sums = [sb(f"sums{b}", [P, UN]) for b in R]
        attn = [sb(f"attn{b}", [P, UN]) for b in R]
        diag_out = [sb(f"diag_out{k}", [P, P]) for k in R]
        exp_out = [sb(f"exp_out{k}", [P, T]) for k in R]
        weighted = [sb(f"weighted{k}", [P, HEADS1, D]) for k in R]
        y = [sb(f"y{b}", [P, TT, D]) for b in R]
        ps_s = [ps(f"ps_s{k}", [P, T]) for k in range(4)]
        ps_v = [ps(f"ps_v{k}", [P, T]) for k in range(4)]
        zeroed, loaded, gp_made = sem("zeroed"), sem("loaded"), sem("gp_made")
        seq_in = [sem(f"seq_in{b}") for b in R]
        stored = [sem(f"stored{b}") for b in R]
        names = "scores_ps bias_ready scores_used attn_pre attn_exp values_ps values_used y_ready seq_used"
        S = {n: sem(n) for n in names.split()}
        dve_steps, dve_passed, pe_passed = sem("dve_steps"), sem("dve_passed"), sem("pe_passed")

        with nc.Block() as block:
            @block.sync
            def _(sp):
                sp.dma_start(b0[:, :], w["b0"].partition_broadcast(P)).then_inc(loaded, 16)
                sp.wait_ge(zeroed, 1)
                for hh in range(2):
                    sp.dma_start(w0[hh * D:(hh + 1) * D, :, hh * D:(hh + 1) * D],
                                 w["W0_heads"].rearrange("(f a) d o -> a d f o", a=2)[hh]).then_inc(loaded, 16)
                sp.wait_ge(loaded, 48)

            @block.gpsimd
            def _(pool):
                pool.memset(ident[:, :], 0.0).then_inc(gp_made, 1)
                pool.wait_ge(gp_made, 1)
                pool.affine_select(out=ident[:, :], in_=ident[:, :], compare_op=ALU.not_equal, fill=1.0, base=0,
                                   pattern=[[-1, P]], channel_multiplier=1).then_inc(gp_made, 1)

            @block.vector
            def _(dve):
                dve.memset(w0[:, :, :], 0.0).then_inc(zeroed, 1)

        with nc.Block() as block:
            @block.sync
            def _(sp):
                sp.sem_inc(S["seq_used"], 2)
                with sp.Fori(0, B // 2) as i:
                    for b in R:
                        sp.wait_ge(S["seq_used"], 2 * i + b + 1)
                        for m, dst in enumerate((qT[b], kT[b], vT[b])):
                            src = qkvT[:, :, bass.ds((2 * i + b) * T + m * NTOK, T)].rearrange("f p t -> p f t")
                            sp.dma_start(dst[:, :, :], src).then_inc(seq_in[b], 16)
                        sp.dma_start(x[b][:, :, :], h_in[bass.ds((2 * i + b) * T, T), :].rearrange("(t p) d -> p t d", p=P)).then_inc(seq_in[b], 16)
                    for b in R:
                        sp.wait_ge(S["y_ready"], 2 * i + b + 1)
                        sp.dma_start(h_out[bass.ds((2 * i + b) * T, T), :].rearrange("(t p) d -> p t d", p=P), y[b][:, :, :]).then_inc(stored[b], 16)
                for b in R:
                    sp.wait_ge(stored[b], 16 * B // 2)

            @block.vector
            def _(dve):
                s = Steps(dve, dve_steps)
                with dve.Fori(0, B // 2) as i:
                    n = [2 * i + 1, 2 * i + 2]
                    s.restart()
                    for b in R:
                        for u in range(UN):
                            t = u // HEADS1
                            dve.wait_ge(S["scores_ps"], UN * (2 * i + b) + u + 1)
                            s.did(dve.tensor_tensor(diag_out[u % 2][:, :], ps_s[u % 4][:, t * P:(t + 1) * P], ident[:, :], ALU.mult))
                            s.did(dve.tensor_reduce(negmax[b][:, u:u + 1], ps_s[u % 4][:, :], AX.X, ALU.max, negate=True))
                            s.wait()
                            s.did(dve.tensor_reduce(diag[b][:, u:u + 1], diag_out[u % 2][:, :], AX.X, ALU.add))
                            dve.tensor_scalar(bias[b][:, u:u + 1], negmax[b][:, u:u + 1], SCALE, None, ALU.mult).then_inc(S["bias_ready"], 1)
                        dve.wait_ge(S["bias_ready"], UN * (2 * i + b + 1))
                        dve.scalar_tensor_tensor(attn[b][:, :], diag[b][:, :], SCALE, bias[b][:, :], ALU.mult, ALU.add).then_inc(S["attn_pre"], 1)
                        dve.wait_ge(S["attn_exp"], n[b])
                        s.did(dve.reciprocal(sums[b][:, :], sums[b][:, :]))
                        s.wait()
                        s.did(dve.tensor_tensor(attn[b][:, :], attn[b][:, :], sums[b][:, :], ALU.mult))
                        s.did(dve.tensor_tensor(x[b][:, :, :], x[b][:, :, :], bc(b0[:, :], 1, TT), ALU.add))
                        s.wait()
                        for t in range(TT):
                            dve.wait_ge(S["values_ps"], TT * (2 * i + b) + t + 1)
                            dve.tensor_tensor(weighted[t % 2][:, :, :], ps_v[t][:, :].rearrange("p (h o) -> p h o", o=D),
                                              bc(attn[b][:, t * HEADS1:(t + 1) * HEADS1], 2, D), ALU.mult).then_inc(S["values_used"], 1)
                            dve.wait_ge(S["values_used"], TT * (2 * i + b) + t + 1)
                            s.did(dve.tensor_reduce(y[b][:, t, :], weighted[t % 2][:, :, :].rearrange("p h o -> p o h"), AX.X, ALU.add))
                            s.wait()
                        s.did(dve.tensor_tensor(y[b][:, :, :], y[b][:, :, :], x[b][:, :, :], ALU.add))
                        s.wait()
                        dve.sem_inc(S["y_ready"], 1)
                        dve.sem_inc(S["seq_used"], 1)
                s.wait()

            @block.scalar
            def _(act):
                with act.Fori(0, B // 2) as i:
                    for b in R:
                        for u in range(UN):
                            act.wait_ge(S["bias_ready"], UN * (2 * i + b) + u + 1)
                            if b or u >= 2:
                                act.wait_ge(S["scores_used"], UN * (2 * i + b) + u - 1)
                            act.activation(exp_out[u % 2][:, :], ps_s[u % 4][:, :], ACT.Exp, bias=bias[b][:, u:u + 1], scale=SCALE,
                                           accum_out=sums[b][:, u:u + 1]).then_inc(S["scores_used"], 1)
                        act.wait_ge(S["attn_pre"], 2 * i + b + 1)
                        act.activation(attn[b][:, :], attn[b][:, :], ACT.Exp).then_inc(S["attn_exp"], 1)

            @block.tensor
            def _(pe):
                with pe.Fori(0, B // 2) as i:
                    for b in R:
                        pe.wait_ge(seq_in[b], 64 * (i + 1))
                        for u in range(UN):
                            t, h = u // HEADS1, u % HEADS1
                            r = slice((h % 2) * D, (h % 2 + 1) * D)
                            if b or u >= 4:
                                pe.wait_ge(S["scores_used"], UN * (2 * i + b) + u - 3)
                            pe.matmul(ps_s[u % 4][:, :], kT[b][r, h // 2, t * P:(t + 1) * P], qT[b][r, h // 2, :],
                                      start=True, stop=True).then_inc(S["scores_ps"], 1)
                            if h == HEADS1 - 1:
                                if b:
                                    pe.wait_ge(S["values_used"], TT * (2 * i) + t + 1)
                                for f in range(PAIRS):
                                    mm = pe.matmul(ps_v[t][:, f * P:(f + 1) * P], vT[b][:, f, t * P:(t + 1) * P], w0[:, f, :], start=True, stop=True)
                                mm.then_inc(S["values_ps"], 1)

        clear_semaphores(nc, sems)


HEADS2, NKEYS, DKEY, TOPK = 8, 64, 32, 16
NKV = NKEYS * NKEYS
GROUPS = 2 * HEADS2
TILES = NTOK // P
LOW = -3.0e38
RUNS, _a = [], 0
while _a < TOPK:
    _n = TOPK // (_a + 1)
    _e = _a
    while _e < TOPK and TOPK // (_e + 1) == _n:
        _e += 1
    RUNS.append((_a, _e, _n))
    _a = _e
CANDS = sum((e - a) * n for a, e, n in RUNS)
KV = 2 * D
GSLOTS = 4


def product_keys(nc, w, h_in, qT_out, kv_out):
    with ExitStack() as ctx:
        def sb(name, shape, dt=F32):
            return ctx.enter_context(nc.sbuf_tensor("pk_" + name, shape, dt))

        def ps(name, shape):
            return ctx.enter_context(nc.psum_tensor("pk_" + name, shape, F32))

        sems = []

        def sem(name):
            sems.append(ctx.enter_context(nc.semaphore("pk_" + name)))
            return sems[-1]

        R = range(2)
        wpkT = sb("wpkT", [DKEY, GROUPS, D])
        keysT = sb("keysT", [DKEY, GROUPS, NKEYS])
        wsim = sb("wsim", [D, GROUPS * NKEYS])
        wq = sb("wq", [D, HEADS2 * D])
        eps = sb("eps", [P, 1])
        ident = sb("ident", [P, P])
        head_base_i = sb("head_base_i", [P, HEADS2], I32)
        head_base = sb("head_base", [P, HEADS2])
        cand_id_i = sb("cand_id_i", [P, CANDS], I32)
        cand_id = sb("cand_id", [P, CANDS])
        x = [sb(f"x{b}", [P, D]) for b in R]
        xn = [sb(f"xn{b}", [P, D]) for b in R]
        stats = [sb(f"stats{b}", [P, 6]) for b in R]
        moments = [sb(f"moments{b}", [P, 2]) for b in R]
        std = [sb(f"std{b}", [P, 1]) for b in R]
        xnT = [sb(f"xnT{b}", [D, P]) for b in R]
        qT = [sb(f"qT{b}", [P, PAIRS, P]) for b in R]
        sim = [sb(f"sim{b}", [P, GROUPS, NKEYS]) for b in R]
        sim_rest = sb("sim_rest", [P, GROUPS, NKEYS])
        top = sb("top", [P, GROUPS, TOPK])
        top_at = sb("top_at", [P, GROUPS, TOPK], U32)
        top_at_f = sb("top_at_f", [P, GROUPS, TOPK])
        cand = sb("cand", [P, HEADS2, CANDS])
        cand_rest = sb("cand_rest", [P, HEADS2, CANDS])
        cand_row = sb("cand_row", [P, HEADS2, CANDS])
        best = sb("best", [P, HEADS2, TOPK])
        best_at = sb("best_at", [P, HEADS2, TOPK], U32)
        best_at_f = sb("best_at_f", [P, HEADS2, TOPK])
        is_cand = [sb(f"is_cand{k}", [P, TOPK, CANDS]) for k in R]
        row_f = sb("row_f", [P, HEADS2, TOPK])
        row = [sb(f"row{b}", [P, HEADS2, TOPK], I32) for b in R]
        weight = [sb(f"weight{b}", [P, HEADS2, TOPK]) for b in R]
        wsum = sb("wsum", [P, HEADS2])
        rows = [sb(f"rows{k}", [P, TOPK, KV]) for k in range(GSLOTS)]
        scaled = [sb(f"scaled{k}", [P, TOPK, KV]) for k in R]
        kv = [sb(f"kv{b}", [P, 2, HEADS2, D]) for b in R]
        ps_T = ps("ps_T", [P, 512])
        ps_q = ps("ps_q", [P, PAIRS, P])
        ps_sim = [ps(f"ps_sim{k}", [P, 512]) for k in range(4)]
        ps_w = ps("ps_w", [P, 512])
        loaded, gp_made, dve_made, pe_made = sem("loaded"), sem("gp_made"), sem("dve_made"), sem("pe_made")
        x_in = [sem(f"x_in{b}") for b in R]
        q_stored = [sem(f"q_stored{b}") for b in R]
        kv_stored = [sem(f"kv_stored{b}") for b in R]
        gathered = [nc.alloc_semaphore(f"pk_gathered{k}") for k in range(GSLOTS)]
        names = ("x_used moments_ready std_ready xn_ready xnT_ps xnT_ready q_ps q_ready sim_ps sim_ready sim_used "
                 "best_centred weight_exp row_ready rows_used kv_ready")
        S = {n: sem(n) for n in names.split()}
        sp_passed = sem("sp_passed")
        dve_steps, dve_passed, pe_passed, pool_passed = sem("dve_steps"), sem("dve_passed"), sem("pe_passed"), sem("pool_passed")

        with nc.Block() as block:
            @block.sync
            def _(sp):
                for dst, src in ((wpkT, "Wq_pkT"), (keysT, "keysT")):
                    sp.dma_start(dst[:, :, :], w[src]).then_inc(loaded, 16)
                sp.dma_start(wq[:, :], w["Wq"]).then_inc(loaded, 16)
                sp.wait_ge(loaded, 48)

            @block.gpsimd
            def _(pool):
                pool.iota(head_base_i[:, :], [[NKV, HEADS2]], base=0, channel_multiplier=0).then_inc(gp_made, 1)
                pool.iota(cand_id_i[:, :], [[1, CANDS]], base=0, channel_multiplier=0).then_inc(gp_made, 1)
                pool.memset(ident[:, :], 0.0).then_inc(gp_made, 1)
                pool.wait_ge(gp_made, 3)
                pool.affine_select(out=ident[:, :], in_=ident[:, :], compare_op=ALU.not_equal, fill=1.0, base=0,
                                   pattern=[[-1, P]], channel_multiplier=1).then_inc(gp_made, 1)

            @block.tensor
            def _(pe):
                pe.wait_ge(loaded, 48)
                for g in range(GROUPS):
                    if g == 8:
                        pe.wait_ge(dve_made, 1)
                    mm = pe.matmul(ps_w[0:D, (g % 8) * NKEYS:(g % 8 + 1) * NKEYS], wpkT[:, g, :], keysT[:, g, :], start=True, stop=True)
                    if g % 8 == 7:
                        mm.then_inc(pe_made, 1)

            @block.vector
            def _(dve):
                dve.memset(eps[:, :], EPS)
                dve.wait_ge(gp_made, 4)
                dve.tensor_copy(head_base[:, :], head_base_i[:, :])
                dve.tensor_copy(cand_id[:, :], cand_id_i[:, :])
                for half in R:
                    dve.wait_ge(pe_made, half + 1)
                    dve.tensor_copy(wsim[:, half * 512:(half + 1) * 512], ps_w[0:D, :]).then_inc(dve_made, 1)

        with nc.Block() as block:
            @block.sync
            def _(sp):
                for b in R:
                    sp.sem_inc(q_stored[b], 16)
                    sp.sem_inc(kv_stored[b], 16)
                    sp.dma_start(x[b][:, :], h_in[b * P:(b + 1) * P, :]).then_inc(x_in[b], 16)

                def store_queries(b, i):
                    held(sp, S["q_ready"], 2 * i + b + 1, sp_passed)
                    sp.dma_start(qT_out[:, :, bass.ds((2 * i + b) * P, P)].rearrange("f p t -> p f t"), qT[b][:, :, :]).then_inc(q_stored[b], 16)

                def store_mixtures(b, i):
                    sp.wait_ge(S["kv_ready"], 2 * i + b + 1)
                    sp.dma_start(kv_out[bass.ds((2 * i + b) * P, P), :], kv[b][:, :, :, :].rearrange("p m h c -> p (m h c)")).then_inc(kv_stored[b], 16)

                with sp.Fori(0, TILES // 2 - 1) as i:
                    for b in R:
                        store_queries(b, i)
                    for b in R:
                        sp.wait_ge(S["x_used"], 2 * i + b + 1)
                        sp.dma_start(x[b][:, :], h_in[bass.ds((2 * i + 2 + b) * P, P), :]).then_inc(x_in[b], 16)
                    for b in R:
                        store_mixtures(b, i)
                for b in R:
                    store_queries(b, TILES // 2 - 1)
                for b in R:
                    store_mixtures(b, TILES // 2 - 1)
                for b in R:
                    sp.wait_ge(q_stored[b], 16 * (TILES // 2 + 1))
                    sp.wait_ge(kv_stored[b], 16 * (TILES // 2 + 1))

            @block.gpsimd
            def _(pool):
                pool.sem_inc(S["rows_used"], GSLOTS)
                with pool.Fori(0, TILES // 2) as i:
                    for b in R:
                        held(pool, S["row_ready"], 2 * i + b + 1, pool_passed)
                        for h in range(HEADS2):
                            held(pool, S["rows_used"], HEADS2 * (2 * i + b) + h + 1, pool_passed)
                            for j in range(TOPK):
                                pool.indirect_dma_start(rows[h % GSLOTS][:, j, :], None, w["table"],
                                                        bass.IndirectOffsetOnAxis(row[b][:, h, j:j + 1], 0)).then_inc(gathered[h % GSLOTS], 16)

            @block.tensor
            def _(pe):
                with pe.Fori(0, TILES // 2) as i:
                    for b in R:
                        n = 2 * i + b + 1
                        held(pe, S["xn_ready"], n, pe_passed)
                        pe.transpose(ps_T[0:D, b * P:(b + 1) * P], xn[b][:, :], ident[:, :]).then_inc(S["xnT_ps"], 1)
                        pe.wait_ge(S["xnT_ready"], n)
                        for k in R:
                            pe.matmul(ps_sim[2 * b + k][:, :], xnT[b][:, :], wsim[:, k * 512:(k + 1) * 512], start=True, stop=True).then_inc(S["sim_ps"], 1)
                        for f in range(PAIRS):
                            mm = pe.matmul(ps_q[:, f, :], wq[:, f * P:(f + 1) * P], xnT[b][:, :], start=True, stop=True)
                        mm.then_inc(S["q_ps"], 1)
                        pe.wait_ge(S["q_ready"], n)

            @block.scalar
            def _(act):
                with act.Fori(0, TILES // 2) as i:
                    for b in R:
                        n = 2 * i + b + 1
                        act.wait_ge(S["moments_ready"], n)
                        act.activation(std[b][:, :], moments[b][:, 1:2], ACT.Sqrt, bias=eps[:, 0:1]).then_inc(S["std_ready"], 1)
                        act.wait_ge(S["xnT_ps"], n)
                        act.activation(xnT[b][:, :], ps_T[0:D, b * P:(b + 1) * P], ACT.Copy).then_inc(S["xnT_ready"], 1)
                        for k in R:
                            act.wait_ge(S["sim_ps"], 2 * (2 * i + b) + k + 1)
                            ins = act.activation(sim[b][:, k * HEADS2:(k + 1) * HEADS2, :], ps_sim[2 * b + k][:, :].rearrange("p (g k) -> p g k", k=NKEYS), ACT.Copy)
                        ins.then_inc(S["sim_ready"], 1)
                        act.wait_ge(S["q_ps"], n)
                        act.wait_ge(q_stored[b], 16 * i + 16)
                        act.activation(qT[b][:, :, :], ps_q[:, :, :], ACT.Copy, scale=float(D) ** -0.5).then_inc(S["q_ready"], 1)
                        act.wait_ge(S["best_centred"], n)
                        act.activation(weight[b][:, :, :], weight[b][:, :, :], ACT.Exp).then_inc(S["weight_exp"], 1)

            @block.vector
            def _(dve):
                s = Steps(dve, dve_steps)

                def normalise(b, i):
                    held(dve, x_in[b], 16 * i + 16, dve_passed)
                    s.did(dve.bn_stats(stats[b][:, :], x[b][:, :]))
                    s.wait()
                    s.did(dve.bn_aggr(moments[b][:, :], stats[b][:, :]))
                    s.wait()
                    dve.sem_inc(S["moments_ready"], 1)
                    dve.wait_ge(S["std_ready"], 2 * i + b + 1)
                    s.did(dve.reciprocal(std[b][:, :], std[b][:, :]))
                    s.wait()
                    s.did(dve.tensor_scalar(xn[b][:, :], x[b][:, :], moments[b][:, 0:1], std[b][:, 0:1], ALU.subtract, ALU.mult))
                    s.wait()
                    dve.sem_inc(S["xn_ready"], 1)
                    dve.sem_inc(S["x_used"], 1)

                def top16(groups, values, at, source, rest):
                    for g in range(groups):
                        s.did(dve.max(values[:, g, 0:8], source[:, g, :]))
                    s.wait()
                    for g in range(groups):
                        s.did(dve.match_replace(rest[:, g, :], values[:, g, 0:8], source[:, g, :], LOW))
                        s.did(dve.max_index(at[:, g, 0:8], values[:, g, 0:8], source[:, g, :]))
                    s.wait()
                    for g in range(groups):
                        s.did(dve.max(values[:, g, 8:16], rest[:, g, :]))
                    s.wait()
                    for g in range(groups):
                        s.did(dve.max_index(at[:, g, 8:16], values[:, g, 8:16], rest[:, g, :]))
                    s.wait()

                def choose(b, i):
                    held(dve, S["sim_ready"], 2 * i + b + 1, dve_passed)
                    top16(GROUPS, top, top_at, sim[b], sim_rest)
                    s.did(dve.tensor_copy(top_at_f[:, :, :], top_at[:, :, :]))
                    s.wait()
                    second = top_at_f[:, HEADS2:GROUPS, :]
                    s.did(dve.tensor_scalar(second, second, float(NKEYS), None, ALU.mult))
                    s.wait()
                    s.did(dve.tensor_tensor(second, second, bc(head_base[:, :], 2, TOPK), ALU.add))
                    s.wait()
                    at = 0
                    for a0, a1, nb in RUNS:
                        na = a1 - a0
                        for src, dst in ((top, cand), (top_at_f, cand_row)):
                            s.did(dve.tensor_tensor(
                                dst[:, :, at:at + na * nb].rearrange("p h (a b) -> p h a b", b=nb),
                                bc(src[:, 0:HEADS2, a0:a1], 3, nb), bc(src[:, HEADS2:GROUPS, 0:nb], 2, na), ALU.add))
                        at += na * nb
                    s.wait()
                    top16(HEADS2, best, best_at, cand, cand_rest)
                    dve.tensor_tensor(weight[b][:, :, :], best[:, :, :], best[:, :, 0:1].broadcast_to([P, HEADS2, TOPK]), ALU.subtract).then_inc(S["best_centred"], 1)
                    s.did(dve.tensor_copy(best_at_f[:, :, :], best_at[:, :, :]))
                    s.wait()
                    for h in range(HEADS2):
                        eq = is_cand[h % 2][:, :, :]
                        s.did(dve.tensor_tensor(eq, bc(cand_id[:, :], 1, TOPK), bc(best_at_f[:, h, :], 2, CANDS), ALU.is_equal))
                        s.wait()
                        s.did(dve.tensor_tensor(eq, eq, bc(cand_row[:, h, :], 1, TOPK), ALU.mult))
                        s.wait()
                        s.did(dve.tensor_reduce(row_f[:, h, :], eq, AX.X, ALU.add))
                    s.wait()
                    s.did(dve.tensor_copy(row[b][:, :, :], row_f[:, :, :]))
                    s.wait()
                    dve.sem_inc(S["row_ready"], 1)
                    dve.wait_ge(S["weight_exp"], 2 * i + b + 1)
                    s.did(dve.tensor_reduce(wsum[:, :], weight[b][:, :, :], AX.X, ALU.add))
                    s.wait()
                    s.did(dve.reciprocal(wsum[:, :], wsum[:, :]))
                    s.wait()
                    s.did(dve.tensor_tensor(weight[b][:, :, :], weight[b][:, :, :], bc(wsum[:, :], 2, TOPK), ALU.mult))
                    s.wait()

                def mix(b, i):
                    dve.wait_ge(kv_stored[b], 16 * i + 16)
                    for h in range(HEADS2):
                        dve.wait_ge(gathered[h % GSLOTS], 16 * TOPK * ((2 * i + b) * (HEADS2 // GSLOTS) + h // GSLOTS + 1))
                        s.did(dve.tensor_tensor(scaled[h % 2][:, :, :], rows[h % GSLOTS][:, :, :], bc(weight[b][:, h, :], 2, KV), ALU.mult))
                        s.wait()
                        dve.sem_inc(S["rows_used"], 1)
                        s.did(dve.tensor_reduce(kv[b][:, :, h, :], scaled[h % 2][:, :, :].rearrange("p j (m c) -> p m c j", m=2), AX.X, ALU.add))
                    s.wait()
                    dve.sem_inc(S["kv_ready"], 1)

                normalise(0, 0)
                choose(0, 0)
                last = TILES // 2 - 1
                with dve.Fori(0, last) as i:
                    s.restart()
                    for b in R:
                        normalise(1 - b, i + b)
                        choose(1 - b, i + b)
                        mix(b, i)
                s.restart()
                normalise(1, last)
                choose(1, last)
                mix(0, last)
                mix(1, last)

        clear_semaphores(nc, sems)


def causal_attention(nc, w, qT_in, kv_in, h_in, h_out):
    with ExitStack() as ctx:
        def sb(name, shape, dt=F32):
            return ctx.enter_context(nc.sbuf_tensor("cau_" + name, shape, dt))

        def ps(name, shape):
            return ctx.enter_context(nc.psum_tensor("cau_" + name, shape, F32))

        sems = []

        def sem(name):
            sems.append(ctx.enter_context(nc.semaphore("cau_" + name)))
            return sems[-1]

        R = range(2)
        MASKED = -1.0e30
        wo = sb("wo", [P, PAIRS, D])
        ident = sb("ident", [P, P])
        future = sb("future", [P, P])
        x = [sb(f"x{b}", [P, TT, D]) for b in R]
        qT = [sb(f"qT{b}", [P, PAIRS, T]) for b in R]
        kv = [sb(f"kv{b}", [P, TT, 2, HEADS2, D]) for b in R]
        kT = sb("kT", [P, PAIRS, T])
        UN = TT * HEADS2
        negmax = sb("negmax", [P, UN])
        sums = sb("sums", [P, UN])
        inv = sb("inv", [P, UN])
        prob = [sb(f"prob{k}", [P, T]) for k in R]
        probT = [sb(f"probT{k}", [P, T]) for k in R]
        out = sb("out", [P, TT, HEADS2, D])
        outT = sb("outT", [P, PAIRS, T])
        y = [sb(f"y{b}", [P, TT, D]) for b in R]
        ps_s = [ps(f"ps_s{k}", [P, T]) for k in range(3)]
        ps_pT = [ps(f"ps_pT{k}", [P, T]) for k in R]
        ps_o = [ps(f"ps_o{k}", [P, T]) for k in R]
        ps_k = ps("ps_k", [P, T])
        loaded, gp_made = sem("loaded"), sem("gp_made")
        seq_in = [sem(f"seq_in{b}") for b in R]
        stored = [sem(f"stored{b}") for b in R]
        names = ("seq_used kT_ps kT_ready scores_ps max_ready probs_ready pT_ps pT_ready out_ps out_part "
                 "oT_ps oT_ready y_ps y_ready")
        S = {n: sem(n) for n in names.split()}
        dve_steps, pe_passed = sem("dve_steps"), sem("pe_passed")

        with nc.Block() as block:
            @block.sync
            def _(sp):
                sp.dma_start(wo[:, :, :], w["Wo"].rearrange("(f p) o -> p f o", p=P)).then_inc(loaded, 16)
                sp.wait_ge(loaded, 16)

            @block.gpsimd
            def _(pool):
                pool.memset(ident[:, :], 0.0).then_inc(gp_made, 1)
                pool.memset(future[:, :], 0.0).then_inc(gp_made, 1)
                pool.wait_ge(gp_made, 2)
                pool.affine_select(out=ident[:, :], in_=ident[:, :], compare_op=ALU.not_equal, fill=1.0, base=0,
                                   pattern=[[-1, P]], channel_multiplier=1).then_inc(gp_made, 1)
                pool.affine_select(out=future[:, :], in_=future[:, :], compare_op=ALU.is_ge, fill=MASKED, base=0,
                                   pattern=[[-1, P]], channel_multiplier=1).then_inc(gp_made, 1)

        with nc.Block() as block:
            @block.sync
            def _(sp):
                sp.sem_inc(S["seq_used"], 2)
                with sp.Fori(0, B // 2) as i:
                    for b in R:
                        sp.wait_ge(S["seq_used"], 2 * i + b + 1)
                        sp.dma_start(kv[b][:, :, :, :, :].rearrange("p t m h c -> p t (m h c)"),
                                     kv_in[bass.ds((2 * i + b) * T, T), :].rearrange("(t p) c -> p t c", p=P)).then_inc(seq_in[b], 16)
                        sp.dma_start(qT[b][:, :, :], qT_in[:, :, bass.ds((2 * i + b) * T, T)].rearrange("f p t -> p f t")).then_inc(seq_in[b], 16)
                        sp.dma_start(x[b][:, :, :], h_in[bass.ds((2 * i + b) * T, T), :].rearrange("(t p) d -> p t d", p=P)).then_inc(seq_in[b], 16)
                    for b in R:
                        sp.wait_ge(S["y_ready"], 2 * i + b + 1)
                        sp.dma_start(h_out[bass.ds((2 * i + b) * T, T), :].rearrange("(t p) d -> p t d", p=P), y[b][:, :, :]).then_inc(stored[b], 16)
                for b in R:
                    sp.wait_ge(stored[b], 16 * B // 2)

            @block.tensor
            def _(pe):
                with pe.Fori(0, B // 2) as i:
                    for b in R:
                        u0 = UN * (2 * i + b)
                        held(pe, seq_in[b], 48 * (i + 1), pe_passed)
                        for f in range(PAIRS):
                            if b or f:
                                pe.wait_ge(S["kT_ready"], PAIRS * (2 * i + b) + f)
                            for t in range(TT):
                                mm = pe.transpose(ps_k[:, t * P:(t + 1) * P], kv[b][:, t, 0, 2 * f:2 * f + 2, :].rearrange("p h c -> p (h c)"), ident[:, :])
                            mm.then_inc(S["kT_ps"], 1)
                        pe.wait_ge(S["kT_ready"], PAIRS * (2 * i + b + 1))

                        def scores(u):
                            t, h = u // HEADS2, u % HEADS2
                            r = slice((h % 2) * D, (h % 2 + 1) * D)
                            if b or u >= 3:
                                pe.wait_ge(S["probs_ready"], u0 + u - 2)
                            q = qT[b][r, h // 2, t * P:(t + 1) * P]
                            own = slice(t * P, (t + 1) * P)
                            if t:
                                pe.matmul(ps_s[u % 3][:, 0:t * P], q, kT[r, h // 2, 0:t * P], start=True, stop=True)
                            pe.matmul(ps_s[u % 3][:, own], q, kT[r, h // 2, own], start=True, stop=False)
                            pe.matmul(ps_s[u % 3][:, own], ident[:, :], future[:, :], start=False, stop=True).then_inc(S["scores_ps"], 1)

                        def transposes(u):
                            t = u // HEADS2
                            pe.wait_ge(S["probs_ready"], u0 + u + 1)
                            if b or u >= 2:
                                pe.wait_ge(S["pT_ready"], u0 + u - 1)
                            for k in range(t + 1):
                                mm = pe.transpose(ps_pT[u % 2][:, k * P:(k + 1) * P], prob[u % 2][:, k * P:(k + 1) * P], ident[:, :])
                            mm.then_inc(S["pT_ps"], 1)

                        def values(u):
                            t, h = u // HEADS2, u % HEADS2
                            pe.wait_ge(S["pT_ready"], u0 + u + 1)
                            if b or u >= 2:
                                pe.wait_ge(S["out_part"], u0 + u - 1)
                            for k in range(t + 1):
                                mm = pe.matmul(ps_o[u % 2][:, 0:D], probT[u % 2][:, k * P:(k + 1) * P], kv[b][:, k, 1, h, :],
                                               start=(k == 0), stop=(k == t))
                            mm.then_inc(S["out_ps"], 1)

                        for step in range(UN + 2):
                            if step < UN:
                                scores(step)
                            if 1 <= step <= UN:
                                transposes(step - 1)
                            if step >= 2:
                                values(step - 2)
                        pe.wait_ge(S["out_part"], u0 + UN)
                        for f in range(PAIRS):
                            if f:
                                pe.wait_ge(S["oT_ready"], PAIRS * (2 * i + b) + f)
                            for t in range(TT):
                                mm = pe.transpose(ps_k[:, t * P:(t + 1) * P], out[:, t, 2 * f:2 * f + 2, :].rearrange("p h c -> p (h c)"), ident[:, :])
                            mm.then_inc(S["oT_ps"], 1)
                        pe.wait_ge(S["oT_ready"], PAIRS * (2 * i + b + 1))
                        for t in range(TT):
                            for f in range(PAIRS):
                                mm = pe.matmul(ps_k[:, t * D:(t + 1) * D], outT[:, f, t * P:(t + 1) * P], wo[:, f, :], start=(f == 0), stop=(f == PAIRS - 1))
                        mm.then_inc(S["y_ps"], 1)
                        pe.wait_ge(S["y_ready"], 2 * i + b + 1)

            @block.scalar
            def _(act):
                with act.Fori(0, B // 2) as i:
                    for b in R:
                        u0 = UN * (2 * i + b)
                        for f in range(PAIRS):
                            act.wait_ge(S["kT_ps"], PAIRS * (2 * i + b) + f + 1)
                            act.activation(kT[:, f, :], ps_k[:, :], ACT.Copy).then_inc(S["kT_ready"], 1)
                        for u in range(UN):
                            w_ = (u // HEADS2 + 1) * P
                            act.wait_ge(S["max_ready"], u0 + u + 1)
                            if b or u >= 2:
                                act.wait_ge(S["pT_ps"], u0 + u - 1)
                            act.activation(prob[u % 2][:, 0:w_], ps_s[u % 3][:, 0:w_], ACT.Exp, bias=negmax[:, u:u + 1],
                                           accum_out=sums[:, u:u + 1]).then_inc(S["probs_ready"], 1)
                        for f in range(PAIRS):
                            act.wait_ge(S["oT_ps"], PAIRS * (2 * i + b) + f + 1)
                            act.activation(outT[:, f, :], ps_k[:, :], ACT.Copy).then_inc(S["oT_ready"], 1)

            @block.vector
            def _(dve):
                s = Steps(dve, dve_steps)
                with dve.Fori(0, B // 2) as i:
                    s.restart()
                    for b in R:
                        u0 = UN * (2 * i + b)

                        def maximum(u):
                            w_ = (u // HEADS2 + 1) * P
                            dve.wait_ge(S["scores_ps"], u0 + u + 1)
                            dve.tensor_reduce(negmax[:, u:u + 1], ps_s[u % 3][:, 0:w_], AX.X, ALU.max, negate=True).then_inc(S["max_ready"], 1)

                        def transposed(u):
                            w_ = (u // HEADS2 + 1) * P
                            dve.wait_ge(S["pT_ps"], u0 + u + 1)
                            if b or u >= 2:
                                dve.wait_ge(S["out_ps"], u0 + u - 1)
                            dve.tensor_copy(probT[u % 2][:, 0:w_], ps_pT[u % 2][:, 0:w_]).then_inc(S["pT_ready"], 1)
                            s.did(dve.reciprocal(inv[:, u:u + 1], sums[:, u:u + 1]))

                        def normalise(u):
                            t, h = u // HEADS2, u % HEADS2
                            dve.wait_ge(S["out_ps"], u0 + u + 1)
                            s.wait()
                            dve.tensor_scalar(out[:, t, h, :], ps_o[u % 2][:, 0:D], inv[:, u:u + 1], None, ALU.mult).then_inc(S["out_part"], 1)

                        for step in range(UN + 2):
                            if step < UN:
                                maximum(step)
                            if 1 <= step <= UN:
                                transposed(step - 1)
                            if step >= 2:
                                normalise(step - 2)
                        dve.wait_ge(S["y_ps"], 2 * i + b + 1)
                        s.did(dve.tensor_tensor(y[b][:, :, :], ps_k[:, 0:TT * D].rearrange("p (t d) -> p t d", d=D), x[b][:, :, :], ALU.add))
                        s.wait()
                        dve.sem_inc(S["y_ready"], 1)
                        dve.sem_inc(S["seq_used"], 1)
                s.wait()

        clear_semaphores(nc, sems)


LAID = (["x"] + ["L0_tok_" + n for n in (
    "emb_byteT hash_rows Wq bq conv_w conv_b Win b_in Wg bg Wi bi WoT bo ln_g ln_b mlp_w mlp_bT Wout bout").split()]
        + ["L0_attn_" + n for n in "WqT bq WkT bk WvT bv WoT bo shift_logits alibi_slope".split()]
        + ["L0_ffn_" + n for n in "W1 b1 Wg bg Wd bd".split()]
        + ["L1_attn_" + n for n in "Wqkv_heads bqkv_heads W0_heads b0".split()]
        + ["L1_ffn_" + n for n in "Wq_pkT keysT Wq table Wo".split()])
def build(nc, a, out):
    outs = [nc.dram_tensor(f"h{n}", (NTOK, D), F32, kind="Internal").ap() for n in range(4)] + [out]
    tok = {k[7:]: v for k, v in a.items() if k.startswith("L0_tok_")}
    xpad = nc.dram_tensor("chars_padded", (B, WMAX + T), I32, kind="Internal").ap()
    pad_chars(nc, a["x"], xpad)
    tower_tok(nc, tok, a["x"], xpad, outs[0])
    shifted_attention(nc, {k[8:]: v for k, v in a.items() if k.startswith("L0_attn_")}, outs[0], outs[1])
    routed_ffn(nc, {k[7:]: v for k, v in a.items() if k.startswith("L0_ffn_")}, outs[1], outs[2])
    at1 = {k[8:]: v for k, v in a.items() if k.startswith("L1_attn_")}
    qkvT = nc.dram_tensor("qkvT", (PAIRS, P, ROWS3), F32, kind="Internal").ap()
    project_qkv(nc, at1, outs[2], qkvT)
    diagonal_attention(nc, at1, qkvT, outs[2], outs[3])
    ff1 = {k[7:]: v for k, v in a.items() if k.startswith("L1_ffn_")}
    qT = nc.dram_tensor("qT", (PAIRS, P, NTOK), F32, kind="Internal").ap()
    kv = nc.dram_tensor("kv", (NTOK, HEADS2 * KV), F32, kind="Internal").ap()
    product_keys(nc, ff1, outs[3], qT, kv)
    causal_attention(nc, ff1, qT, kv, outs[3], outs[4])


def kernel(**inputs):
    import numpy as np
    import concourse.bacc as bacc
    from concourse.bass_utils import run_bass_kernel_spmd

    laid = {k: np.asarray(v) for k, v in inputs.items()}
    t = {}
    t["L0_tok_emb_byteT"] = laid["L0_tok_emb_byte"].T
    t["L0_tok_WoT"] = laid["L0_tok_Wo"].T
    t["L0_tok_mlp_bT"] = laid["L0_tok_mlp_b"].T
    t["L0_tok_hash_rows"] = laid["L0_tok_hash_tables"].reshape(NW * HASH_MOD, E_TOK)
    for n in "qkvo":
        t[f"L0_attn_W{n}T"] = laid[f"L0_attn_W{n}"].T
    t["L1_attn_Wqkv_heads"] = laid["L1_attn_Wqkv"].reshape(D, 3, D, HEADS1).transpose(0, 1, 3, 2).reshape(D, -1)
    t["L1_attn_bqkv_heads"] = laid["L1_attn_bqkv"].reshape(3, D, HEADS1).transpose(0, 2, 1).reshape(-1)
    t["L1_attn_W0_heads"] = laid["L1_attn_W0"].reshape(D, HEADS1, D).transpose(1, 0, 2)
    t["L1_ffn_Wq_pkT"] = laid["L1_ffn_Wq_pk"].reshape(D, GROUPS, DKEY).transpose(2, 1, 0)
    t["L1_ffn_keysT"] = laid["L1_ffn_pk_keys"].transpose(3, 0, 2, 1).reshape(DKEY, GROUPS, NKEYS)
    t["L1_ffn_table"] = np.concatenate([laid["L1_ffn_keys_table"], laid["L1_ffn_values_table"]], axis=1)
    laid.update(t)
    nc = bacc.Bacc("TRN2", target_bir_lowering=False, num_devices=1)
    arrays, aps = {}, {}
    for name in LAID:
        v = np.ascontiguousarray(laid[name])
        arrays["in_" + name] = v
        aps[name] = nc.dram_tensor("in_" + name, v.shape, mybir.dt.from_np(v.dtype), kind="ExternalInput").ap()
    out = nc.dram_tensor("out_0", (NTOK, D), F32, kind="ExternalOutput").ap()
    build(nc, aps, out)
    r = run_bass_kernel_spmd(nc, [arrays], core_ids=[0]).results[0]
    return r["out_0"].reshape(B, T, D)
```

```python
from contextlib import ExitStack

import concourse.bass as bass
from concourse import mybir

F32 = mybir.dt.float32
BF16 = mybir.dt.bfloat16
I32 = mybir.dt.int32
U32 = mybir.dt.uint32
ALU = mybir.AluOpType
ACT = mybir.ActivationFunctionType
AX = mybir.AxisListType

P = 128
D = 64
B, T = 8, 512
NTOK = B * T
TT = T // P
EPS = 1e-5


class Steps:

    def __init__(self, eng, sem):
        self.eng, self.sem, self.n = eng, sem, 0

    def did(self, ins):
        ins.then_inc(self.sem, 1)
        self.n += 1
        return self.n

    def wait(self, n=None):
        self.eng.wait_ge(self.sem, self.n if n is None else n)

    def restart(self):
        self.wait()
        self.eng.sem_clear(self.sem)
        self.n = 0


def held(eng, sem, value, passed):
    eng.wait_ge(sem, value)
    eng.sem_inc(passed, 1)


def bc(ap, axis, n):
    a = ap.unsqueeze(axis)
    shape = list(a.shape)
    shape[axis] = n
    return a.broadcast_to(shape)


def ln_moments(dve, s, x, stats, moments):
    for t in range(TT):
        s.did(dve.bn_stats(stats[:, t, :], x[:, t, :]))
    s.wait()
    for t in range(TT):
        s.did(dve.bn_aggr(moments[:, t, :], stats[:, t, :]))
    s.wait()


def ln_apply(dve, s, xn, x, moments, std):
    s.did(dve.reciprocal(std[:, :], std[:, :]))
    s.wait()
    for t in range(TT):
        ins = dve.tensor_scalar(xn[:, t, :], x[:, t, :], moments[:, t, 0:1], std[:, t:t + 1], ALU.subtract, ALU.mult)
        if t < TT - 1:
            s.did(ins)
    return ins


def clear_semaphores(nc, sems):
    with nc.Block() as block:
        @block.sync
        def _(sp):
            for one in sems:
                sp.sem_clear(one)
E_TOK, H_TOK, S_TOK, KC, NM, NR = 64, 128, 32, 4, 4, 3
VOCAB, BASE, HASH_MOD = 64, 257, 1024
WINDOWS, MATCH_OFFSETS = (2, 4, 8, 16), (1, 2, 4, 8)
NW, WMAX, CHUNK = len(WINDOWS), 16, 32
NCH = T // CHUNK


def pad_chars(nc, x, xpad):
    with ExitStack() as ctx:
        fill = ctx.enter_context(nc.sbuf_tensor("pad_fill", [B, WMAX], I32))
        filled = ctx.enter_context(nc.semaphore("pad_filled"))
        written = ctx.enter_context(nc.semaphore("pad_written"))
        copied = ctx.enter_context(nc.semaphore("pad_copied"))
        with nc.Block() as block:
            @block.vector
            def _(dve):
                dve.memset(fill[:, :], -1).then_inc(filled, 1)

            @block.sync
            def _(sp):
                sp.dma_start(xpad[:, WMAX:WMAX + T], x).then_inc(copied, 16)
                sp.wait_ge(filled, 1)
                sp.dma_start(xpad[:, 0:WMAX], fill[:, :]).then_inc(written, 16)
                sp.wait_ge(copied, 16)
                sp.wait_ge(written, 16)

        clear_semaphores(nc, [filled, written, copied])


def tower_tok(nc, w, x, xpad, h_out):
    with ExitStack() as ctx:
        def sb(name, shape, dt=F32):
            return ctx.enter_context(nc.sbuf_tensor("tok_" + name, shape, dt))

        def ps(name, shape):
            return ctx.enter_context(nc.psum_tensor("tok_" + name, shape, F32))

        sems = []

        def sem(name):
            sems.append(ctx.enter_context(nc.semaphore("tok_" + name)))
            return sems[-1]

        embT = sb("embT", [E_TOK, VOCAB])
        wq = sb("wq", [E_TOK, E_TOK])
        bq = sb("bq", [1, E_TOK])
        conv_w = sb("conv_w", [E_TOK, KC])
        conv_b = sb("conv_b", [E_TOK, 1])
        win_byte = sb("win_byte", [E_TOK, H_TOK])
        win_hash = sb("win_hash", [E_TOK, H_TOK])
        win_match = sb("win_match", [NM, H_TOK])
        b_in = sb("b_in", [H_TOK, 1])
        wg = sb("wg", [H_TOK, S_TOK])
        bg = sb("bg", [S_TOK, 1])
        wi = sb("wi", [H_TOK, S_TOK])
        bi = sb("bi", [S_TOK, 1])
        woT = sb("woT", [H_TOK, S_TOK])
        bo = sb("bo", [H_TOK, 1])
        ln_g = sb("ln_g", [H_TOK, 1])
        ln_b = sb("ln_b", [H_TOK, 1])
        mlp_w = sb("mlp_w", [H_TOK, NR, H_TOK])
        mlp_b = sb("mlp_b", [H_TOK, NR])
        wout = sb("wout", [H_TOK, D])
        bout = sb("bout", [1, D])
        q_table = sb("q_table", [VOCAB, E_TOK])
        in_table = sb("in_table", [VOCAB, H_TOK])
        wo_centred = sb("wo_centred", [S_TOK, H_TOK])
        bo_centred = sb("bo_centred", [H_TOK, 1])
        ident = sb("ident", [P, P])
        centre = sb("centre", [P, P])
        mean_all = sb("mean_all", [P, P])
        ones_row = sb("ones_row", [1, P])
        eps = sb("eps", [P, 1])
        vocab_id_i = sb("vocab_id_i", [VOCAB, 1], I32)
        vocab_id = sb("vocab_id", [VOCAB, 1])
        in_chunk = sb("in_chunk", [S_TOK, T])
        chunk_start = sb("chunk_start", [S_TOK, T])
        powers = sb("powers", [P, WMAX])
        table_base = sb("table_base", [P, NW], I32)
        windows = sb("windows", [P, B * TT, WMAX], I32)
        windows_f = sb("windows_f", [P, B * TT, WMAX])
        hash_sum = sb("hash_sum", [P, B * TT, NW])
        hash_idx = sb("hash_idx", [P, (B + 2) * TT, NW], I32)
        loaded, gp_made, dve_made, pe_made = sem("loaded"), sem("gp_made"), sem("dve_made"), sem("pe_made")
        windows_loaded = sem("windows_loaded")
        psw = ps("psw", [P, 512])
        WEIGHTS = [(embT, w["emb_byteT"]), (wq, w["Wq"]), (bq, w["bq"].unsqueeze(0)),
                   (conv_w, w["conv_w"].rearrange("c a k -> c (a k)")), (conv_b, w["conv_b"].unsqueeze(1)),
                   (win_byte, w["Win"][0:E_TOK, :]), (win_hash, w["Win"][E_TOK:2 * E_TOK, :]),
                   (win_match, w["Win"][2 * E_TOK:2 * E_TOK + NM, :]), (b_in, w["b_in"].unsqueeze(1)),
                   (wg, w["Wg"]), (bg, w["bg"].unsqueeze(1)), (wi, w["Wi"]), (bi, w["bi"].unsqueeze(1)),
                   (woT, w["WoT"]), (bo, w["bo"].unsqueeze(1)), (ln_g, w["ln_g"].unsqueeze(1)),
                   (ln_b, w["ln_b"].unsqueeze(1)), (wout, w["Wout"]), (bout, w["bout"].unsqueeze(0)),
                   (mlp_b, w["mlp_bT"])]

        with nc.Block() as block:
            @block.sync
            def _(sp):
                for b in range(B):
                    src = bass.AP(xpad.tensor, xpad.offset + b * (WMAX + T) + 1, [[1, P], [P, TT], [1, WMAX]])
                    sp.dma_start(windows[:, b * TT:(b + 1) * TT, :], src).then_inc(windows_loaded, 16)
                for dst, src in WEIGHTS:
                    sp.dma_start(dst[:, :], src).then_inc(loaded, 16)
                sp.dma_start(mlp_w[:, :, :], w["mlp_w"].rearrange("l i o -> i l o")).then_inc(loaded, 16)

            @block.gpsimd
            def _(pool):
                pool.iota(vocab_id_i[:, :], [[0, 1]], base=0, channel_multiplier=1).then_inc(gp_made, 1)
                pool.iota(table_base[:, :], [[HASH_MOD, NW]], base=0, channel_multiplier=0).then_inc(gp_made, 1)
                pool.memset(ident[:, :], 0.0).then_inc(gp_made, 1)
                pool.wait_ge(gp_made, 3)
                pool.affine_select(out=ident[:, :], in_=ident[:, :], compare_op=ALU.not_equal, fill=1.0, base=0,
                                   pattern=[[-1, P]], channel_multiplier=1).then_inc(gp_made, 1)

            @block.vector
            def _(dve):
                s = Steps(dve, dve_made)
                s.did(dve.memset(mean_all[:, :], 1.0 / H_TOK))
                s.did(dve.memset(ones_row[:, :], 1.0))
                s.did(dve.memset(eps[:, :], EPS))
                s.did(dve.memset(in_chunk[:, :], 1.0))
                s.did(dve.memset(chunk_start[:, :], 0.0))
                power = 1
                for j in range(WMAX):
                    s.did(dve.memset(powers[:, WMAX - 1 - j:WMAX - j], float(power)))
                    power = power * BASE % HASH_MOD
                s.wait()
                s.did(dve.memset(in_chunk[:, 0:T:CHUNK], 0.0))
                s.did(dve.memset(chunk_start[:, 0:T:CHUNK], 1.0))
                dve.wait_ge(gp_made, 4)
                s.did(dve.tensor_copy(vocab_id[:, :], vocab_id_i[:, :]))
                s.did(dve.tensor_tensor(centre[:, :], ident[:, :], mean_all[:, :], ALU.subtract))
                dve.wait_ge(windows_loaded, 16 * B)
                s.did(dve.tensor_scalar(windows_f[:, :, :], windows[:, :, :], 0.0, None, ALU.max))
                s.wait()
                s.did(dve.tensor_tensor(windows_f[:, :, :], windows_f[:, :, :], bc(powers[:, :], 1, B * TT), ALU.mult))
                s.wait()
                for n, width in enumerate(WINDOWS):
                    s.did(dve.tensor_reduce(hash_sum[:, :, n], windows_f[:, :, WMAX - width:WMAX], AX.X, ALU.add))
                s.wait()
                hashes = hash_idx[:, 0:B * TT, :]
                s.did(dve.memset(hash_idx[:, B * TT:, :], 0))
                s.did(dve.tensor_copy(hashes, hash_sum[:, :, :]))
                s.wait()
                s.did(dve.tensor_scalar(hashes, hashes, HASH_MOD - 1, None, ALU.bitwise_and))
                s.wait()
                s.did(dve.tensor_tensor(hashes, hashes, bc(table_base[:, :], 1, B * TT), ALU.add))
                dve.wait_ge(pe_made, 1)
                s.did(dve.tensor_copy(q_table[:, :], psw[0:VOCAB, 0:E_TOK]))
                s.did(dve.tensor_copy(in_table[:, :], psw[0:VOCAB, 64:192]))
                s.did(dve.tensor_copy(wo_centred[:, :], psw[0:S_TOK, 192:320]))
                s.did(dve.tensor_copy(bo_centred[:, :], psw[:, 320:321]))
                s.wait()

            @block.tensor
            def _(pe):
                pe.wait_ge(loaded, 16 * (len(WEIGHTS) + 1))
                pe.wait_ge(dve_made, 5 + WMAX + 4)
                pe.matmul(psw[0:VOCAB, 0:E_TOK], embT[:, :], wq[:, :], start=True, stop=False)
                pe.matmul(psw[0:VOCAB, 0:E_TOK], ones_row[:, 0:VOCAB], bq[:, :], start=False, stop=True)
                pe.matmul(psw[0:VOCAB, 64:192], embT[:, :], win_byte[:, :], start=True, stop=True)
                pe.matmul(psw[0:S_TOK, 192:320], woT[:, :], centre[:, :], start=True, stop=True)
                pe.matmul(psw[:, 320:321], centre[:, :], bo[:, :], start=True, stop=True).then_inc(pe_made, 1)

        R = range(2)
        chars = sb("chars", [VOCAB, 2, T], I32)
        shifted = sb("shifted", [NM, 2, T], I32)
        own = sb("own", [NM, 2, T], I32)
        idx_now = sb("idx_now", [P, 2, TT * NW], I32)
        rows = [sb(f"rows{b}", [P, TT, NW, E_TOK]) for b in R]
        onehot = [sb(f"onehot{b}", [VOCAB, T]) for b in R]
        match = [sb(f"match{b}", [NM, T]) for b in R]
        prod = [sb(f"prod{b}", [P, TT, NW, E_TOK]) for b in R]
        score = [sb(f"score{b}", [P, TT, NW]) for b in R]
        score_e = [sb(f"score_e{b}", [P, TT, NW]) for b in R]
        smax = [sb(f"smax{b}", [P, TT]) for b in R]
        ssum = [sb(f"ssum{b}", [P, TT]) for b in R]
        feat = [sb(f"feat{b}", [P, TT, E_TOK]) for b in R]
        featT = [sb(f"featT{b}", [E_TOK, KC - 1 + T]) for b in R]
        conv = [[sb(f"conv{b}_{k}", [E_TOK, T]) for k in R] for b in R]
        hash_act = [sb(f"hash_act{b}", [E_TOK, T]) for b in R]
        h1 = [sb(f"h1_{b}", [H_TOK, T]) for b in R]
        gate = [sb(f"gate{b}", [S_TOK, T]) for b in R]
        one_minus = [sb(f"one_minus{b}", [S_TOK, T]) for b in R]
        drive = [sb(f"drive{b}", [S_TOK, T]) for b in R]
        gate_in = [sb(f"gate_in{b}", [S_TOK, T]) for b in R]
        gate_start = [sb(f"gate_start{b}", [S_TOK, T]) for b in R]
        cum_a = [sb(f"cum_a{b}", [S_TOK, T]) for b in R]
        cum_wb = [sb(f"cum_wb{b}", [S_TOK, T]) for b in R]
        carry = [sb(f"carry{b}", [S_TOK, 1 + NCH]) for b in R]
        states = [sb(f"states{b}", [S_TOK, T]) for b in R]
        cen = [sb(f"cen{b}", [H_TOK, T]) for b in R]
        sq = [sb(f"sq{b}", [H_TOK, T]) for b in R]
        hid = [sb(f"hid{b}", [H_TOK, T]) for b in R]
        hid_act = [sb(f"hid_act{b}", [H_TOK, T]) for b in R]
        h_tok = [sb(f"h_tok{b}", [P, TT, D]) for b in R]
        ps_q = [ps(f"ps_q{b}", [P, TT, E_TOK]) for b in R]
        ps_h = [ps(f"ps_h{b}", [P, 512]) for b in R]
        ps_s = [ps(f"ps_s{b}", [P, 512]) for b in R]

        chars_in = [sem(f"chars_in{b}") for b in R]
        rows_in = [nc.alloc_semaphore(f"tok_rows_in{b}") for b in R]
        stored = [sem(f"stored{b}") for b in R]
        names = ("idx_ready chars_used rows_used q_ready scores_centred exps_ready feat_ready featT_ready conv_ready "
                 "hash_ready onehot_ready in_ready h1_ready gates_ready gates_act drive_pre drive_ready states_ready "
                 "centred_ready squares_ready var_ready std_ready hid_ready mlp_lin mlp_ready mlp_act out_ready h_ready")
        S = {n: sem(n) for n in names.split()}
        dve_steps, pool_passed, dve_passed, pe_passed = sem("dve_steps"), sem("pool_passed"), sem("dve_passed"), sem("pe_passed")

        with nc.Block() as block:
            @block.sync
            def _(sp):
                sp.sem_inc(S["chars_used"], 2)
                for b in R:
                    sp.sem_inc(stored[b], 16)

                def load(i):
                    for b in R:
                        sp.wait_ge(S["chars_used"], 2 * i + b + 1)
                        row = 2 * i + b
                        seq = x[bass.ds(row, 1), :]
                        sp.dma_start(chars[:, b, :], seq.partition_broadcast(VOCAB).rearrange("p a t -> p (a t)")).then_inc(chars_in[b], 16)
                        sp.dma_start(own[:, b, :], seq.partition_broadcast(NM).rearrange("p a t -> p (a t)")).then_inc(chars_in[b], 16)
                        for n, k in enumerate(MATCH_OFFSETS):
                            sp.dma_start(shifted[n:n + 1, b, :], xpad[bass.ds(row, 1), WMAX - k:WMAX - k + T]).then_inc(chars_in[b], 16)

                def store(i):
                    for b in R:
                        sp.wait_ge(S["h_ready"], 2 * i + b + 1)
                        dst = h_out[bass.ds((2 * i + b) * T, T), :].rearrange("(t p) d -> p t d", p=P)
                        sp.dma_start(dst, h_tok[b][:, :, :]).then_inc(stored[b], 16)

                load(0)
                with sp.Fori(0, B // 2 - 1) as i:
                    load(i + 1)
                    store(i)
                store(B // 2 - 1)
                for b in R:
                    sp.wait_ge(stored[b], 16 * (B // 2 + 1))

            @block.gpsimd
            def _(pool):
                pool.sem_inc(S["rows_used"], 2)
                with pool.Fori(0, B // 2) as i:
                    for b in R:
                        pool.wait_ge(S["rows_used"], 2 * i + b + 1)
                        held(pool, S["idx_ready"], 2 * i + b + 1, pool_passed)
                        for t in range(TT):
                            for n in range(NW):
                                pool.indirect_dma_start(
                                    rows[b][:, t, n, :], None, w["hash_rows"],
                                    bass.IndirectOffsetOnAxis(idx_now[:, b, t * NW + n:t * NW + n + 1], 0),
                                ).then_inc(rows_in[b], 16)

            @block.vector
            def _(dve):
                s = Steps(dve, dve_steps)
                for b in R:
                    s.did(dve.memset(featT[b][:, 0:KC - 1], 0.0))
                    s.did(dve.memset(carry[b][:, 0:1], 0.0))
                s.wait()

                def indices(i, b):
                    dve.tensor_copy(idx_now[:, b, :], hash_idx[:, bass.ds((2 * i + b) * TT, TT), :].rearrange("p t n -> p (t n)")).then_inc(S["idx_ready"], 1)

                for b in R:
                    indices(0, b)
                with dve.Fori(0, B // 2) as i:
                    n = [2 * i + 1, 2 * i + 2]
                    s.restart()
                    mark = [0, 0]
                    for b in R:
                        dve.wait_ge(chars_in[b], 16 * 6 * (i + 1))
                        dve.tensor_scalar(onehot[b][:, :], chars[:, b, :], vocab_id[:, 0:1], None, ALU.is_equal).then_inc(S["onehot_ready"], 1)
                        s.did(dve.tensor_tensor(match[b][:, :], shifted[:, b, :], own[:, b, :], ALU.is_equal))
                        s.wait()
                        dve.sem_inc(S["chars_used"], 1)
                    for b in R:
                        dve.wait_ge(S["q_ready"], n[b])
                        dve.wait_ge(rows_in[b], 16 * TT * NW * (i + 1))
                        s.did(dve.tensor_tensor(prod[b][:, :, :, :], rows[b][:, :, :, :], bc(ps_q[b][:, :, :], 2, NW), ALU.mult))
                        s.wait()
                        s.did(dve.tensor_reduce(score[b][:, :, :], prod[b][:, :, :, :], AX.X, ALU.add))
                        s.wait()
                        s.did(dve.tensor_reduce(smax[b][:, :], score[b][:, :, :], AX.X, ALU.max))
                        s.wait()
                        dve.tensor_tensor(score[b][:, :, :], score[b][:, :, :], bc(smax[b][:, :], 2, NW), ALU.subtract).then_inc(S["scores_centred"], 1)
                    for b in R:
                        dve.wait_ge(S["exps_ready"], n[b])
                        s.did(dve.tensor_reduce(ssum[b][:, :], score_e[b][:, :, :], AX.X, ALU.add))
                        s.wait()
                        s.did(dve.reciprocal(ssum[b][:, :], ssum[b][:, :]))
                        s.wait()
                        s.did(dve.tensor_tensor(score_e[b][:, :, :], score_e[b][:, :, :], bc(ssum[b][:, :], 2, NW), ALU.mult))
                        s.wait()
                        s.did(dve.tensor_tensor(prod[b][:, :, :, :], rows[b][:, :, :, :], bc(score_e[b][:, :, :], 3, E_TOK), ALU.mult))
                        s.wait()
                        indices(i + 1, b)
                        dve.sem_inc(S["rows_used"], 1)
                        dve.tensor_reduce(feat[b][:, :, :], prod[b][:, :, :, :].rearrange("p t s e -> p t e s"), AX.X, ALU.add).then_inc(S["feat_ready"], 1)
                    for b in R:
                        dve.wait_ge(S["featT_ready"], n[b])
                        s.did(dve.tensor_copy(featT[b][:, KC - 1:], ps_s[b][0:E_TOK, :]))
                        s.wait()
                        s.did(dve.tensor_scalar(conv[b][0][:, :], featT[b][:, 0:T], conv_w[:, 0:1], None, ALU.mult))
                        for k in range(1, KC):
                            s.wait()
                            ins = dve.scalar_tensor_tensor(conv[b][k % 2][:, :], featT[b][:, k:k + T], conv_w[:, k:k + 1], conv[b][(k + 1) % 2][:, :], ALU.mult, ALU.add)
                            if k < KC - 1:
                                s.did(ins)
                        ins.then_inc(S["conv_ready"], 1)
                    for b in R:
                        dve.wait_ge(S["gates_act"], n[b])
                        s.did(dve.tensor_scalar(one_minus[b][:, :], gate[b][:, :], -1.0, 1.0, ALU.mult, ALU.add))
                        s.did(dve.tensor_scalar(gate[b][:, :], gate[b][:, :], 1e-6, None, ALU.max))
                        s.wait()
                        s.did(dve.tensor_tensor(drive[b][:, :], drive[b][:, :], one_minus[b][:, :], ALU.mult))
                        s.did(dve.tensor_tensor(gate_in[b][:, :], gate[b][:, :], in_chunk[:, :], ALU.mult))
                        s.did(dve.tensor_tensor(gate_start[b][:, :], gate[b][:, :], chunk_start[:, :], ALU.mult))
                        s.wait()
                        s.did(dve.tensor_tensor_scan(cum_a[b][:, :], gate_in[b][:, :], gate_start[b][:, :], 0.0, ALU.mult, ALU.add))
                        s.wait()
                        s.did(dve.tensor_scalar(gate_in[b][:, :], cum_a[b][:, :], 1e-8, None, ALU.max))
                        s.wait()
                        s.did(dve.reciprocal(gate_in[b][:, :], gate_in[b][:, :]))
                        s.wait()
                        s.did(dve.tensor_tensor(drive[b][:, :], drive[b][:, :], gate_in[b][:, :], ALU.mult))
                        s.wait()
                        s.did(dve.tensor_tensor_scan(cum_wb[b][:, :], in_chunk[:, :], drive[b][:, :], 0.0, ALU.mult, ALU.add))
                        s.wait()
                        s.did(dve.tensor_tensor_scan(carry[b][:, 1:], cum_wb[b][:, CHUNK - 1:T:CHUNK], cum_a[b][:, CHUNK - 1:T:CHUNK], 0.0, ALU.add, ALU.mult))
                        s.wait()
                        s.did(dve.tensor_tensor(cum_wb[b][:, :].rearrange("p (c k) -> p c k", k=CHUNK), cum_wb[b][:, :].rearrange("p (c k) -> p c k", k=CHUNK), bc(carry[b][:, 0:NCH], 2, CHUNK), ALU.add))
                        s.wait()
                        dve.tensor_tensor(states[b][:, :], cum_wb[b][:, :], cum_a[b][:, :], ALU.mult).then_inc(S["states_ready"], 1)
                    for b in R:
                        dve.wait_ge(S["std_ready"], n[b])
                        s.did(dve.reciprocal(sq[b][:, :], sq[b][:, :]))
                        s.wait()
                        s.did(dve.tensor_tensor(cen[b][:, :], cen[b][:, :], sq[b][:, :], ALU.mult))
                        s.wait()
                        dve.tensor_scalar(hid[b][:, :], cen[b][:, :], ln_g[:, 0:1], ln_b[:, 0:1], ALU.mult, ALU.add).then_inc(S["hid_ready"], 1)
                    for l in range(NR):
                        for b in R:
                            dve.wait_ge(S["mlp_act"], 2 * NR * i + 2 * l + b + 1)
                            dve.tensor_tensor(hid[b][:, :], hid[b][:, :], hid_act[b][:, :], ALU.add).then_inc(S["mlp_ready"], 1)
                    for b in R:
                        dve.wait_ge(stored[b], 16 * i + 16)
                        dve.wait_ge(S["out_ready"], n[b])
                        s.did(dve.tensor_copy(h_tok[b][:, :, :], ps_q[b][:, :, :]))
                        s.wait()
                        dve.sem_inc(S["h_ready"], 1)
                s.wait()

            @block.scalar
            def _(act):
                with act.Fori(0, B // 2) as i:
                    n = [2 * i + 1, 2 * i + 2]
                    for b in R:
                        act.wait_ge(S["scores_centred"], n[b])
                        act.activation(score_e[b][:, :, :], score[b][:, :, :], ACT.Exp, scale=float(E_TOK) ** -0.5).then_inc(S["exps_ready"], 1)
                    for b in R:
                        act.wait_ge(S["conv_ready"], n[b])
                        act.activation(hash_act[b][:, :], conv[b][(KC - 1) % 2][:, :], ACT.Silu, bias=conv_b[:, 0:1]).then_inc(S["hash_ready"], 1)
                    for b in R:
                        act.wait_ge(S["in_ready"], n[b])
                        act.activation(h1[b][:, :], ps_h[b][:, :], ACT.Silu, bias=b_in[:, 0:1]).then_inc(S["h1_ready"], 1)
                    for b in R:
                        act.wait_ge(S["gates_ready"], n[b])
                        act.activation(drive[b][:, :], ps_h[b][0:S_TOK, :], ACT.Identity, bias=bi[:, 0:1])
                        act.activation(gate[b][:, :], ps_s[b][0:S_TOK, :], ACT.Sigmoid, bias=bg[:, 0:1]).then_inc(S["gates_act"], 1)
                    for b in R:
                        act.wait_ge(S["centred_ready"], n[b])
                        act.activation(cen[b][:, :], ps_h[b][:, :], ACT.Identity, bias=bo_centred[:, 0:1])
                        act.activation(sq[b][:, :], ps_h[b][:, :], ACT.Square, bias=bo_centred[:, 0:1]).then_inc(S["squares_ready"], 1)
                    for b in R:
                        act.wait_ge(S["var_ready"], n[b])
                        act.activation(sq[b][:, :], ps_s[b][:, :], ACT.Sqrt, bias=eps[:, 0:1]).then_inc(S["std_ready"], 1)
                    for l in range(NR):
                        for b in R:
                            act.wait_ge(S["mlp_lin"], 2 * NR * i + 2 * l + b + 1)
                            act.activation(hid_act[b][:, :], ps_h[b][:, :], ACT.Silu, bias=mlp_b[:, l:l + 1]).then_inc(S["mlp_act"], 1)

            @block.tensor
            def _(pe):
                with pe.Fori(0, B // 2) as i:
                    n = [2 * i + 1, 2 * i + 2]
                    for b in R:
                        pe.wait_ge(S["onehot_ready"], n[b])
                        for t in range(TT):
                            mm = pe.matmul(ps_q[b][:, t, :], onehot[b][:, t * P:(t + 1) * P], q_table[:, :], start=True, stop=True)
                        mm.then_inc(S["q_ready"], 1)
                    for b in R:
                        held(pe, S["feat_ready"], n[b], pe_passed)
                        for t in range(TT):
                            mm = pe.transpose(ps_s[b][0:E_TOK, t * P:(t + 1) * P], feat[b][:, t, :], ident[:, :])
                        mm.then_inc(S["featT_ready"], 1)
                    for b in R:
                        pe.wait_ge(S["hash_ready"], n[b])
                        pe.matmul(ps_h[b][:, :], in_table[:, :], onehot[b][:, :], start=True, stop=False)
                        pe.matmul(ps_h[b][:, :], win_match[:, :], match[b][:, :], start=False, stop=False)
                        pe.matmul(ps_h[b][:, :], win_hash[:, :], hash_act[b][:, :], start=False, stop=True).then_inc(S["in_ready"], 1)
                    for b in R:
                        pe.wait_ge(S["h1_ready"], n[b])
                        pe.matmul(ps_s[b][0:S_TOK, :], wg[:, :], h1[b][:, :], start=True, stop=True)
                        pe.matmul(ps_h[b][0:S_TOK, :], wi[:, :], h1[b][:, :], start=True, stop=True).then_inc(S["gates_ready"], 1)
                    for b in R:
                        pe.wait_ge(S["states_ready"], n[b])
                        pe.matmul(ps_h[b][:, :], centre[:, :], h1[b][:, :], start=True, stop=False)
                        pe.matmul(ps_h[b][:, :], wo_centred[:, :], states[b][:, :], start=False, stop=True).then_inc(S["centred_ready"], 1)
                    for b in R:
                        pe.wait_ge(S["squares_ready"], n[b])
                        pe.matmul(ps_s[b][:, :], mean_all[:, :], sq[b][:, :], start=True, stop=True).then_inc(S["var_ready"], 1)
                    for l in range(NR):
                        for b in R:
                            if l == 0:
                                pe.wait_ge(S["hid_ready"], n[b])
                            else:
                                pe.wait_ge(S["mlp_ready"], 2 * NR * i + 2 * (l - 1) + b + 1)
                            pe.matmul(ps_h[b][:, :], mlp_w[:, l, :], hid[b][:, :], start=True, stop=True).then_inc(S["mlp_lin"], 1)
                    for b in R:
                        pe.wait_ge(S["mlp_ready"], 2 * NR * i + 2 * (NR - 1) + b + 1)
                        for t in range(TT):
                            pe.matmul(ps_q[b][:, t, :], hid[b][:, t * P:(t + 1) * P], wout[:, :], start=True, stop=False)
                            mm = pe.matmul(ps_q[b][:, t, :], ones_row[:, :], bout[:, :], start=False, stop=True)
                        mm.then_inc(S["out_ready"], 1)

        clear_semaphores(nc, sems)


HEADS0, DH0 = 4, 16
SHIFTS = (0, 4, 8, 12)
NSH, PAD0, WINDOW = len(SHIFTS), max(SHIFTS), 64
FB = 2 * T - P
UNITS = TT * HEADS0
HIGH, MIDDLE, LOWER = range(3)
QPARTS = (HIGH, HIGH, HIGH, MIDDLE, MIDDLE, LOWER)
KPARTS = (HIGH, MIDDLE, LOWER, HIGH, MIDDLE, HIGH)
STACK = len(QPARTS) * DH0


def shifted_attention(nc, w, h_in, h_out):
    with ExitStack() as ctx:
        def sb(name, shape, dt=F32):
            return ctx.enter_context(nc.sbuf_tensor("at0_" + name, shape, dt))

        def ps(name, shape):
            return ctx.enter_context(nc.psum_tensor("at0_" + name, shape, F32))

        sems = []

        def sem(name):
            sems.append(ctx.enter_context(nc.semaphore("at0_" + name)))
            return sems[-1]

        wq = sb("wq", [D + 1, HEADS0, len(QPARTS), DH0])
        wk = sb("wk", [D + 1, HEADS0, len(QPARTS), DH0])
        less_high = [sb(f"less_high{m}", [STACK, 1]) for m in range(2)]
        less_middle = [sb(f"less_middle{m}", [STACK, 1]) for m in range(2)]
        wv = sb("wv", [D + 1, D])
        wo = sb("wo", [D + 1, D])
        logits = sb("logits", [P, HEADS0, NSH])
        lmax = sb("lmax", [P, HEADS0])
        log_pi = sb("log_pi", [P, HEADS0, NSH])
        slope = sb("slope", [P, HEADS0])
        tiny = sb("tiny", [P, 1])
        eps = sb("eps", [P, 1])
        ident = sb("ident", [P, P])
        dist_i = sb("dist_i", [P, FB], I32)
        dist = sb("dist", [P, FB])
        mask = sb("mask", [P, FB])
        alibi = [sb(f"alibi{k}", [P, FB]) for k in range(2)]
        bias = sb("bias", [P, HEADS0, NSH, FB])
        loaded, gp_made, dve_made, act_made = sem("loaded"), sem("gp_made"), sem("dve_made"), sem("act_made")

        x = sb("x", [P, TT, D])
        xn = sb("xn", [P, TT, D])
        stats = sb("stats", [P, TT, 6])
        moments = sb("moments", [P, TT, 2])
        std = sb("std", [P, TT])
        xnT = sb("xnT", [D + 1, T])
        qS = [[sb(f"qS{b}_{h}", [STACK, T], BF16) for h in range(HEADS0)] for b in range(2)]
        kS = [[sb(f"kS{b}_{h}", [STACK, PAD0 + T], BF16) for h in range(HEADS0)] for b in range(2)]
        high = [sb(f"high{k}", [STACK, T], BF16) for k in range(2)]
        middle = [sb(f"middle{k}", [STACK, T], BF16) for k in range(2)]
        rest = [sb(f"rest{k}", [STACK, T]) for k in range(2)]
        vT = sb("vT", [D, PAD0 + T])
        vsumT = [sb(f"vsumT{k}", [D, T]) for k in range(2)]
        vsum = [sb(f"vsum{b}", [P, TT, D]) for b in range(2)]
        att = [sb(f"att{k}", [P, NSH, T]) for k in range(2)]
        prob = [sb(f"prob{k}", [P, NSH, T]) for k in range(2)]
        psum_p = [sb(f"psum_p{k}", [P, NSH // 2, T]) for k in range(3)]
        probT = [sb(f"probT{k}", [P, TT, P]) for k in range(2)]
        rowmax = [sb(f"rowmax{k}", [P, NSH // 2]) for k in range(2)]
        negmax = [sb(f"negmax{k}", [P, 1]) for k in range(2)]
        total = [sb(f"total{k}", [P, 1]) for k in range(6)]
        inv = [sb(f"inv{k}", [P, 1]) for k in range(6)]
        context = sb("context", [P, TT, D])
        contextT = sb("contextT", [D + 1, T])
        y = [sb(f"y{b}", [P, TT, D]) for b in range(2)]
        ps_att = [ps(f"ps_att{s}", [P, 2, T]) for s in range(NSH // 2)]
        ps_T = ps("ps_T", [P, T])
        ps_pT = ps("ps_pT", [P, T])
        ps_c = ps("ps_c", [P, T])
        ps_v = ps("ps_v", [P, T])

        x_in, x_used, stored = sem("x_in"), sem("x_used"), sem("stored")
        names = ("moments_ready std_ready xn_ready T_ps T_used high_ready middle_ready parts_ready vsum_made "
                 "scores_ready scores_used max_ready probs_ready summed pT_ps pT_ready "
                 "ctx_ps context_part context_ready y_ps y_ready")
        S = {n: sem(n) for n in names.split()}
        dve_steps, act_steps, gp_steps = sem("dve_steps"), sem("act_steps"), sem("gp_steps")
        dve_passed, pe_passed = sem("dve_passed"), sem("pe_passed")

        LOADS = 16 * (4 * len(QPARTS) + 6)

        with nc.Block() as block:
            @block.sync
            def _(sp):
                for dst, name in ((wq, "q"), (wk, "k")):
                    for n in range(len(QPARTS)):
                        sp.dma_start(dst[0:D, :, n, :], w[f"W{name}T"].rearrange("i (h d) -> i h d", h=HEADS0)).then_inc(loaded, 16)
                        sp.dma_start(dst[D:D + 1, :, n, :], w[f"b{name}"].unsqueeze(0).rearrange("a (h d) -> a h d", h=HEADS0)).then_inc(loaded, 16)
                for dst, name in ((wv, "v"), (wo, "o")):
                    sp.dma_start(dst[0:D, :], w[f"W{name}T"]).then_inc(loaded, 16)
                    sp.dma_start(dst[D:D + 1, :], w[f"b{name}"].unsqueeze(0)).then_inc(loaded, 16)
                sp.dma_start(logits[:, :, :], w["shift_logits"].partition_broadcast(P)).then_inc(loaded, 16)
                sp.dma_start(slope[:, :], w["alibi_slope"].partition_broadcast(P)).then_inc(loaded, 16)
                sp.wait_ge(loaded, LOADS)

            @block.gpsimd
            def _(pool):
                pool.iota(dist_i[:, :], [[1, FB]], base=P - T, channel_multiplier=-1).then_inc(gp_made, 1)
                pool.memset(ident[:, :], 0.0).then_inc(gp_made, 1)
                pool.wait_ge(gp_made, 2)
                pool.affine_select(out=ident[:, :], in_=ident[:, :], compare_op=ALU.not_equal, fill=1.0, base=0,
                                   pattern=[[-1, P]], channel_multiplier=1).then_inc(gp_made, 1)
                count = 3
                for parts, high_sign, middle_sign in ((QPARTS, less_high[0], less_middle[0]), (KPARTS, less_high[1], less_middle[1])):
                    for tile, least in ((high_sign, MIDDLE), (middle_sign, LOWER)):
                        pool.memset(tile[:, :], 0.0).then_inc(gp_made, 1)
                        count += 1
                        for n, part in enumerate(parts):
                            if part >= least:
                                for first, sign in ((n * DH0, -1.0), ((n + 1) * DH0, 0.0)):
                                    pool.wait_ge(gp_made, count)
                                    if first < STACK:
                                        pool.affine_select(out=tile[:, :], in_=tile[:, :], compare_op=ALU.is_gt, fill=sign, base=first,
                                                           pattern=[[0, 1]], channel_multiplier=-1).then_inc(gp_made, 1)
                                        count += 1

            @block.scalar
            def _(act):
                act.wait_ge(dve_made, 1)
                act.activation(log_pi[:, :, :], logits[:, :, :], ACT.Exp).then_inc(act_made, 1)
                act.wait_ge(dve_made, 2)
                act.activation(log_pi[:, :, :], logits[:, :, :], ACT.Ln, bias=tiny[:, 0:1]).then_inc(act_made, 1)

            @block.vector
            def _(dve):
                s = Steps(dve, dve_steps)
                s.did(dve.memset(tiny[:, :], 1e-8))
                s.did(dve.memset(eps[:, :], EPS))
                for b in range(2):
                    for h in range(HEADS0):
                        s.did(dve.memset(kS[b][h][:, 0:PAD0], 0.0))
                s.did(dve.memset(vT[:, 0:PAD0], 0.0))
                s.did(dve.memset(xnT[D:D + 1, :], 1.0))
                s.did(dve.memset(contextT[D:D + 1, :], 1.0))
                dve.wait_ge(gp_made, 3)
                s.did(dve.tensor_copy(dist[:, :], dist_i[:, :]))
                s.wait()
                s.did(dve.tensor_scalar(mask[:, :], dist[:, :], float(WINDOW), 10000.0, ALU.is_lt, ALU.mult))
                s.wait()
                s.did(dve.scalar_tensor_tensor(mask[:, :], dist[:, :], 0.0, mask[:, :], ALU.is_ge, ALU.mult))
                s.wait()
                s.did(dve.tensor_scalar(mask[:, :], mask[:, :], -10000.0, None, ALU.add))
                s.did(dve.tensor_scalar(dist[:, :], dist[:, :], 0.0, None, ALU.max))
                dve.wait_ge(loaded, LOADS)
                s.did(dve.tensor_scalar(slope[:, :], slope[:, :], -1.0, None, ALU.mult))
                s.did(dve.tensor_scalar(wq[:, :, :, :], wq[:, :, :, :], float(DH0) ** -0.5, None, ALU.mult))
                s.wait()
                s.did(dve.tensor_reduce(lmax[:, :], logits[:, :, :], AX.X, ALU.max))
                s.wait()
                dve.tensor_tensor(logits[:, :, :], logits[:, :, :], bc(lmax[:, :], 2, NSH), ALU.subtract).then_inc(dve_made, 1)
                dve.wait_ge(act_made, 1)
                s.did(dve.tensor_reduce(lmax[:, :], log_pi[:, :, :], AX.X, ALU.add))
                s.wait()
                s.did(dve.reciprocal(lmax[:, :], lmax[:, :]))
                s.wait()
                dve.tensor_tensor(logits[:, :, :], log_pi[:, :, :], bc(lmax[:, :], 2, NSH), ALU.mult).then_inc(dve_made, 1)
                dve.wait_ge(act_made, 2)
                for h in range(HEADS0):
                    s.did(dve.scalar_tensor_tensor(alibi[h % 2][:, :], dist[:, :], slope[:, h:h + 1], mask[:, :], ALU.mult, ALU.add))
                    s.wait()
                    for j in range(NSH):
                        s.did(dve.tensor_scalar(bias[:, h, j, :], alibi[h % 2][:, :], log_pi[:, h, j:j + 1], None, ALU.add))
                s.wait()

        TRANSPOSE, VALUE, PART, SUM = 0, 1, 2, 2 + 2 * HEADS0
        ITEMS = SUM + 1

        def use(k, n):
            return n if isinstance(k, int) and k == 0 else k * (ITEMS + 1) + (n - 1)

        def context_use(i):
            if isinstance(i, int) and i == B - 1:
                return i * (ITEMS + 1) + ITEMS
            return i * (ITEMS + 1) + 2 * ITEMS

        FIRST = 3

        def sequences(eng, prepare, body):
            prepare(0, 0)
            with eng.Fori(0, B // 2 - 1) as q:
                body(2 * q, 0, True)
                body(2 * q + 1, 1, True)
            body(B - 2, 0, True)
            body(B - 1, 1, False)

        with nc.Block() as block:
            @block.sync
            def _(sp):
                sp.sem_inc(stored, 32)

                def load(k, b):
                    if not (isinstance(k, int) and k == 0):
                        sp.wait_ge(x_used, k)
                    sp.dma_start(x[:, :, :], h_in[bass.ds(k * T, T), :].rearrange("(t p) d -> p t d", p=P)).then_inc(x_in, 16)

                def body(i, b, more):
                    if more:
                        load(i + 1, 1 - b)
                    sp.wait_ge(S["y_ready"], i + 1)
                    sp.dma_start(h_out[bass.ds(i * T, T), :].rearrange("(t p) d -> p t d", p=P), y[b][:, :, :]).then_inc(stored, 16)

                sequences(sp, load, body)
                sp.wait_ge(stored, 16 * (B + 2))

            @block.vector
            def _(dve):
                dve.sem_clear(dve_steps)
                s = Steps(dve, dve_steps)

                def moment(k):
                    held(dve, x_in, 16 * k + 16, dve_passed)
                    ln_moments(dve, s, x, stats, moments)
                    dve.sem_inc(S["moments_ready"], 1)

                def normalised(k, b):
                    dve.wait_ge(S["std_ready"], k + 1)
                    s.did(ln_apply(dve, s, xn, x, moments, std))
                    dve.wait_ge(stored, 16 * k + 16)
                    s.wait()
                    dve.sem_inc(S["xn_ready"], 1)
                    s.did(dve.tensor_copy(y[b][:, :, :], x[:, :, :]))
                    s.wait()
                    dve.sem_inc(x_used, 1)

                def rests(k, m):
                    dve.wait_ge(S["high_ready"], 2 * HEADS0 * k + m + 1)
                    if m >= 2:
                        dve.wait_ge(S["parts_ready"], 2 * HEADS0 * k + m - 1)
                    dve.scalar_tensor_tensor(rest[m % 2][:, :], high[m % 2][:, :], less_high[m % 2][:, 0:1], ps_T[0:STACK, :],
                                             ALU.mult, ALU.add).then_inc(S["T_used"], 1)

                def stacks(k, b, m):
                    dst = kS[b][m // 2][:, PAD0:] if m % 2 else qS[b][m // 2][:, :]
                    dve.wait_ge(S["middle_ready"], 2 * HEADS0 * k + m + 1)
                    dve.scalar_tensor_tensor(dst, middle[m % 2][:, :], less_middle[m % 2][:, 0:1], rest[m % 2][:, :],
                                             ALU.mult, ALU.add).then_inc(S["parts_ready"], 1)

                def prepare(k, b):
                    moment(k)
                    normalised(k, b)
                    for m in range(2 * HEADS0 + 1):
                        if m < 2 * HEADS0:
                            rests(k, m)
                        if m >= 1:
                            stacks(k, b, m - 1)
                    s.restart()

                def body(i, b, more):
                    def maxima(u):
                        qt, h, k = u // HEADS0, u % HEADS0, u % 2
                        off = T - P - qt * P
                        if u >= 2:
                            dve.wait_ge(S["probs_ready"], UNITS * i + u - 1)
                        for g in range(2):
                            held(dve, S["scores_ready"], 2 * UNITS * i + 2 * u + g + 1, dve_passed)
                            dve.tensor_tensor_reduce(att[k][:, 2 * g:2 * g + 2, :], ps_att[g][:, :, :], bias[:, h, 2 * g:2 * g + 2, off:off + T], 1.0, -3.0e38,
                                                     ALU.add, ALU.max, rowmax[k][:, g:g + 1]).then_inc(S["scores_used"], 1)
                        dve.wait_ge(S["scores_used"], 2 * UNITS * i + 2 * u + 2)
                        dve.tensor_reduce(negmax[k][:, :], rowmax[k][:, :], AX.X, ALU.max, negate=True).then_inc(S["max_ready"], 1)

                    def inverse(u):
                        dve.wait_ge(S["probs_ready"], UNITS * i + u + 1)
                        s.did(dve.reciprocal(inv[u % 6][:, :], total[u % 6][:, :]))

                    def normalise(u):
                        qt, h = u // HEADS0, u % HEADS0
                        dve.wait_ge(S["ctx_ps"], UNITS * i + u + 1)
                        s.wait()
                        dve.tensor_scalar(context[:, qt, h * DH0:(h + 1) * DH0], [ps_c, ps_v][u % 2][:, u * DH0:(u + 1) * DH0], inv[u % 6][:, 0:1], None,
                                          ALU.mult).then_inc(S["context_part"], 1)

                    for step in range(UNITS + 5):
                        m = step - FIRST - PART
                        if step < UNITS:
                            maxima(step)
                        if more and 0 <= m < 2 * HEADS0:
                            rests(i + 1, m)
                        if step >= 5:
                            normalise(step - 5)
                        if 2 <= step <= UNITS + 1:
                            inverse(step - 2)
                        if more and 1 <= m <= 2 * HEADS0:
                            stacks(i + 1, 1 - b, m - 1)
                        if more and step == FIRST - 2:
                            moment(i + 1)
                        if more and step == FIRST - 1:
                            normalised(i + 1, 1 - b)
                    dve.wait_ge(S["context_part"], UNITS * i + UNITS)
                    dve.sem_inc(S["context_ready"], 1)
                    dve.wait_ge(S["T_ps"], context_use(i) + 1)
                    dve.tensor_copy(contextT[0:D, :], ps_T[0:D, :]).then_inc(S["T_used"], 1)
                    dve.wait_ge(S["y_ps"], i + 1)
                    s.did(dve.tensor_tensor(y[b][:, :, :], ps_v[:, 0:TT * D].rearrange("p (t d) -> p t d", d=D), y[b][:, :, :], ALU.add))
                    s.wait()
                    dve.sem_inc(S["y_ready"], 1)
                    s.restart()

                sequences(dve, prepare, body)

            @block.scalar
            def _(act):
                def root(k):
                    act.wait_ge(S["moments_ready"], k + 1)
                    act.activation(std[:, :], moments[:, :, 1], ACT.Sqrt, bias=eps[:, 0:1]).then_inc(S["std_ready"], 1)

                def item(k, b, n):
                    act.wait_ge(S["T_ps"], use(k, n) + 1)
                    if n == TRANSPOSE:
                        act.activation(xnT[0:D, :], ps_T[0:D, :], ACT.Copy).then_inc(S["T_used"], 1)
                    elif n == VALUE:
                        act.activation(vT[:, PAD0:], ps_T[0:D, :], ACT.Copy).then_inc(S["T_used"], 1)
                    elif n < SUM:
                        act.activation(high[n % 2][:, :], ps_T[0:STACK, :], ACT.Copy).then_inc(S["high_ready"], 1)
                    else:
                        act.activation(vsum[b][:, :, :], ps_T[:, 0:TT * D].rearrange("p (t d) -> p t d", d=D), ACT.Copy).then_inc(S["T_used"], 1)

                def middles(k, m):
                    act.wait_ge(S["T_used"], use(k, PART + m) + 2)
                    if m >= 2:
                        act.wait_ge(S["parts_ready"], 2 * HEADS0 * k + m - 1)
                    act.activation(middle[m % 2][:, :], rest[m % 2][:, :], ACT.Copy).then_inc(S["middle_ready"], 1)

                def step_of(k, b, n):
                    if n < ITEMS:
                        item(k, b, n)
                    if PART < n <= SUM:
                        middles(k, n - PART - 1)

                def prepare(k, b):
                    root(k)
                    for n in range(ITEMS):
                        if n < SUM:
                            item(k, b, n)
                        if PART < n <= SUM:
                            middles(k, n - PART - 1)
                        if n == SUM:
                            item(k, b, n)

                def body(i, b, more):
                    def exponentials(u):
                        act.wait_ge(S["max_ready"], UNITS * i + u + 1)
                        if u >= 2:
                            act.wait_ge(S["summed"], UNITS * i + u - 1)
                        act.activation(prob[u % 2][:, :, :], att[u % 2][:, :, :], ACT.Exp, bias=negmax[u % 2][:, 0:1],
                                       accum_out=total[u % 6][:, 0:1]).then_inc(S["probs_ready"], 1)

                    def transposed(u):
                        act.wait_ge(S["pT_ps"], UNITS * i + u + 1)
                        if u >= 2:
                            act.wait_ge(S["ctx_ps"], UNITS * i + u - 1)
                        act.activation(probT[u % 2][:, :, :], ps_pT[:, :].rearrange("p (t q) -> p t q", t=TT), ACT.Copy).then_inc(S["pT_ready"], 1)

                    for step in range(UNITS + 3):
                        if more and step == FIRST - 1:
                            root(i + 1)
                        if more and 0 <= step - FIRST < ITEMS:
                            step_of(i + 1, 1 - b, step - FIRST)
                        if step >= 3:
                            transposed(step - 3)
                        if step < UNITS:
                            exponentials(step)

                sequences(act, prepare, body)

            @block.gpsimd
            def _(pool):
                pool.sem_clear(gp_steps)
                s = Steps(pool, gp_steps)

                def summed_values(k, part):
                    if part == 0:
                        pool.wait_ge(S["T_used"], use(k, VALUE) + 2)
                        s.did(pool.tensor_tensor(vsumT[0][:, :], vT[:, PAD0:PAD0 + T], vT[:, PAD0 - SHIFTS[1]:PAD0 - SHIFTS[1] + T], ALU.add))
                    elif part == 1:
                        s.did(pool.tensor_tensor(vsumT[1][:, :], vT[:, PAD0 - SHIFTS[2]:PAD0 - SHIFTS[2] + T], vT[:, PAD0 - SHIFTS[3]:PAD0 - SHIFTS[3] + T], ALU.add))
                    else:
                        s.wait()
                        pool.tensor_tensor(vsumT[0][:, :], vsumT[0][:, :], vsumT[1][:, :], ALU.add).then_inc(S["vsum_made"], 1)
                        s.restart()

                def prepare(k, b):
                    for part in range(3):
                        summed_values(k, part)

                def body(i, b, more):
                    for u in range(UNITS):
                        pool.wait_ge(S["probs_ready"], UNITS * i + u + 1)
                        if u >= 3:
                            pool.wait_ge(S["pT_ps"], UNITS * i + u - 2)
                        pool.tensor_tensor(psum_p[u % 3][:, :, :], prob[u % 2][:, 0:2, :], prob[u % 2][:, 2:4, :], ALU.add).then_inc(S["summed"], 1)
                        if more and 0 <= u - FIRST - 2 < 3:
                            summed_values(i + 1, u - FIRST - 2)

                sequences(pool, prepare, body)

            @block.tensor
            def _(pe):
                pe.sem_inc(S["T_used"], 1)

                def item(k, n):
                    if n == TRANSPOSE:
                        held(pe, S["xn_ready"], k + 1, pe_passed)
                    if n == SUM:
                        held(pe, S["vsum_made"], k + 1, pe_passed)
                    held(pe, S["T_used"], use(k, n) + 1, pe_passed)
                    if n == TRANSPOSE:
                        for t in range(TT):
                            mm = pe.transpose(ps_T[0:D, t * P:(t + 1) * P], xn[:, t, :], ident[:, :])
                    elif n == VALUE:
                        mm = pe.matmul(ps_T[0:D, :], wv[:, :], xnT[:, :], start=True, stop=True)
                    elif n < SUM:
                        m = n - PART
                        mm = pe.matmul(ps_T[0:STACK, :], [wq, wk][m % 2][:, m // 2, :, :].rearrange("i n d -> i (n d)"), xnT[:, :],
                                       start=True, stop=True)
                    else:
                        for t in range(TT):
                            mm = pe.transpose(ps_T[:, t * D:(t + 1) * D], vsumT[0][:, t * P:(t + 1) * P], ident[0:D, 0:D])
                    mm.then_inc(S["T_ps"], 1)

                def prepare(k, b):
                    for n in range(ITEMS):
                        item(k, n)

                def body(i, b, more):
                    def scores(u):
                        qt, h = u // HEADS0, u % HEADS0
                        for j, shift in enumerate(SHIFTS):
                            if u >= 1 and j % 2 == 0:
                                held(pe, S["scores_used"], 2 * UNITS * i + 2 * (u - 1) + j // 2 + 1, pe_passed)
                            mm = pe.matmul(ps_att[j // 2][:, j % 2, :], qS[b][h][:, qt * P:(qt + 1) * P], kS[b][h][:, PAD0 - shift:PAD0 - shift + T],
                                           start=True, stop=True)
                            if j % 2 == 1:
                                mm.then_inc(S["scores_ready"], 1)

                    def transposes(u):
                        pe.wait_ge(S["summed"], UNITS * i + u + 1)
                        if u >= 1:
                            pe.wait_ge(S["pT_ready"], UNITS * i + u)
                        for t in range(TT):
                            for j in range(NSH // 2):
                                mm = pe.matmul(ps_pT[:, t * P:(t + 1) * P], psum_p[u % 3][:, j, t * P:(t + 1) * P], ident[:, :],
                                               start=(j == 0), stop=(j == NSH // 2 - 1))
                        mm.then_inc(S["pT_ps"], 1)

                    def values(u):
                        h = u % HEADS0
                        pe.wait_ge(S["pT_ready"], UNITS * i + u + 1)
                        if u >= 2:
                            pe.wait_ge(S["context_part"], UNITS * i + u - 1)
                        for t in range(TT):
                            mm = pe.matmul([ps_c, ps_v][u % 2][:, u * DH0:(u + 1) * DH0], probT[u % 2][:, t, :], vsum[b][:, t, h * DH0:(h + 1) * DH0],
                                           start=(t == 0), stop=(t == TT - 1))
                        mm.then_inc(S["ctx_ps"], 1)

                    pe.wait_ge(S["T_used"], use(i, SUM) + 2)
                    pe.wait_ge(S["parts_ready"], 2 * HEADS0 * i + 2 * HEADS0)
                    for step in range(UNITS + 4):
                        if step < UNITS:
                            scores(step)
                        if more and 0 <= step - FIRST < ITEMS:
                            item(i + 1, step - FIRST)
                        if 3 <= step < UNITS + 3:
                            transposes(step - 3)
                        if step >= 4:
                            values(step - 4)
                    held(pe, S["context_ready"], i + 1, pe_passed)
                    held(pe, S["T_used"], context_use(i) + 1, pe_passed)
                    for t in range(TT):
                        mm = pe.transpose(ps_T[0:D, t * P:(t + 1) * P], context[:, t, :], ident[:, :])
                    mm.then_inc(S["T_ps"], 1)
                    pe.wait_ge(S["T_used"], context_use(i) + 2)
                    for t in range(TT):
                        mm = pe.matmul(ps_v[:, t * D:(t + 1) * D], contextT[:, t * P:(t + 1) * P], wo[:, :], start=True, stop=True)
                    mm.then_inc(S["y_ps"], 1)

                sequences(pe, prepare, body)

        clear_semaphores(nc, sems)


HID0, EXPERTS = 256, 8
HC0 = HID0 // P


def routed_ffn(nc, w, h_in, h_out):
    with ExitStack() as ctx:
        def sb(name, shape, dt=F32):
            return ctx.enter_context(nc.sbuf_tensor("ff0_" + name, shape, dt))

        def ps(name, shape):
            return ctx.enter_context(nc.psum_tensor("ff0_" + name, shape, F32))

        sems = []

        def sem(name):
            sems.append(ctx.enter_context(nc.semaphore("ff0_" + name)))
            return sems[-1]

        w1 = sb("w1", [D + 1, HID0])
        wg = sb("wg", [P, HC0, EXPERTS])
        bg = sb("bg", [1, EXPERTS])
        wd = sb("wd", [P, HC0, EXPERTS * D])
        bd = sb("bd", [1, EXPERTS * D])
        ones_row = sb("ones_row", [1, P])
        eps = sb("eps", [P, 1])
        ident = sb("ident", [P, P])
        expert_id_i = sb("expert_id_i", [P, EXPERTS], I32)
        expert_id = sb("expert_id", [P, EXPERTS])
        R = range(2)
        x = [sb(f"x{b}", [P, TT, D]) for b in R]
        xn = [sb(f"xn{b}", [P, TT, D]) for b in R]
        stats = [sb(f"stats{b}", [P, TT, 6]) for b in R]
        moments = [sb(f"moments{b}", [P, TT, 2]) for b in R]
        std = [sb(f"std{b}", [P, TT]) for b in R]
        xnT = [sb(f"xnT{b}", [D + 1, T]) for b in R]
        hidT = [sb(f"hidT{b}", [P, HC0, T]) for b in R]
        prob = [sb(f"prob{b}", [P, TT, EXPERTS]) for b in R]
        pmax = [sb(f"pmax{b}", [P, TT]) for b in R]
        psum_e = [sb(f"psum_e{b}", [P, TT]) for b in R]
        top8 = [sb(f"top8{b}", [P, TT, 8]) for b in R]
        top8_at = [sb(f"top8_at{b}", [P, TT, 8], U32) for b in R]
        best = [sb(f"best{b}", [P, TT]) for b in R]
        pick = [sb(f"pick{b}", [P, TT, EXPERTS]) for b in R]
        picked = [sb(f"picked{b}", [P, EXPERTS, D]) for b in R]
        y = [sb(f"y{b}", [P, TT, D]) for b in R]
        ps_T = ps("ps_T", [P, T])
        ps_hid = [ps(f"ps_hid{k}", [P, T]) for k in R]
        ps_g = ps("ps_g", [P, T])
        ps_y = [ps(f"ps_y{k}", [P, EXPERTS * D]) for k in range(4)]
        loaded, gp_made, x_used = sem("loaded"), sem("gp_made"), sem("x_used")
        x_in = [sem(f"x_in{b}") for b in R]
        stored = [sem(f"stored{b}") for b in R]
        names = ("moments_ready std_ready xn_ready xnT_ps xnT_ready hid_ps hid_ready gates_ps gates_centred gates_exp "
                 "y_ps y_used y_ready")
        S = {n: sem(n) for n in names.split()}
        dve_steps, dve_passed, pe_passed = sem("dve_steps"), sem("dve_passed"), sem("pe_passed")

        with nc.Block() as block:
            @block.sync
            def _(sp):
                for dst, src in ((w1[0:D, :], w["W1"]), (w1[D:D + 1, :], w["b1"].unsqueeze(0)),
                                 (wg[:, :, :], w["Wg"].rearrange("(c p) e -> p c e", p=P)), (bg[:, :], w["bg"].unsqueeze(0)),
                                 (bd[:, :], w["bd"].rearrange("e d -> (e d)").unsqueeze(0))):
                    sp.dma_start(dst, src).then_inc(loaded, 16)
                for c in range(HC0):
                    sp.dma_start(wd[:, c, :].rearrange("p (e d) -> p e d", e=EXPERTS),
                                 w["Wd"][:, c * P:(c + 1) * P, :].rearrange("e p d -> p e d")).then_inc(loaded, 16)
                sp.wait_ge(loaded, 16 * (5 + HC0))

            @block.gpsimd
            def _(pool):
                pool.iota(expert_id_i[:, :], [[1, EXPERTS]], base=0, channel_multiplier=0).then_inc(gp_made, 1)
                pool.memset(ident[:, :], 0.0).then_inc(gp_made, 1)
                pool.wait_ge(gp_made, 2)
                pool.affine_select(out=ident[:, :], in_=ident[:, :], compare_op=ALU.not_equal, fill=1.0, base=0,
                                   pattern=[[-1, P]], channel_multiplier=1).then_inc(gp_made, 1)

            @block.vector
            def _(dve):
                s = Steps(dve, dve_steps)
                s.did(dve.memset(ones_row[:, :], 1.0))
                s.did(dve.memset(eps[:, :], EPS))
                for b in R:
                    s.did(dve.memset(xnT[b][D:D + 1, :], 1.0))
                dve.wait_ge(gp_made, 3)
                s.did(dve.tensor_copy(expert_id[:, :], expert_id_i[:, :]))
                s.wait()
                dve.sem_clear(dve_steps)

        with nc.Block() as block:
            @block.sync
            def _(sp):
                sp.sem_inc(x_used, 2)
                with sp.Fori(0, B // 2) as i:
                    for b in R:
                        sp.wait_ge(x_used, 2 * i + b + 1)
                        sp.dma_start(x[b][:, :, :], h_in[bass.ds((2 * i + b) * T, T), :].rearrange("(t p) d -> p t d", p=P)).then_inc(x_in[b], 16)
                    for b in R:
                        sp.wait_ge(S["y_ready"], 2 * i + b + 1)
                        sp.dma_start(h_out[bass.ds((2 * i + b) * T, T), :].rearrange("(t p) d -> p t d", p=P), y[b][:, :, :]).then_inc(stored[b], 16)
                for b in R:
                    sp.wait_ge(stored[b], 16 * B // 2)

            @block.vector
            def _(dve):
                s = Steps(dve, dve_steps)
                with dve.Fori(0, B // 2) as i:
                    n = [2 * i + 1, 2 * i + 2]
                    s.restart()
                    for b in R:
                        held(dve, x_in[b], 16 * i + 16, dve_passed)
                        ln_moments(dve, s, x[b], stats[b], moments[b])
                        dve.sem_inc(S["moments_ready"], 1)
                    for b in R:
                        dve.wait_ge(S["std_ready"], n[b])
                        ln_apply(dve, s, xn[b], x[b], moments[b], std[b]).then_inc(S["xn_ready"], 1)
                    for b in R:
                        dve.wait_ge(S["xnT_ps"], n[b])
                        dve.tensor_copy(xnT[b][0:D, :], ps_T[0:D, :]).then_inc(S["xnT_ready"], 1)
                    for b in R:
                        dve.wait_ge(S["gates_ps"], n[b])
                        g = ps_g[:, 0:TT * EXPERTS].rearrange("p (t e) -> p t e", e=EXPERTS)
                        s.did(dve.tensor_reduce(pmax[b][:, :], g, AX.X, ALU.max))
                        s.wait()
                        dve.tensor_tensor(prob[b][:, :, :], g, bc(pmax[b][:, :], 2, EXPERTS), ALU.subtract).then_inc(S["gates_centred"], 1)
                    for b in R:
                        dve.wait_ge(S["gates_exp"], n[b])
                        s.did(dve.tensor_reduce(psum_e[b][:, :], prob[b][:, :, :], AX.X, ALU.add))
                        s.wait()
                        s.did(dve.reciprocal(psum_e[b][:, :], psum_e[b][:, :]))
                        s.wait()
                        s.did(dve.tensor_tensor(prob[b][:, :, :], prob[b][:, :, :], bc(psum_e[b][:, :], 2, EXPERTS), ALU.mult))
                        s.wait()
                        for t in range(TT):
                            s.did(dve.max(top8[b][:, t, :], prob[b][:, t, :]))
                        s.wait()
                        for t in range(TT):
                            s.did(dve.max_index(top8_at[b][:, t, :], top8[b][:, t, :], prob[b][:, t, :]))
                        s.wait()
                        s.did(dve.tensor_copy(best[b][:, :], top8_at[b][:, :, 0]))
                        s.wait()
                        s.did(dve.tensor_tensor(pick[b][:, :, :], bc(expert_id[:, :], 1, TT), bc(best[b][:, :], 2, EXPERTS), ALU.is_equal))
                        s.wait()
                        s.did(dve.tensor_tensor(pick[b][:, :, :], pick[b][:, :, :], prob[b][:, :, :], ALU.mult))
                        s.wait()
                        for t in range(TT):
                            dve.wait_ge(S["y_ps"], 2 * TT * i + TT * b + t + 1)
                            dve.tensor_tensor(picked[t % 2][:, :, :], ps_y[t][:, :].rearrange("p (e d) -> p e d", e=EXPERTS),
                                              bc(pick[b][:, t, :], 2, D), ALU.mult).then_inc(S["y_used"], 1)
                            dve.wait_ge(S["y_used"], 2 * TT * i + TT * b + t + 1)
                            s.did(dve.tensor_reduce(y[b][:, t, :], picked[t % 2][:, :, :].rearrange("p e d -> p d e"), AX.X, ALU.add))
                            s.wait()
                        s.did(dve.tensor_tensor(y[b][:, :, :], y[b][:, :, :], x[b][:, :, :], ALU.add))
                        s.wait()
                        dve.sem_inc(x_used, 1)
                        dve.sem_inc(S["y_ready"], 1)
                s.wait()

            @block.scalar
            def _(act):
                with act.Fori(0, B // 2) as i:
                    n = [2 * i + 1, 2 * i + 2]
                    for b in R:
                        act.wait_ge(S["moments_ready"], n[b])
                        act.activation(std[b][:, :], moments[b][:, :, 1], ACT.Sqrt, bias=eps[:, 0:1]).then_inc(S["std_ready"], 1)
                    for b in R:
                        for c in range(HC0):
                            act.wait_ge(S["hid_ps"], 2 * HC0 * i + HC0 * b + c + 1)
                            act.activation(hidT[b][:, c, :], ps_hid[c][:, :], ACT.Gelu).then_inc(S["hid_ready"], 1)
                    for b in R:
                        act.wait_ge(S["gates_centred"], n[b])
                        act.activation(prob[b][:, :, :], prob[b][:, :, :], ACT.Exp).then_inc(S["gates_exp"], 1)

            @block.tensor
            def _(pe):
                with pe.Fori(0, B // 2) as i:
                    n = [2 * i + 1, 2 * i + 2]
                    for b in R:
                        if b == 1:
                            pe.wait_ge(S["xnT_ready"], n[0])
                        held(pe, S["xn_ready"], n[b], pe_passed)
                        for t in range(TT):
                            mm = pe.transpose(ps_T[0:D, t * P:(t + 1) * P], xn[b][:, t, :], ident[:, :])
                        mm.then_inc(S["xnT_ps"], 1)
                    for b in R:
                        pe.wait_ge(S["xnT_ready"], n[b])
                        for c in range(HC0):
                            if b == 1:
                                pe.wait_ge(S["hid_ready"], 2 * HC0 * i + c + 1)
                            pe.matmul(ps_hid[c][:, :], w1[:, c * P:(c + 1) * P], xnT[b][:, :], start=True, stop=True).then_inc(S["hid_ps"], 1)
                    for b in R:
                        pe.wait_ge(S["hid_ready"], 2 * HC0 * i + HC0 * (b + 1))
                        if b == 1:
                            pe.wait_ge(S["gates_centred"], n[0])
                        for t in range(TT):
                            out = ps_g[:, t * EXPERTS:(t + 1) * EXPERTS]
                            for c in range(HC0):
                                pe.matmul(out, hidT[b][:, c, t * P:(t + 1) * P], wg[:, c, :], start=(c == 0), stop=False)
                            mm = pe.matmul(out, ones_row[:, :], bg[:, :], start=False, stop=True)
                        mm.then_inc(S["gates_ps"], 1)
                        for t in range(TT):
                            if b == 1:
                                pe.wait_ge(S["y_used"], 2 * TT * i + t + 1)
                            for c in range(HC0):
                                pe.matmul(ps_y[t][:, :], hidT[b][:, c, t * P:(t + 1) * P], wd[:, c, :], start=(c == 0), stop=False)
                            pe.matmul(ps_y[t][:, :], ones_row[:, :], bd[:, :], start=False, stop=True).then_inc(S["y_ps"], 1)

        clear_semaphores(nc, sems)


HEADS1 = 8
PAIRS = HEADS1 // 2
ROWS3 = 3 * NTOK


def project_qkv(nc, w, h_in, qkvT):
    with ExitStack() as ctx:
        def sb(name, shape, dt=F32):
            return ctx.enter_context(nc.sbuf_tensor("prj_" + name, shape, dt))

        def ps(name, shape):
            return ctx.enter_context(nc.psum_tensor("prj_" + name, shape, F32))

        sems = []

        def sem(name):
            sems.append(ctx.enter_context(nc.semaphore("prj_" + name)))
            return sems[-1]

        R = range(2)
        wqkv = sb("wqkv", [D + 1, 3, PAIRS, P])
        eps = sb("eps", [P, 1])
        ident = sb("ident", [P, P])
        x = [sb(f"x{b}", [P, TT, D]) for b in R]
        xn = [sb(f"xn{b}", [P, TT, D]) for b in R]
        stats = [sb(f"stats{b}", [P, TT, 6]) for b in R]
        moments = [sb(f"moments{b}", [P, TT, 2]) for b in R]
        std = [sb(f"std{b}", [P, TT]) for b in R]
        xnT = [sb(f"xnT{b}", [D + 1, T]) for b in R]
        rows = [sb(f"rows{k}", [P, T, 3]) for k in range(4)]
        ps_T = ps("ps_T", [P, T])
        ps_r = [ps(f"ps_r{k}", [P, T]) for k in range(6)]
        loaded, gp_made, x_used = sem("loaded"), sem("gp_made"), sem("x_used")
        x_in = [sem(f"x_in{b}") for b in R]
        stored = [sem(f"stored{k}") for k in range(4)]
        names = "moments_ready std_ready xn_ready xnT_ps xnT_ready rows_ps"
        S = {n: sem(n) for n in names.split()}
        rows_dve, rows_act = sem("rows_dve"), sem("rows_act")
        dve_steps, dve_passed, pe_passed = sem("dve_steps"), sem("dve_passed"), sem("pe_passed")

        with nc.Block() as block:
            @block.sync
            def _(sp):
                sp.dma_start(wqkv[0:D, :, :, :].rearrange("i c f m -> i (c f m)"), w["Wqkv_heads"]).then_inc(loaded, 16)
                sp.dma_start(wqkv[D:D + 1, :, :, :].rearrange("i c f m -> i (c f m)"), w["bqkv_heads"].unsqueeze(0)).then_inc(loaded, 16)
                sp.wait_ge(loaded, 32)

            @block.gpsimd
            def _(pool):
                pool.memset(ident[:, :], 0.0).then_inc(gp_made, 1)
                pool.wait_ge(gp_made, 1)
                pool.affine_select(out=ident[:, :], in_=ident[:, :], compare_op=ALU.not_equal, fill=1.0, base=0,
                                   pattern=[[-1, P]], channel_multiplier=1).then_inc(gp_made, 1)

            @block.vector
            def _(dve):
                dve.memset(eps[:, :], EPS)
                for b in R:
                    dve.memset(xnT[b][D:D + 1, :], 1.0)

        with nc.Block() as block:
            @block.sync
            def _(sp):
                sp.sem_inc(x_used, 2)
                for f in range(PAIRS):
                    sp.sem_inc(stored[f], 16)
                with sp.Fori(0, B // 2) as i:
                    for b in R:
                        sp.wait_ge(x_used, 2 * i + b + 1)
                        sp.dma_start(x[b][:, :, :], h_in[bass.ds((2 * i + b) * T, T), :].rearrange("(t p) d -> p t d", p=P)).then_inc(x_in[b], 16)
                    for b in R:
                        for f in range(PAIRS):
                            sp.wait_ge(rows_act, 4 * (2 * i + b) + f + 1)
                            sp.wait_ge(rows_dve, 4 * (2 * i + b) + f + 1)
                            sp.dma_start(qkvT[f, :, bass.ds((2 * i + b) * 3 * T, 3 * T)],
                                         rows[f][:, :, :].rearrange("p t c -> p (t c)")).then_inc(stored[f], 16)
                for f in range(PAIRS):
                    sp.wait_ge(stored[f], 16 * (B + 1))

            @block.vector
            def _(dve):
                s = Steps(dve, dve_steps)
                with dve.Fori(0, B // 2) as i:
                    n = [2 * i + 1, 2 * i + 2]
                    s.restart()
                    for b in R:
                        held(dve, x_in[b], 16 * i + 16, dve_passed)
                        ln_moments(dve, s, x[b], stats[b], moments[b])
                        dve.sem_inc(S["moments_ready"], 1)
                    for b in R:
                        dve.wait_ge(S["std_ready"], n[b])
                        s.did(ln_apply(dve, s, xn[b], x[b], moments[b], std[b]))
                        s.wait()
                        dve.sem_inc(S["xn_ready"], 1)
                        dve.sem_inc(x_used, 1)
                    for b in R:
                        dve.wait_ge(S["xnT_ps"], n[b])
                        dve.tensor_copy(xnT[b][0:D, :], ps_T[0:D, :]).then_inc(S["xnT_ready"], 1)
                    for b in R:
                        for f in range(PAIRS):
                            dve.wait_ge(stored[f], 16 * (2 * i + b) + 16)
                            dve.wait_ge(S["rows_ps"], 12 * (2 * i + b) + 3 * f + 1)
                            dve.tensor_copy(rows[f][:, :, 0], ps_r[3 * (f % 2)][:, :]).then_inc(rows_dve, 1)
                s.wait()

            @block.scalar
            def _(act):
                with act.Fori(0, B // 2) as i:
                    n = [2 * i + 1, 2 * i + 2]
                    for b in R:
                        act.wait_ge(S["moments_ready"], n[b])
                        act.activation(std[b][:, :], moments[b][:, :, 1], ACT.Sqrt, bias=eps[:, 0:1]).then_inc(S["std_ready"], 1)
                    for b in R:
                        for f in range(PAIRS):
                            act.wait_ge(stored[f], 16 * (2 * i + b) + 16)
                            for c in range(1, 3):
                                act.wait_ge(S["rows_ps"], 12 * (2 * i + b) + 3 * f + c + 1)
                                ins = act.activation(rows[f][:, :, c], ps_r[3 * (f % 2) + c][:, :], ACT.Copy)
                            ins.then_inc(rows_act, 1)

            @block.tensor
            def _(pe):
                with pe.Fori(0, B // 2) as i:
                    n = [2 * i + 1, 2 * i + 2]
                    for b in R:
                        if b == 1:
                            pe.wait_ge(S["xnT_ready"], n[0])
                        held(pe, S["xn_ready"], n[b], pe_passed)
                        for t in range(TT):
                            mm = pe.transpose(ps_T[0:D, t * P:(t + 1) * P], xn[b][:, t, :], ident[:, :])
                        mm.then_inc(S["xnT_ps"], 1)
                    for b in R:
                        pe.wait_ge(S["xnT_ready"], n[b])
                        for f in range(PAIRS):
                            if b or f >= 2:
                                pe.wait_ge(rows_dve, 4 * (2 * i + b) + f - 1)
                                pe.wait_ge(rows_act, 4 * (2 * i + b) + f - 1)
                            for c in range(3):
                                pe.matmul(ps_r[3 * (f % 2) + c][:, :], wqkv[:, c, f, :], xnT[b][:, :], start=True, stop=True).then_inc(S["rows_ps"], 1)

        clear_semaphores(nc, sems)


HEADS2, NKEYS, DKEY, TOPK = 8, 64, 32, 16
NKV = NKEYS * NKEYS
GROUPS = 2 * HEADS2
LOW = -3.0e38
MASKED = -1.0e30
RUNS, _a = [], 0
while _a < TOPK:
    _n = TOPK // (_a + 1)
    _e = _a
    while _e < TOPK and TOPK // (_e + 1) == _n:
        _e += 1
    RUNS.append((_a, _e, _n))
    _a = _e
CANDS = sum((e - a) * n for a, e, n in RUNS)
KV = 2 * D
GSLOTS = 4
UN = TT * HEADS2


class Round:

    def __init__(self, q, c):
        self.q, self.c = q, c
        self.par = c % 2
        loop = q is not None
        self.dia = loop or c < B - 1
        self.mix = loop or 0 <= c < B
        self.cau = loop or c >= 1

    def at(self, each, offset):
        if self.q is None:
            return each * self.c + offset
        return 2 * each * self.q + (each * self.c + offset)

    def chosen(self, t):
        return self.q is not None or 0 <= 4 * self.c + t + 1 < B * TT

    def compared(self, t):
        return self.q is not None or 0 <= 4 * self.c + t + 2 < B * TT

    def front_uses(self, t):
        first = self.q is None and self.c < 0
        if first:
            return t + 3 * max(0, t - 2)
        each = 3 if not self.dia else 4
        return self.at(16, 10 + each * t)


def rounds(eng, body):
    body(Round(None, -1))
    body(Round(None, 0))
    with eng.Fori(0, B // 2 - 1) as q:
        body(Round(q, 1))
        body(Round(q, 2))
    body(Round(None, B - 1))
    body(Round(None, B))


def past(eng, sem, value):
    if not isinstance(value, int) or value > 0:
        eng.wait_ge(sem, value)


def idx_probs(u):
    return PAIRS + u + max(0, (u - 1) // HEADS2)


def idx_outs(t):
    return PAIRS + min(8 * t + 9, UN) + t


TUSES = PAIRS + UN + TT
OUSES = UN + TT


def idx_values(u):
    return u + u // HEADS2


def sequence_pipeline(nc, w1, w2, qkvT, h_in, h_mid, h_out):
    with ExitStack() as ctx:
        def sb(name, shape, dt=F32):
            return ctx.enter_context(nc.sbuf_tensor("sq_" + name, shape, dt))

        def ps(name):
            return ctx.enter_context(nc.psum_tensor("sq_" + name, [P, 512], F32))

        sems = []

        def sem(name):
            sems.append(ctx.enter_context(nc.semaphore("sq_" + name)))
            return sems[-1]

        R = range(2)
        SCALE = float(D) ** -0.5
        ident = sb("ident", [P, P])
        eps = sb("eps", [P, 1])
        w0 = sb("w0", [P, PAIRS, 2 * D])
        b0 = sb("b0", [P, D])
        d_q, d_k, d_v = (sb("d_" + n, [P, PAIRS, T]) for n in "qkv")
        d_x = sb("d_x", [P, TT, D])
        d_negmax, d_bias, d_diag, d_sums, d_attn = (sb("d_" + n, [P, UN]) for n in ("negmax", "bias", "diag", "sums", "attn"))
        diag_out = [sb(f"diag_out{k}", [P, P]) for k in R]
        exp_out = [sb(f"exp_out{k}", [P, T]) for k in R]
        weighted = sb("weighted", [P, HEADS1, D])
        mid = sb("mid", [P, TT, D])
        stats = sb("stats", [P, 6])
        moments = sb("moments", [P, 2])
        std = sb("std", [P, 1])
        xn = sb("xn", [P, D])
        xnT = sb("xnT", [D, TT, P])
        wpkT = sb("wpkT", [DKEY, GROUPS, D])
        keysT = sb("keysT", [DKEY, GROUPS, NKEYS])
        wsim = sb("wsim", [D, GROUPS * NKEYS])
        wq = sb("wq", [D, HEADS2 * D])
        head_base_i = sb("head_base_i", [P, HEADS2], I32)
        head_base = sb("head_base", [P, HEADS2])
        cand_id_i = sb("cand_id_i", [P, CANDS], I32)
        cand_id = sb("cand_id", [P, CANDS])
        sim = [sb(f"sim{b}", [P, GROUPS, NKEYS]) for b in R]
        sim_rest = sb("sim_rest", [P, GROUPS, NKEYS])
        top = sb("top", [P, GROUPS, TOPK])
        top_at = sb("top_at", [P, GROUPS, TOPK], U32)
        top_at_f = sb("top_at_f", [P, GROUPS, TOPK])
        cand = sb("cand", [P, HEADS2, CANDS])
        cand_rest = sb("cand_rest", [P, HEADS2, CANDS])
        cand_row = sb("cand_row", [P, HEADS2, CANDS])
        best = sb("best", [P, HEADS2, TOPK])
        best_at = sb("best_at", [P, HEADS2, TOPK], U32)
        best_at_f = sb("best_at_f", [P, HEADS2, TOPK])
        is_cand = [sb(f"is_cand{k}", [P, TOPK, CANDS]) for k in R]
        row_f = sb("row_f", [P, HEADS2, TOPK])
        row = [sb(f"row{b}", [P, HEADS2, TOPK], I32) for b in R]
        weight = [sb(f"weight{b}", [P, HEADS2, TOPK]) for b in R]
        wsum = sb("wsum", [P, HEADS2])
        rows = [sb(f"rows{k}", [P, TOPK, KV]) for k in range(GSLOTS)]
        qT = [sb(f"qT{b}", [P, PAIRS, T]) for b in R]
        kv = [sb(f"kv{b}", [P, TT, 2, HEADS2, D]) for b in R]
        future = sb("future", [P, P])
        wo = sb("wo", [P, PAIRS, D])
        c_x = sb("c_x", [P, TT, D])
        kT = sb("kT", [P, PAIRS, T])
        c_negmax, c_sums, c_inv = (sb("c_" + n, [P, UN]) for n in ("negmax", "sums", "inv"))
        prob = [sb(f"prob{k}", [P, T]) for k in R]
        probT = [sb(f"probT{k}", [P, T]) for k in R]
        out = [sb(f"out{k}", [P, HEADS2, D]) for k in R]
        outT = sb("outT", [P, PAIRS, P])
        y = sb("y", [P, TT, D])
        ps_d = [ps(f"ps_d{k}") for k in R]
        ps_v = ps("ps_v")
        ps_f = ps("ps_f")
        ps_c = [ps(f"ps_c{k}") for k in R]
        ps_t = ps("ps_t")
        ps_o = ps("ps_o")

        loaded, gp_made, dve_made, pe_made, zeroed = sem("loaded"), sem("gp_made"), sem("dve_made"), sem("pe_made"), sem("zeroed")
        names = ("d_in d_used d_scores d_bias d_exp d_pre d_attn d_vals d_vals_used mid_ready "
                 "moments_ready std_ready xn_ready f_ps f_used sim_ready sim_used best_centred weight_exp row_ready "
                 "rows_used q_ready kv_ready c_in c_used c_scores c_max c_probs t_ps t_used o_ps o_used y_ready y_stored")
        S = {n: sem(n) for n in names.split()}
        mid_stored = [sem(f"mid_stored{t}") for t in range(TT)]
        dve_steps, sp_passed, dve_passed, pe_passed, pool_passed = (sem(n) for n in ("dve_steps", "sp_passed", "dve_passed", "pe_passed", "pool_passed"))
        gathered = [nc.alloc_semaphore(f"sq_gathered{k}") for k in range(GSLOTS)]

        with nc.Block() as block:
            @block.sync
            def _(sp):
                for dst, src in ((wpkT, "Wq_pkT"), (keysT, "keysT")):
                    sp.dma_start(dst[:, :, :], w2[src]).then_inc(loaded, 16)
                sp.wait_ge(loaded, 32)
                sp.dma_start(wq[:, :], w2["Wq"]).then_inc(loaded, 16)
                sp.dma_start(wo[:, :, :], w2["Wo"].rearrange("(f p) o -> p f o", p=P)).then_inc(loaded, 16)
                sp.dma_start(b0[:, :], w1["b0"].partition_broadcast(P)).then_inc(loaded, 16)
                sp.wait_ge(zeroed, 1)
                for hh in range(2):
                    sp.dma_start(w0[hh * D:(hh + 1) * D, :, hh * D:(hh + 1) * D],
                                 w1["W0_heads"].rearrange("(f a) d o -> a d f o", a=2)[hh]).then_inc(loaded, 16)
                sp.wait_ge(loaded, 112)

            @block.gpsimd
            def _(pool):
                pool.iota(head_base_i[:, :], [[NKV, HEADS2]], base=0, channel_multiplier=0).then_inc(gp_made, 1)
                pool.iota(cand_id_i[:, :], [[1, CANDS]], base=0, channel_multiplier=0).then_inc(gp_made, 1)
                pool.memset(ident[:, :], 0.0).then_inc(gp_made, 1)
                pool.memset(future[:, :], 0.0).then_inc(gp_made, 1)
                pool.wait_ge(gp_made, 4)
                pool.affine_select(out=ident[:, :], in_=ident[:, :], compare_op=ALU.not_equal, fill=1.0, base=0,
                                   pattern=[[-1, P]], channel_multiplier=1).then_inc(gp_made, 1)
                pool.affine_select(out=future[:, :], in_=future[:, :], compare_op=ALU.is_ge, fill=MASKED, base=0,
                                   pattern=[[-1, P]], channel_multiplier=1).then_inc(gp_made, 1)

            @block.tensor
            def _(pe):
                pe.wait_ge(loaded, 32)
                for g in range(GROUPS):
                    if g == 8:
                        pe.wait_ge(dve_made, 1)
                    mm = pe.matmul(ps_f[0:D, (g % 8) * NKEYS:(g % 8 + 1) * NKEYS], wpkT[:, g, :], keysT[:, g, :], start=True, stop=True)
                    if g % 8 == 7:
                        mm.then_inc(pe_made, 1)

            @block.vector
            def _(dve):
                dve.memset(w0[:, :, :], 0.0).then_inc(zeroed, 1)
                dve.memset(eps[:, :], EPS)
                dve.wait_ge(gp_made, 4)
                dve.tensor_copy(head_base[:, :], head_base_i[:, :])
                dve.tensor_copy(cand_id[:, :], cand_id_i[:, :])
                for half in R:
                    dve.wait_ge(pe_made, half + 1)
                    dve.tensor_copy(wsim[:, half * 512:(half + 1) * 512], ps_f[0:D, :]).then_inc(dve_made, 1)

        with nc.Block() as block:
            @block.sync
            def _(sp):
                for name in ("d_used", "c_used"):
                    sp.sem_inc(S[name], 1)
                for t in range(TT):
                    sp.sem_inc(mid_stored[t], 16)
                sp.sem_inc(S["y_stored"], 16)

                def body(r):
                    if r.dia:
                        sp.wait_ge(S["d_used"], r.at(1, 2))
                        for m, dst in enumerate((d_q, d_k, d_v)):
                            src = qkvT[:, :, bass.ds(r.at(T, T + m * NTOK), T)].rearrange("f p t -> p f t")
                            sp.dma_start(dst[:, :, :], src).then_inc(S["d_in"], 16)
                        sp.dma_start(d_x[:, :, :], h_in[bass.ds(r.at(T, T), T), :].rearrange("(t p) d -> p t d", p=P)).then_inc(S["d_in"], 16)
                    if r.cau:
                        held(sp, S["c_used"], r.at(1, 0), sp_passed)
                        for t in range(TT):
                            sp.wait_ge(mid_stored[t], r.at(16, 16))
                        sp.dma_start(c_x[:, :, :], h_mid[bass.ds(r.at(T, -T), T), :].rearrange("(t p) d -> p t d", p=P)).then_inc(S["c_in"], 16)
                    if r.dia:
                        for t in range(TT):
                            sp.wait_ge(S["mid_ready"], r.at(TT, TT + t + 1))
                            sp.dma_start(h_mid[bass.ds(r.at(T, T + t * P), P), :], mid[:, t, :]).then_inc(mid_stored[t], 16)
                    if r.cau:
                        sp.wait_ge(S["y_ready"], r.at(1, 0))
                        sp.dma_start(h_out[bass.ds(r.at(T, -T), T), :].rearrange("(t p) d -> p t d", p=P), y[:, :, :]).then_inc(S["y_stored"], 16)

                rounds(sp, body)
                for t in range(TT):
                    sp.wait_ge(mid_stored[t], 16 * (B + 1))
                sp.wait_ge(S["y_stored"], 16 * (B + 1))

            @block.gpsimd
            def _(pool):
                pool.sem_inc(S["rows_used"], GSLOTS)

                def body(r):
                    for j in range(UN if r.mix else 0):
                        t, h = divmod(j, HEADS2)
                        if h == 0:
                            held(pool, S["row_ready"], r.at(TT, t + 1), pool_passed)
                        held(pool, S["rows_used"], r.at(UN, j + 1), pool_passed)
                        for k in range(TOPK):
                            pool.indirect_dma_start(rows[j % GSLOTS][:, k, :], None, w2["table"],
                                                    bass.IndirectOffsetOnAxis(row[t % 2][:, h, k:k + 1], 0)).then_inc(gathered[j % GSLOTS], 16)

                rounds(pool, body)

            @block.tensor
            def _(pe):
                pe.sem_inc(S["d_exp"], 2)
                pe.sem_inc(S["d_vals_used"], 1)
                pe.sem_inc(S["f_used"], 1)
                pe.sem_inc(S["c_scores"], 1)
                pe.sem_inc(S["c_probs"], 2)
                pe.sem_inc(S["t_used"], 1)
                pe.sem_inc(S["o_used"], 1)

                def body(r):
                    def t_at(n):
                        return r.at(TUSES, n - TUSES)

                    def o_at(n):
                        return r.at(OUSES, n - OUSES)

                    def diagonal_scores(u):
                        t, h = divmod(u, HEADS1)
                        f = slice((h % 2) * D, (h % 2 + 1) * D)
                        pe.wait_ge(S["d_exp"], r.at(UN, UN + u + 1))
                        pe.matmul(ps_d[u % 2][:, :], d_k[f, h // 2, t * P:(t + 1) * P], d_q[f, h // 2, :],
                                  start=True, stop=True).then_inc(S["d_scores"], 1)

                    def causal_scores(u):
                        t, h = divmod(u, HEADS2)
                        f = slice((h % 2) * D, (h % 2 + 1) * D)
                        pe.wait_ge(S["c_probs"], r.at(UN, u + 1 - UN))
                        q = qT[1 - r.par][f, h // 2, t * P:(t + 1) * P]
                        own = slice(t * P, (t + 1) * P)
                        if t:
                            pe.matmul(ps_c[u % 2][:, 0:t * P], q, kT[f, h // 2, 0:t * P], start=True, stop=True)
                        pe.matmul(ps_c[u % 2][:, own], q, kT[f, h // 2, own], start=True, stop=False)
                        pe.matmul(ps_c[u % 2][:, own], ident[:, :], future[:, :], start=False, stop=True).then_inc(S["c_scores"], 1)

                    def causal_transposes(u):
                        pe.wait_ge(S["c_probs"], r.at(UN, u + 3 - UN))
                        pe.wait_ge(S["t_used"], t_at(idx_probs(u) + 1))
                        for k in range(u // HEADS2 + 1):
                            mm = pe.transpose(ps_t[:, k * P:(k + 1) * P], prob[u % 2][:, k * P:(k + 1) * P], ident[:, :])
                        mm.then_inc(S["t_ps"], 1)

                    def causal_values(u):
                        t, h = divmod(u, HEADS2)
                        pe.wait_ge(S["t_used"], t_at(idx_probs(u) + 2))
                        pe.wait_ge(S["o_used"], o_at(idx_values(u) + 1))
                        for k in range(t + 1):
                            mm = pe.matmul(ps_o[:, 0:D], probT[u % 2][:, k * P:(k + 1) * P], kv[1 - r.par][:, k, 1, h, :],
                                           start=(k == 0), stop=(k == t))
                        mm.then_inc(S["o_ps"], 1)

                    def causal_projection(t):
                        pe.wait_ge(S["t_used"], t_at(idx_outs(t) + 1))
                        pe.wait_ge(S["o_used"], o_at(idx_values(8 * t + 7) + 2))
                        for f in range(PAIRS):
                            mm = pe.transpose(ps_t[:, f * P:(f + 1) * P], out[t % 2][:, 2 * f:2 * f + 2, :].rearrange("p h c -> p (h c)"), ident[:, :])
                        mm.then_inc(S["t_ps"], 1)
                        pe.wait_ge(S["t_used"], t_at(idx_outs(t) + 2))
                        for f in range(PAIRS):
                            mm = pe.matmul(ps_o[:, 0:D], outT[:, f, :], wo[:, f, :], start=(f == 0), stop=(f == PAIRS - 1))
                        mm.then_inc(S["o_ps"], 1)

                    if r.cau:
                        pe.wait_ge(S["q_ready"], r.at(TT, 0))
                        held(pe, S["kv_ready"], r.at(1, 0), pe_passed)
                        for f in range(PAIRS):
                            pe.wait_ge(S["t_used"], t_at(f + 1))
                            for t in range(TT):
                                mm = pe.transpose(ps_t[:, t * P:(t + 1) * P], kv[1 - r.par][:, t, 0, 2 * f:2 * f + 2, :].rearrange("p h c -> p (h c)"), ident[:, :])
                            mm.then_inc(S["t_ps"], 1)
                        pe.wait_ge(S["t_used"], t_at(PAIRS + 1))
                        causal_scores(0)
                    if r.dia:
                        pe.wait_ge(S["d_in"], r.at(64, 128))
                        diagonal_scores(0)
                    for j in range(UN + 2):
                        t, h = divmod(j, 8)
                        if r.dia and j + 1 < UN:
                            diagonal_scores(j + 1)
                        if r.cau:
                            if j + 1 < UN:
                                causal_scores(j + 1)
                            if 1 <= j <= UN:
                                causal_transposes(j - 1)
                            if j >= 2:
                                causal_values(j - 2)
                        if j < UN and 2 <= h <= 4 and r.compared(t):
                            x = xnT[:, (t + 2) % TT, :]
                            pe.wait_ge(S["f_used"], r.front_uses(t) + h - 1)
                            if h < 4:
                                mm = pe.matmul(ps_f[:, :], x, wsim[:, (h - 2) * 512:(h - 1) * 512], start=True, stop=True)
                            else:
                                for f in range(PAIRS):
                                    mm = pe.matmul(ps_f[:, f * P:(f + 1) * P], wq[:, f * P:(f + 1) * P], x, start=True, stop=True)
                            mm.then_inc(S["f_ps"], 1)
                        if j < UN and h == 7 and r.dia:
                            pe.wait_ge(S["d_vals_used"], r.at(TT, TT + t + 1))
                            for f in range(PAIRS):
                                mm = pe.matmul(ps_v[:, f * P:(f + 1) * P], d_v[:, f, t * P:(t + 1) * P], w0[:, f, :], start=True, stop=True)
                            mm.then_inc(S["d_vals"], 1)
                            pe.wait_ge(S["f_used"], r.front_uses(t) + (3 if r.compared(t) else 0) + 1)
                            held(pe, S["xn_ready"], r.at(TT, TT + t + 1), pe_passed)
                            pe.transpose(ps_f[0:D, 0:P], xn[:, :], ident[:, :]).then_inc(S["f_ps"], 1)
                        if r.cau and j >= 9 and h == 1:
                            causal_projection(t - 1)

                rounds(pe, body)

            @block.scalar
            def _(act):
                def body(r):
                    def t_at(n):
                        return r.at(TUSES, n - TUSES)

                    if r.cau:
                        for f in range(PAIRS):
                            act.wait_ge(S["t_ps"], t_at(f + 1))
                            act.activation(kT[:, f, :], ps_t[:, :], ACT.Copy).then_inc(S["t_used"], 1)
                    for j in range(UN + 2):
                        t, h = divmod(j, 8)
                        if r.dia and j < UN:
                            act.wait_ge(S["d_bias"], r.at(UN, UN + j + 1))
                            act.wait_ge(S["d_exp"], r.at(UN, UN + j + 1))
                            act.activation(exp_out[j % 2][:, :], ps_d[j % 2][:, :], ACT.Exp, bias=d_bias[:, j:j + 1], scale=SCALE,
                                           accum_out=d_sums[:, j:j + 1]).then_inc(S["d_exp"], 1)
                        if r.cau:
                            if j < UN:
                                w_ = (t + 1) * P
                                act.wait_ge(S["c_max"], r.at(UN, j + 1 - UN))
                                act.activation(prob[j % 2][:, 0:w_], ps_c[j % 2][:, 0:w_], ACT.Exp, bias=c_negmax[:, j:j + 1],
                                               accum_out=c_sums[:, j:j + 1]).then_inc(S["c_probs"], 1)
                            if 1 <= j <= UN:
                                u = j - 1
                                w_ = (u // HEADS2 + 1) * P
                                if u >= 2:
                                    act.wait_ge(S["o_ps"], r.at(OUSES, idx_values(u - 2) + 1 - OUSES))
                                act.wait_ge(S["t_ps"], t_at(idx_probs(u) + 1))
                                act.activation(probT[u % 2][:, 0:w_], ps_t[:, 0:w_], ACT.Copy).then_inc(S["t_used"], 1)
                        if j < UN and 2 <= h <= 4 and r.compared(t):
                            n = (t + 2) % TT
                            act.wait_ge(S["f_ps"], r.front_uses(t) + h - 1)
                            if h < 4:
                                if h == 2:
                                    act.wait_ge(S["sim_used"], r.at(TT, t + 3))
                                ins = act.activation(sim[t % 2][:, (h - 2) * HEADS2:(h - 1) * HEADS2, :], ps_f[:, :].rearrange("p (g k) -> p g k", k=NKEYS), ACT.Copy)
                                ins.then_inc(S["f_used"], 1)
                                if h == 3:
                                    act.wait_ge(S["f_used"], r.front_uses(t) + 3)
                                    act.sem_inc(S["sim_ready"], 1)
                            else:
                                past(act, S["c_scores"], r.at(UN, (1 - UN) if t < 2 else (8 * (t - 1) + 1 - UN)))
                                half = r.par if t < 2 else 1 - r.par
                                act.activation(qT[half][:, :, n * P:(n + 1) * P], ps_f[:, :].rearrange("p (f t) -> p f t", t=P), ACT.Copy,
                                               scale=float(D) ** -0.5).then_inc(S["f_used"], 1)
                                act.wait_ge(S["f_used"], r.front_uses(t) + 4)
                                act.sem_inc(S["q_ready"], 1)
                        if j < UN and h == 5 and r.chosen(t):
                            act.wait_ge(S["best_centred"], r.at(TT, t + 2))
                            wt = weight[(t + 1) % 2]
                            act.activation(wt[:, :, :], wt[:, :, :], ACT.Exp).then_inc(S["weight_exp"], 1)
                        if j < UN and h == 7 and r.dia:
                            a = d_attn[:, t * HEADS1:(t + 1) * HEADS1]
                            act.wait_ge(S["d_pre"], r.at(TT, TT + t + 1))
                            act.activation(a, a, ACT.Exp).then_inc(S["d_attn"], 1)
                            act.wait_ge(S["moments_ready"], r.at(TT, TT + t + 1))
                            act.activation(std[:, :], moments[:, 1:2], ACT.Sqrt, bias=eps[:, 0:1]).then_inc(S["std_ready"], 1)
                            act.wait_ge(S["f_ps"], r.front_uses(t) + (3 if r.compared(t) else 0) + 1)
                            act.activation(xnT[:, t, :], ps_f[0:D, 0:P], ACT.Copy).then_inc(S["f_used"], 1)
                        if r.cau and j >= 9 and h == 1:
                            act.wait_ge(S["t_ps"], t_at(idx_outs(t - 1) + 1))
                            act.activation(outT[:, :, :], ps_t[:, :].rearrange("p (f t) -> p f t", t=P), ACT.Copy).then_inc(S["t_used"], 1)

                rounds(act, body)

            @block.vector
            def _(dve):
                s = Steps(dve, dve_steps)
                dve.sem_inc(S["sim_used"], 2)

                def diagonal_unit(r, u):
                    t = u // HEADS1
                    dve.wait_ge(S["d_scores"], r.at(UN, UN + u + 1))
                    s.did(dve.tensor_tensor(diag_out[u % 2][:, :], ps_d[u % 2][:, t * P:(t + 1) * P], ident[:, :], ALU.mult))
                    s.did(dve.tensor_reduce(d_negmax[:, u:u + 1], ps_d[u % 2][:, :], AX.X, ALU.max, negate=True))
                    s.wait()
                    s.did(dve.tensor_reduce(d_diag[:, u:u + 1], diag_out[u % 2][:, :], AX.X, ALU.add))
                    dve.tensor_scalar(d_bias[:, u:u + 1], d_negmax[:, u:u + 1], SCALE, None, ALU.mult).then_inc(S["d_bias"], 1)
                    if u % HEADS1 == HEADS1 - 1:
                        units = slice(u + 1 - HEADS1, u + 1)
                        s.wait()
                        dve.wait_ge(S["d_bias"], r.at(UN, UN + u + 1))
                        dve.scalar_tensor_tensor(d_attn[:, units], d_diag[:, units], SCALE, d_bias[:, units], ALU.mult, ALU.add).then_inc(S["d_pre"], 1)

                def diagonal_tile(r, t):
                    units = slice(t * HEADS1, (t + 1) * HEADS1)
                    dve.wait_ge(S["d_attn"], r.at(TT, TT + t + 1))
                    s.did(dve.reciprocal(d_sums[:, units], d_sums[:, units]))
                    s.did(dve.tensor_tensor(d_x[:, t, :], d_x[:, t, :], b0[:, :], ALU.add))
                    s.wait()
                    s.did(dve.tensor_tensor(d_attn[:, units], d_attn[:, units], d_sums[:, units], ALU.mult))
                    s.wait()
                    dve.wait_ge(S["d_vals"], r.at(TT, TT + t + 1))
                    s.did(dve.tensor_tensor(weighted[:, :, :], ps_v[:, :].rearrange("p (h o) -> p h o", o=D), bc(d_attn[:, units], 2, D), ALU.mult))
                    s.wait()
                    dve.sem_inc(S["d_vals_used"], 1)
                    dve.wait_ge(mid_stored[t], r.at(16, 32))
                    s.did(dve.tensor_reduce(mid[:, t, :], weighted[:, :, :].rearrange("p h o -> p o h"), AX.X, ALU.add))
                    s.wait()
                    s.did(dve.tensor_tensor(mid[:, t, :], mid[:, t, :], d_x[:, t, :], ALU.add))
                    s.wait()
                    dve.sem_inc(S["mid_ready"], 1)
                    if t == TT - 1:
                        dve.sem_inc(S["d_used"], 1)
                    s.did(dve.bn_stats(stats[:, :], mid[:, t, :]))
                    s.wait()
                    s.did(dve.bn_aggr(moments[:, :], stats[:, :]))
                    s.wait()
                    dve.sem_inc(S["moments_ready"], 1)
                    dve.wait_ge(S["std_ready"], r.at(TT, TT + t + 1))
                    s.did(dve.reciprocal(std[:, :], std[:, :]))
                    past(dve, S["f_ps"], r.front_uses(t))
                    s.wait()
                    s.did(dve.tensor_scalar(xn[:, :], mid[:, t, :], moments[:, 0:1], std[:, 0:1], ALU.subtract, ALU.mult))
                    s.wait()
                    dve.sem_inc(S["xn_ready"], 1)

                def best8(groups, values, at, source, rest):
                    for g in range(groups):
                        s.did(dve.max(values[:, g, 0:8], source[:, g, :]))
                    s.wait()
                    for g in range(groups):
                        s.did(dve.match_replace(rest[:, g, :], values[:, g, 0:8], source[:, g, :], LOW))
                        s.did(dve.max_index(at[:, g, 0:8], values[:, g, 0:8], source[:, g, :]))
                    s.wait()

                def next8(groups, values, at, rest):
                    for g in range(groups):
                        s.did(dve.max(values[:, g, 8:16], rest[:, g, :]))
                    s.wait()
                    for g in range(groups):
                        s.did(dve.max_index(at[:, g, 8:16], values[:, g, 8:16], rest[:, g, :]))
                    s.wait()

                def candidates():
                    s.did(dve.tensor_copy(top_at_f[:, :, :], top_at[:, :, :]))
                    s.wait()
                    second = top_at_f[:, HEADS2:GROUPS, :]
                    s.did(dve.tensor_scalar(second, second, float(NKEYS), None, ALU.mult))
                    s.wait()
                    s.did(dve.tensor_tensor(second, second, bc(head_base[:, :], 2, TOPK), ALU.add))
                    s.wait()
                    at = 0
                    for a0, a1, nb in RUNS:
                        na = a1 - a0
                        for src, dst in ((top, cand), (top_at_f, cand_row)):
                            s.did(dve.tensor_tensor(
                                dst[:, :, at:at + na * nb].rearrange("p h (a b) -> p h a b", b=nb),
                                bc(src[:, 0:HEADS2, a0:a1], 3, nb), bc(src[:, HEADS2:GROUPS, 0:nb], 2, na), ALU.add))
                        at += na * nb
                    s.wait()

                def table_rows(heads):
                    for h in heads:
                        eq = is_cand[h % 2][:, :, :]
                        s.did(dve.tensor_tensor(eq, bc(cand_id[:, :], 1, TOPK), bc(best_at_f[:, h, :], 2, CANDS), ALU.is_equal))
                        s.wait()
                        s.did(dve.tensor_tensor(eq, eq, bc(cand_row[:, h, :], 1, TOPK), ALU.mult))
                        s.wait()
                        s.did(dve.tensor_reduce(row_f[:, h, :], eq, AX.X, ALU.add))
                    s.wait()

                def choose(r, t, piece):
                    b = (t + 1) % 2
                    if piece == 0:
                        held(dve, S["sim_ready"], r.at(TT, t + 2), dve_passed)
                        best8(GROUPS, top, top_at, sim[b], sim_rest)
                        dve.sem_inc(S["sim_used"], 1)
                    elif piece == 1:
                        next8(GROUPS, top, top_at, sim_rest)
                    elif piece == 2:
                        candidates()
                    elif piece == 3:
                        best8(HEADS2, best, best_at, cand, cand_rest)
                    elif piece == 4:
                        next8(HEADS2, best, best_at, cand_rest)
                        dve.tensor_tensor(weight[b][:, :, :], best[:, :, :], best[:, :, 0:1].broadcast_to([P, HEADS2, TOPK]), ALU.subtract).then_inc(S["best_centred"], 1)
                        s.did(dve.tensor_copy(best_at_f[:, :, :], best_at[:, :, :]))
                        s.wait()
                    elif piece == 5:
                        table_rows(range(HEADS2 // 2))
                    elif piece == 6:
                        table_rows(range(HEADS2 // 2, HEADS2))
                        s.did(dve.tensor_copy(row[b][:, :, :], row_f[:, :, :]))
                        s.wait()
                        dve.sem_inc(S["row_ready"], 1)
                        dve.wait_ge(S["weight_exp"], r.at(TT, t + 2))
                        s.did(dve.tensor_reduce(wsum[:, :], weight[b][:, :, :], AX.X, ALU.add))
                        s.wait()
                        s.did(dve.reciprocal(wsum[:, :], wsum[:, :]))
                        s.wait()
                        s.did(dve.tensor_tensor(weight[b][:, :, :], weight[b][:, :, :], bc(wsum[:, :], 2, TOPK), ALU.mult))
                        s.wait()

                def mix(r, u):
                    t, h = divmod(u, HEADS2)
                    slot = rows[u % GSLOTS]
                    dve.wait_ge(gathered[u % GSLOTS], r.at(16 * TOPK * UN // GSLOTS, 16 * TOPK * (u // GSLOTS + 1)))
                    s.did(dve.tensor_tensor(slot[:, :, :], slot[:, :, :], bc(weight[t % 2][:, h, :], 2, KV), ALU.mult))
                    s.wait()
                    s.did(dve.tensor_reduce(kv[r.par][:, t, :, h, :], slot[:, :, :].rearrange("p j (m c) -> p m c j", m=2), AX.X, ALU.add))
                    s.wait()
                    dve.sem_inc(S["rows_used"], 1)
                    if u == UN - 1:
                        dve.sem_inc(S["kv_ready"], 1)

                def causal_max(r, u):
                    w_ = (u // HEADS2 + 1) * P
                    dve.wait_ge(S["c_scores"], r.at(UN, u + 2 - UN))
                    dve.tensor_reduce(c_negmax[:, u:u + 1], ps_c[u % 2][:, 0:w_], AX.X, ALU.max, negate=True).then_inc(S["c_max"], 1)

                def causal_normalise(r, u):
                    t, h = divmod(u, HEADS2)
                    dve.wait_ge(S["o_ps"], r.at(OUSES, idx_values(u) + 1 - OUSES))
                    s.did(dve.reciprocal(c_inv[:, u:u + 1], c_sums[:, u:u + 1]))
                    s.wait()
                    dve.tensor_scalar(out[t % 2][:, h, :], ps_o[:, 0:D], c_inv[:, u:u + 1], None, ALU.mult).then_inc(S["o_used"], 1)

                def causal_tile(r, t):
                    if t == 0:
                        dve.wait_ge(S["c_in"], r.at(16, 0))
                        dve.wait_ge(S["y_stored"], r.at(16, 0))
                    dve.wait_ge(S["o_ps"], r.at(OUSES, idx_values(8 * t + 7) + 2 - OUSES))
                    dve.tensor_tensor(y[:, t, :], ps_o[:, 0:D], c_x[:, t, :], ALU.add).then_inc(S["o_used"], 1)
                    if t == TT - 1:
                        dve.wait_ge(S["o_used"], r.at(OUSES, 1))
                        dve.sem_inc(S["y_ready"], 1)
                        dve.sem_inc(S["c_used"], 1)

                def body(r):
                    if r.dia:
                        held(dve, S["d_in"], r.at(64, 128), dve_passed)
                    for j in range(UN + 2):
                        t, h = divmod(j, 8)
                        if r.dia and j < UN:
                            diagonal_unit(r, j)
                        if j < UN and r.chosen(t):
                            choose(r, t, h)
                        if r.cau and j < UN:
                            causal_max(r, j)
                        if r.cau and j >= 2:
                            causal_normalise(r, j - 2)
                        if r.mix and j < UN:
                            mix(r, j)
                        if r.cau and j >= 9 and h == 1:
                            causal_tile(r, t - 1)
                        if r.dia and j < UN and h == 7:
                            diagonal_tile(r, t)
                    s.restart()

                rounds(dve, body)

        clear_semaphores(nc, sems)


LAID = (["x"] + ["L0_tok_" + n for n in (
    "emb_byteT hash_rows Wq bq conv_w conv_b Win b_in Wg bg Wi bi WoT bo ln_g ln_b mlp_w mlp_bT Wout bout").split()]
        + ["L0_attn_" + n for n in "WqT bq WkT bk WvT bv WoT bo shift_logits alibi_slope".split()]
        + ["L0_ffn_" + n for n in "W1 b1 Wg bg Wd bd".split()]
        + ["L1_attn_" + n for n in "Wqkv_heads bqkv_heads W0_heads b0".split()]
        + ["L1_ffn_" + n for n in "Wq_pkT keysT Wq table Wo".split()])
def build(nc, a, out):
    outs = [nc.dram_tensor(f"h{n}", (NTOK, D), F32, kind="Internal").ap() for n in range(4)] + [out]
    tok = {k[7:]: v for k, v in a.items() if k.startswith("L0_tok_")}
    xpad = nc.dram_tensor("chars_padded", (B, WMAX + T), I32, kind="Internal").ap()
    pad_chars(nc, a["x"], xpad)
    tower_tok(nc, tok, a["x"], xpad, outs[0])
    shifted_attention(nc, {k[8:]: v for k, v in a.items() if k.startswith("L0_attn_")}, outs[0], outs[1])
    routed_ffn(nc, {k[7:]: v for k, v in a.items() if k.startswith("L0_ffn_")}, outs[1], outs[2])
    at1 = {k[8:]: v for k, v in a.items() if k.startswith("L1_attn_")}
    qkvT = nc.dram_tensor("qkvT", (PAIRS, P, ROWS3), F32, kind="Internal").ap()
    project_qkv(nc, at1, outs[2], qkvT)
    ff1 = {k[7:]: v for k, v in a.items() if k.startswith("L1_ffn_")}
    sequence_pipeline(nc, at1, ff1, qkvT, outs[2], outs[3], outs[4])


def kernel(**inputs):
    import numpy as np
    import concourse.bacc as bacc
    from concourse.bass_utils import run_bass_kernel_spmd

    laid = {k: np.asarray(v) for k, v in inputs.items()}
    t = {}
    t["L0_tok_emb_byteT"] = laid["L0_tok_emb_byte"].T
    t["L0_tok_WoT"] = laid["L0_tok_Wo"].T
    t["L0_tok_mlp_bT"] = laid["L0_tok_mlp_b"].T
    t["L0_tok_hash_rows"] = laid["L0_tok_hash_tables"].reshape(NW * HASH_MOD, E_TOK)
    for n in "qkvo":
        t[f"L0_attn_W{n}T"] = laid[f"L0_attn_W{n}"].T
    t["L1_attn_Wqkv_heads"] = laid["L1_attn_Wqkv"].reshape(D, 3, D, HEADS1).transpose(0, 1, 3, 2).reshape(D, -1)
    t["L1_attn_bqkv_heads"] = laid["L1_attn_bqkv"].reshape(3, D, HEADS1).transpose(0, 2, 1).reshape(-1)
    t["L1_attn_W0_heads"] = laid["L1_attn_W0"].reshape(D, HEADS1, D).transpose(1, 0, 2)
    t["L1_ffn_Wq_pkT"] = laid["L1_ffn_Wq_pk"].reshape(D, GROUPS, DKEY).transpose(2, 1, 0)
    t["L1_ffn_keysT"] = laid["L1_ffn_pk_keys"].transpose(3, 0, 2, 1).reshape(DKEY, GROUPS, NKEYS)
    t["L1_ffn_table"] = np.concatenate([laid["L1_ffn_keys_table"], laid["L1_ffn_values_table"]], axis=1)
    laid.update(t)
    nc = bacc.Bacc("TRN2", target_bir_lowering=False, num_devices=1)
    arrays, aps = {}, {}
    for name in LAID:
        v = np.ascontiguousarray(laid[name])
        arrays["in_" + name] = v
        aps[name] = nc.dram_tensor("in_" + name, v.shape, mybir.dt.from_np(v.dtype), kind="ExternalInput").ap()
    out = nc.dram_tensor("out_0", (NTOK, D), F32, kind="ExternalOutput").ap()
    build(nc, aps, out)
    r = run_bass_kernel_spmd(nc, [arrays], core_ids=[0]).results[0]
    return r["out_0"].reshape(B, T, D)
```

```python
from contextlib import ExitStack

import concourse.bass as bass
from concourse import mybir

F32 = mybir.dt.float32
BF16 = mybir.dt.bfloat16
I32 = mybir.dt.int32
U32 = mybir.dt.uint32
ALU = mybir.AluOpType
ACT = mybir.ActivationFunctionType
AX = mybir.AxisListType

P = 128
D = 64
B, T = 8, 512
NTOK = B * T
TT = T // P
EPS = 1e-5


class Steps:

    def __init__(self, eng, sem):
        self.eng, self.sem, self.n = eng, sem, 0

    def did(self, ins):
        ins.then_inc(self.sem, 1)
        self.n += 1
        return self.n

    def wait(self, n=None):
        self.eng.wait_ge(self.sem, self.n if n is None else n)

    def restart(self):
        self.wait()
        self.eng.sem_clear(self.sem)
        self.n = 0


def held(eng, sem, value, passed):
    eng.wait_ge(sem, value)
    eng.sem_inc(passed, 1)


def bc(ap, axis, n):
    a = ap.unsqueeze(axis)
    shape = list(a.shape)
    shape[axis] = n
    return a.broadcast_to(shape)


def ln_moments(dve, s, x, stats, moments):
    for t in range(TT):
        s.did(dve.bn_stats(stats[:, t, :], x[:, t, :]))
    s.wait()
    for t in range(TT):
        s.did(dve.bn_aggr(moments[:, t, :], stats[:, t, :]))
    s.wait()


def ln_apply(dve, s, xn, x, moments, std):
    s.did(dve.reciprocal(std[:, :], std[:, :]))
    s.wait()
    for t in range(TT):
        ins = dve.tensor_scalar(xn[:, t, :], x[:, t, :], moments[:, t, 0:1], std[:, t:t + 1], ALU.subtract, ALU.mult)
        if t < TT - 1:
            s.did(ins)
    return ins


def clear_semaphores(nc, sems):
    with nc.Block() as block:
        @block.sync
        def _(sp):
            for one in sems:
                sp.sem_clear(one)
E_TOK, H_TOK, S_TOK, KC, NM, NR = 64, 128, 32, 4, 4, 3
VOCAB, BASE, HASH_MOD = 64, 257, 1024
WINDOWS, MATCH_OFFSETS = (2, 4, 8, 16), (1, 2, 4, 8)
NW, WMAX, CHUNK = len(WINDOWS), 16, 32
NCH = T // CHUNK


def pad_chars(nc, x, xpad):
    with ExitStack() as ctx:
        fill = ctx.enter_context(nc.sbuf_tensor("pad_fill", [B, WMAX], I32))
        filled = ctx.enter_context(nc.semaphore("pad_filled"))
        written = ctx.enter_context(nc.semaphore("pad_written"))
        copied = ctx.enter_context(nc.semaphore("pad_copied"))
        with nc.Block() as block:
            @block.vector
            def _(dve):
                dve.memset(fill[:, :], -1).then_inc(filled, 1)

            @block.sync
            def _(sp):
                sp.dma_start(xpad[:, WMAX:WMAX + T], x).then_inc(copied, 16)
                sp.wait_ge(filled, 1)
                sp.dma_start(xpad[:, 0:WMAX], fill[:, :]).then_inc(written, 16)
                sp.wait_ge(copied, 16)
                sp.wait_ge(written, 16)

        clear_semaphores(nc, [filled, written, copied])


def tower_tok(nc, w, x, xpad, h_out):
    with ExitStack() as ctx:
        def sb(name, shape, dt=F32):
            return ctx.enter_context(nc.sbuf_tensor("tok_" + name, shape, dt))

        def ps(name, shape):
            return ctx.enter_context(nc.psum_tensor("tok_" + name, shape, F32))

        sems = []

        def sem(name):
            sems.append(ctx.enter_context(nc.semaphore("tok_" + name)))
            return sems[-1]

        embT = sb("embT", [E_TOK, VOCAB])
        wq = sb("wq", [E_TOK, E_TOK])
        bq = sb("bq", [1, E_TOK])
        conv_w = sb("conv_w", [E_TOK, KC])
        conv_b = sb("conv_b", [E_TOK, 1])
        win_byte = sb("win_byte", [E_TOK, H_TOK])
        win_hash = sb("win_hash", [E_TOK, H_TOK])
        win_match = sb("win_match", [NM, H_TOK])
        b_in = sb("b_in", [H_TOK, 1])
        wg = sb("wg", [H_TOK, S_TOK])
        bg = sb("bg", [S_TOK, 1])
        wi = sb("wi", [H_TOK, S_TOK])
        bi = sb("bi", [S_TOK, 1])
        woT = sb("woT", [H_TOK, S_TOK])
        bo = sb("bo", [H_TOK, 1])
        ln_g = sb("ln_g", [H_TOK, 1])
        ln_b = sb("ln_b", [H_TOK, 1])
        mlp_w = sb("mlp_w", [H_TOK, NR, H_TOK])
        mlp_b = sb("mlp_b", [H_TOK, NR])
        wout = sb("wout", [H_TOK, D])
        bout = sb("bout", [1, D])
        q_table = sb("q_table", [VOCAB, E_TOK])
        in_table = sb("in_table", [VOCAB, H_TOK])
        wo_centred = sb("wo_centred", [S_TOK, H_TOK])
        bo_centred = sb("bo_centred", [H_TOK, 1])
        ident = sb("ident", [P, P])
        centre = sb("centre", [P, P])
        mean_all = sb("mean_all", [P, P])
        ones_row = sb("ones_row", [1, P])
        eps = sb("eps", [P, 1])
        vocab_id_i = sb("vocab_id_i", [VOCAB, 1], I32)
        vocab_id = sb("vocab_id", [VOCAB, 1])
        in_chunk = sb("in_chunk", [S_TOK, T])
        chunk_start = sb("chunk_start", [S_TOK, T])
        powers = sb("powers", [P, WMAX])
        table_base = sb("table_base", [P, NW], I32)
        windows = sb("windows", [P, B * TT, WMAX], I32)
        windows_f = sb("windows_f", [P, B * TT, WMAX])
        hash_sum = sb("hash_sum", [P, B * TT, NW])
        hash_idx = sb("hash_idx", [P, (B + 2) * TT, NW], I32)
        loaded, gp_made, dve_made, pe_made = sem("loaded"), sem("gp_made"), sem("dve_made"), sem("pe_made")
        windows_loaded = sem("windows_loaded")
        psw = ps("psw", [P, 512])
        WEIGHTS = [(embT, w["emb_byteT"]), (wq, w["Wq"]), (bq, w["bq"].unsqueeze(0)),
                   (conv_w, w["conv_w"].rearrange("c a k -> c (a k)")), (conv_b, w["conv_b"].unsqueeze(1)),
                   (win_byte, w["Win"][0:E_TOK, :]), (win_hash, w["Win"][E_TOK:2 * E_TOK, :]),
                   (win_match, w["Win"][2 * E_TOK:2 * E_TOK + NM, :]), (b_in, w["b_in"].unsqueeze(1)),
                   (wg, w["Wg"]), (bg, w["bg"].unsqueeze(1)), (wi, w["Wi"]), (bi, w["bi"].unsqueeze(1)),
                   (woT, w["WoT"]), (bo, w["bo"].unsqueeze(1)), (ln_g, w["ln_g"].unsqueeze(1)),
                   (ln_b, w["ln_b"].unsqueeze(1)), (wout, w["Wout"]), (bout, w["bout"].unsqueeze(0)),
                   (mlp_b, w["mlp_bT"])]

        with nc.Block() as block:
            @block.sync
            def _(sp):
                for b in range(B):
                    src = bass.AP(xpad.tensor, xpad.offset + b * (WMAX + T) + 1, [[1, P], [P, TT], [1, WMAX]])
                    sp.dma_start(windows[:, b * TT:(b + 1) * TT, :], src).then_inc(windows_loaded, 16)
                for dst, src in WEIGHTS:
                    sp.dma_start(dst[:, :], src).then_inc(loaded, 16)
                sp.dma_start(mlp_w[:, :, :], w["mlp_w"].rearrange("l i o -> i l o")).then_inc(loaded, 16)

            @block.gpsimd
            def _(pool):
                pool.iota(vocab_id_i[:, :], [[0, 1]], base=0, channel_multiplier=1).then_inc(gp_made, 1)
                pool.iota(table_base[:, :], [[HASH_MOD, NW]], base=0, channel_multiplier=0).then_inc(gp_made, 1)
                pool.memset(ident[:, :], 0.0).then_inc(gp_made, 1)
                pool.wait_ge(gp_made, 3)
                pool.affine_select(out=ident[:, :], in_=ident[:, :], compare_op=ALU.not_equal, fill=1.0, base=0,
                                   pattern=[[-1, P]], channel_multiplier=1).then_inc(gp_made, 1)

            @block.vector
            def _(dve):
                s = Steps(dve, dve_made)
                s.did(dve.memset(mean_all[:, :], 1.0 / H_TOK))
                s.did(dve.memset(ones_row[:, :], 1.0))
                s.did(dve.memset(eps[:, :], EPS))
                s.did(dve.memset(in_chunk[:, :], 1.0))
                s.did(dve.memset(chunk_start[:, :], 0.0))
                power = 1
                for j in range(WMAX):
                    s.did(dve.memset(powers[:, WMAX - 1 - j:WMAX - j], float(power)))
                    power = power * BASE % HASH_MOD
                s.wait()
                s.did(dve.memset(in_chunk[:, 0:T:CHUNK], 0.0))
                s.did(dve.memset(chunk_start[:, 0:T:CHUNK], 1.0))
                dve.wait_ge(gp_made, 4)
                s.did(dve.tensor_copy(vocab_id[:, :], vocab_id_i[:, :]))
                s.did(dve.tensor_tensor(centre[:, :], ident[:, :], mean_all[:, :], ALU.subtract))
                dve.wait_ge(windows_loaded, 16 * B)
                s.did(dve.tensor_scalar(windows_f[:, :, :], windows[:, :, :], 0.0, None, ALU.max))
                s.wait()
                s.did(dve.tensor_tensor(windows_f[:, :, :], windows_f[:, :, :], bc(powers[:, :], 1, B * TT), ALU.mult))
                s.wait()
                for n, width in enumerate(WINDOWS):
                    s.did(dve.tensor_reduce(hash_sum[:, :, n], windows_f[:, :, WMAX - width:WMAX], AX.X, ALU.add))
                s.wait()
                hashes = hash_idx[:, 0:B * TT, :]
                s.did(dve.memset(hash_idx[:, B * TT:, :], 0))
                s.did(dve.tensor_copy(hashes, hash_sum[:, :, :]))
                s.wait()
                s.did(dve.tensor_scalar(hashes, hashes, HASH_MOD - 1, None, ALU.bitwise_and))
                s.wait()
                s.did(dve.tensor_tensor(hashes, hashes, bc(table_base[:, :], 1, B * TT), ALU.add))
                dve.wait_ge(pe_made, 1)
                s.did(dve.tensor_copy(q_table[:, :], psw[0:VOCAB, 0:E_TOK]))
                s.did(dve.tensor_copy(in_table[:, :], psw[0:VOCAB, 64:192]))
                s.did(dve.tensor_copy(wo_centred[:, :], psw[0:S_TOK, 192:320]))
                s.did(dve.tensor_copy(bo_centred[:, :], psw[:, 320:321]))
                s.wait()

            @block.tensor
            def _(pe):
                pe.wait_ge(loaded, 16 * (len(WEIGHTS) + 1))
                pe.wait_ge(dve_made, 5 + WMAX + 4)
                pe.matmul(psw[0:VOCAB, 0:E_TOK], embT[:, :], wq[:, :], start=True, stop=False)
                pe.matmul(psw[0:VOCAB, 0:E_TOK], ones_row[:, 0:VOCAB], bq[:, :], start=False, stop=True)
                pe.matmul(psw[0:VOCAB, 64:192], embT[:, :], win_byte[:, :], start=True, stop=True)
                pe.matmul(psw[0:S_TOK, 192:320], woT[:, :], centre[:, :], start=True, stop=True)
                pe.matmul(psw[:, 320:321], centre[:, :], bo[:, :], start=True, stop=True).then_inc(pe_made, 1)

        R = range(2)
        chars = sb("chars", [VOCAB, 2, T], I32)
        shifted = sb("shifted", [NM, 2, T], I32)
        own = sb("own", [NM, 2, T], I32)
        idx_now = sb("idx_now", [P, 2, TT * NW], I32)
        rows = [sb(f"rows{b}", [P, TT, NW, E_TOK]) for b in R]
        onehot = [sb(f"onehot{b}", [VOCAB, T]) for b in R]
        match = [sb(f"match{b}", [NM, T]) for b in R]
        prod = [sb(f"prod{b}", [P, TT, NW, E_TOK]) for b in R]
        score = [sb(f"score{b}", [P, TT, NW]) for b in R]
        score_e = [sb(f"score_e{b}", [P, TT, NW]) for b in R]
        smax = [sb(f"smax{b}", [P, TT]) for b in R]
        ssum = [sb(f"ssum{b}", [P, TT]) for b in R]
        feat = [sb(f"feat{b}", [P, TT, E_TOK]) for b in R]
        featT = [sb(f"featT{b}", [E_TOK, KC - 1 + T]) for b in R]
        conv = [[sb(f"conv{b}_{k}", [E_TOK, T]) for k in R] for b in R]
        hash_act = [sb(f"hash_act{b}", [E_TOK, T]) for b in R]
        h1 = [sb(f"h1_{b}", [H_TOK, T]) for b in R]
        gate = [sb(f"gate{b}", [S_TOK, T]) for b in R]
        one_minus = [sb(f"one_minus{b}", [S_TOK, T]) for b in R]
        drive = [sb(f"drive{b}", [S_TOK, T]) for b in R]
        gate_in = [sb(f"gate_in{b}", [S_TOK, T]) for b in R]
        gate_start = [sb(f"gate_start{b}", [S_TOK, T]) for b in R]
        cum_a = [sb(f"cum_a{b}", [S_TOK, T]) for b in R]
        cum_wb = [sb(f"cum_wb{b}", [S_TOK, T]) for b in R]
        carry = [sb(f"carry{b}", [S_TOK, 1 + NCH]) for b in R]
        states = [sb(f"states{b}", [S_TOK, T]) for b in R]
        cen = [sb(f"cen{b}", [H_TOK, T]) for b in R]
        sq = [sb(f"sq{b}", [H_TOK, T]) for b in R]
        hid = [sb(f"hid{b}", [H_TOK, T]) for b in R]
        hid_act = [sb(f"hid_act{b}", [H_TOK, T]) for b in R]
        h_tok = [sb(f"h_tok{b}", [P, TT, D]) for b in R]
        ps_q = [ps(f"ps_q{b}", [P, TT, E_TOK]) for b in R]
        ps_h = [ps(f"ps_h{b}", [P, 512]) for b in R]
        ps_s = [ps(f"ps_s{b}", [P, 512]) for b in R]

        chars_in = [sem(f"chars_in{b}") for b in R]
        rows_in = [nc.alloc_semaphore(f"tok_rows_in{b}") for b in R]
        stored = [sem(f"stored{b}") for b in R]
        names = ("idx_ready chars_used rows_used q_ready scores_centred exps_ready feat_ready featT_ready conv_ready "
                 "hash_ready onehot_ready in_ready h1_ready gates_ready gates_act states_ready "
                 "centred_ready squares_ready var_ready std_ready hid_ready mlp_lin mlp_ready mlp_act out_ready h_ready")
        S = {n: sem(n) for n in names.split()}
        dve_steps, pool_passed, pe_passed = sem("dve_steps"), sem("pool_passed"), sem("pe_passed")

        with nc.Block() as block:
            @block.sync
            def _(sp):
                sp.sem_inc(S["chars_used"], 2)
                for b in R:
                    sp.sem_inc(stored[b], 16)

                def load(i):
                    for b in R:
                        sp.wait_ge(S["chars_used"], 2 * i + b + 1)
                        row = 2 * i + b
                        seq = x[bass.ds(row, 1), :]
                        sp.dma_start(chars[:, b, :], seq.partition_broadcast(VOCAB).rearrange("p a t -> p (a t)")).then_inc(chars_in[b], 16)
                        sp.dma_start(own[:, b, :], seq.partition_broadcast(NM).rearrange("p a t -> p (a t)")).then_inc(chars_in[b], 16)
                        for n, k in enumerate(MATCH_OFFSETS):
                            sp.dma_start(shifted[n:n + 1, b, :], xpad[bass.ds(row, 1), WMAX - k:WMAX - k + T]).then_inc(chars_in[b], 16)

                def store(i):
                    for b in R:
                        sp.wait_ge(S["h_ready"], 2 * i + b + 1)
                        dst = h_out[bass.ds((2 * i + b) * T, T), :].rearrange("(t p) d -> p t d", p=P)
                        sp.dma_start(dst, h_tok[b][:, :, :]).then_inc(stored[b], 16)

                load(0)
                with sp.Fori(0, B // 2 - 1) as i:
                    load(i + 1)
                    store(i)
                store(B // 2 - 1)
                for b in R:
                    sp.wait_ge(stored[b], 16 * (B // 2 + 1))

            @block.gpsimd
            def _(pool):
                pool.sem_inc(S["rows_used"], 2)
                with pool.Fori(0, B // 2) as i:
                    for b in R:
                        pool.wait_ge(S["rows_used"], 2 * i + b + 1)
                        held(pool, S["idx_ready"], 2 * i + b + 1, pool_passed)
                        for t in range(TT):
                            for n in range(NW):
                                pool.indirect_dma_start(
                                    rows[b][:, t, n, :], None, w["hash_rows"],
                                    bass.IndirectOffsetOnAxis(idx_now[:, b, t * NW + n:t * NW + n + 1], 0),
                                ).then_inc(rows_in[b], 16)

            @block.vector
            def _(dve):
                s = Steps(dve, dve_steps)
                for b in R:
                    s.did(dve.memset(featT[b][:, 0:KC - 1], 0.0))
                    s.did(dve.memset(carry[b][:, 0:1], 0.0))
                s.wait()

                def indices(i, b):
                    dve.tensor_copy(idx_now[:, b, :], hash_idx[:, bass.ds((2 * i + b) * TT, TT), :].rearrange("p t n -> p (t n)")).then_inc(S["idx_ready"], 1)

                for b in R:
                    indices(0, b)
                with dve.Fori(0, B // 2) as i:
                    n = [2 * i + 1, 2 * i + 2]
                    s.restart()
                    mark = [0, 0]
                    for b in R:
                        dve.wait_ge(chars_in[b], 16 * 6 * (i + 1))
                        dve.tensor_scalar(onehot[b][:, :], chars[:, b, :], vocab_id[:, 0:1], None, ALU.is_equal).then_inc(S["onehot_ready"], 1)
                        s.did(dve.tensor_tensor(match[b][:, :], shifted[:, b, :], own[:, b, :], ALU.is_equal))
                        s.wait()
                        dve.sem_inc(S["chars_used"], 1)
                    for b in R:
                        dve.wait_ge(S["q_ready"], n[b])
                        dve.wait_ge(rows_in[b], 16 * TT * NW * (i + 1))
                        s.did(dve.tensor_tensor(prod[b][:, :, :, :], rows[b][:, :, :, :], bc(ps_q[b][:, :, :], 2, NW), ALU.mult))
                        s.wait()
                        s.did(dve.tensor_reduce(score[b][:, :, :], prod[b][:, :, :, :], AX.X, ALU.add))
                        s.wait()
                        s.did(dve.tensor_reduce(smax[b][:, :], score[b][:, :, :], AX.X, ALU.max))
                        s.wait()
                        dve.tensor_tensor(score[b][:, :, :], score[b][:, :, :], bc(smax[b][:, :], 2, NW), ALU.subtract).then_inc(S["scores_centred"], 1)
                    for b in R:
                        dve.wait_ge(S["exps_ready"], n[b])
                        s.did(dve.tensor_reduce(ssum[b][:, :], score_e[b][:, :, :], AX.X, ALU.add))
                        s.wait()
                        s.did(dve.reciprocal(ssum[b][:, :], ssum[b][:, :]))
                        s.wait()
                        s.did(dve.tensor_tensor(score_e[b][:, :, :], score_e[b][:, :, :], bc(ssum[b][:, :], 2, NW), ALU.mult))
                        s.wait()
                        s.did(dve.tensor_tensor(prod[b][:, :, :, :], rows[b][:, :, :, :], bc(score_e[b][:, :, :], 3, E_TOK), ALU.mult))
                        s.wait()
                        indices(i + 1, b)
                        dve.sem_inc(S["rows_used"], 1)
                        dve.tensor_reduce(feat[b][:, :, :], prod[b][:, :, :, :].rearrange("p t s e -> p t e s"), AX.X, ALU.add).then_inc(S["feat_ready"], 1)
                    for b in R:
                        dve.wait_ge(S["featT_ready"], n[b])
                        s.did(dve.tensor_copy(featT[b][:, KC - 1:], ps_s[b][0:E_TOK, :]))
                        s.wait()
                        s.did(dve.tensor_scalar(conv[b][0][:, :], featT[b][:, 0:T], conv_w[:, 0:1], None, ALU.mult))
                        for k in range(1, KC):
                            s.wait()
                            ins = dve.scalar_tensor_tensor(conv[b][k % 2][:, :], featT[b][:, k:k + T], conv_w[:, k:k + 1], conv[b][(k + 1) % 2][:, :], ALU.mult, ALU.add)
                            if k < KC - 1:
                                s.did(ins)
                        ins.then_inc(S["conv_ready"], 1)
                    for b in R:
                        dve.wait_ge(S["gates_act"], n[b])
                        s.did(dve.tensor_scalar(one_minus[b][:, :], gate[b][:, :], -1.0, 1.0, ALU.mult, ALU.add))
                        s.did(dve.tensor_scalar(gate[b][:, :], gate[b][:, :], 1e-6, None, ALU.max))
                        s.wait()
                        s.did(dve.tensor_tensor(drive[b][:, :], drive[b][:, :], one_minus[b][:, :], ALU.mult))
                        s.did(dve.tensor_tensor(gate_in[b][:, :], gate[b][:, :], in_chunk[:, :], ALU.mult))
                        s.did(dve.tensor_tensor(gate_start[b][:, :], gate[b][:, :], chunk_start[:, :], ALU.mult))
                        s.wait()
                        s.did(dve.tensor_tensor_scan(cum_a[b][:, :], gate_in[b][:, :], gate_start[b][:, :], 0.0, ALU.mult, ALU.add))
                        s.wait()
                        s.did(dve.tensor_scalar(gate_in[b][:, :], cum_a[b][:, :], 1e-8, None, ALU.max))
                        s.wait()
                        s.did(dve.reciprocal(gate_in[b][:, :], gate_in[b][:, :]))
                        s.wait()
                        s.did(dve.tensor_tensor(drive[b][:, :], drive[b][:, :], gate_in[b][:, :], ALU.mult))
                        s.wait()
                        s.did(dve.tensor_tensor_scan(cum_wb[b][:, :], in_chunk[:, :], drive[b][:, :], 0.0, ALU.mult, ALU.add))
                        s.wait()
                        s.did(dve.tensor_tensor_scan(carry[b][:, 1:], cum_wb[b][:, CHUNK - 1:T:CHUNK], cum_a[b][:, CHUNK - 1:T:CHUNK], 0.0, ALU.add, ALU.mult))
                        s.wait()
                        s.did(dve.tensor_tensor(cum_wb[b][:, :].rearrange("p (c k) -> p c k", k=CHUNK), cum_wb[b][:, :].rearrange("p (c k) -> p c k", k=CHUNK), bc(carry[b][:, 0:NCH], 2, CHUNK), ALU.add))
                        s.wait()
                        dve.tensor_tensor(states[b][:, :], cum_wb[b][:, :], cum_a[b][:, :], ALU.mult).then_inc(S["states_ready"], 1)
                    for b in R:
                        dve.wait_ge(S["std_ready"], n[b])
                        s.did(dve.reciprocal(sq[b][:, :], sq[b][:, :]))
                        s.wait()
                        s.did(dve.tensor_tensor(cen[b][:, :], cen[b][:, :], sq[b][:, :], ALU.mult))
                        s.wait()
                        dve.tensor_scalar(hid[b][:, :], cen[b][:, :], ln_g[:, 0:1], ln_b[:, 0:1], ALU.mult, ALU.add).then_inc(S["hid_ready"], 1)
                    for l in range(NR):
                        for b in R:
                            dve.wait_ge(S["mlp_act"], 2 * NR * i + 2 * l + b + 1)
                            dve.tensor_tensor(hid[b][:, :], hid[b][:, :], hid_act[b][:, :], ALU.add).then_inc(S["mlp_ready"], 1)
                    for b in R:
                        dve.wait_ge(stored[b], 16 * i + 16)
                        dve.wait_ge(S["out_ready"], n[b])
                        s.did(dve.tensor_copy(h_tok[b][:, :, :], ps_q[b][:, :, :]))
                        s.wait()
                        dve.sem_inc(S["h_ready"], 1)
                s.wait()

            @block.scalar
            def _(act):
                with act.Fori(0, B // 2) as i:
                    n = [2 * i + 1, 2 * i + 2]
                    for b in R:
                        act.wait_ge(S["scores_centred"], n[b])
                        act.activation(score_e[b][:, :, :], score[b][:, :, :], ACT.Exp, scale=float(E_TOK) ** -0.5).then_inc(S["exps_ready"], 1)
                    for b in R:
                        act.wait_ge(S["conv_ready"], n[b])
                        act.activation(hash_act[b][:, :], conv[b][(KC - 1) % 2][:, :], ACT.Silu, bias=conv_b[:, 0:1]).then_inc(S["hash_ready"], 1)
                    for b in R:
                        act.wait_ge(S["in_ready"], n[b])
                        act.activation(h1[b][:, :], ps_h[b][:, :], ACT.Silu, bias=b_in[:, 0:1]).then_inc(S["h1_ready"], 1)
                    for b in R:
                        act.wait_ge(S["gates_ready"], n[b])
                        act.activation(drive[b][:, :], ps_h[b][0:S_TOK, :], ACT.Identity, bias=bi[:, 0:1])
                        act.activation(gate[b][:, :], ps_s[b][0:S_TOK, :], ACT.Sigmoid, bias=bg[:, 0:1]).then_inc(S["gates_act"], 1)
                    for b in R:
                        act.wait_ge(S["centred_ready"], n[b])
                        act.activation(cen[b][:, :], ps_h[b][:, :], ACT.Identity, bias=bo_centred[:, 0:1])
                        act.activation(sq[b][:, :], ps_h[b][:, :], ACT.Square, bias=bo_centred[:, 0:1]).then_inc(S["squares_ready"], 1)
                    for b in R:
                        act.wait_ge(S["var_ready"], n[b])
                        act.activation(sq[b][:, :], ps_s[b][:, :], ACT.Sqrt, bias=eps[:, 0:1]).then_inc(S["std_ready"], 1)
                    for l in range(NR):
                        for b in R:
                            act.wait_ge(S["mlp_lin"], 2 * NR * i + 2 * l + b + 1)
                            act.activation(hid_act[b][:, :], ps_h[b][:, :], ACT.Silu, bias=mlp_b[:, l:l + 1]).then_inc(S["mlp_act"], 1)

            @block.tensor
            def _(pe):
                with pe.Fori(0, B // 2) as i:
                    n = [2 * i + 1, 2 * i + 2]
                    for b in R:
                        pe.wait_ge(S["onehot_ready"], n[b])
                        for t in range(TT):
                            mm = pe.matmul(ps_q[b][:, t, :], onehot[b][:, t * P:(t + 1) * P], q_table[:, :], start=True, stop=True)
                        mm.then_inc(S["q_ready"], 1)
                    for b in R:
                        held(pe, S["feat_ready"], n[b], pe_passed)
                        for t in range(TT):
                            mm = pe.transpose(ps_s[b][0:E_TOK, t * P:(t + 1) * P], feat[b][:, t, :], ident[:, :])
                        mm.then_inc(S["featT_ready"], 1)
                    for b in R:
                        pe.wait_ge(S["hash_ready"], n[b])
                        pe.matmul(ps_h[b][:, :], in_table[:, :], onehot[b][:, :], start=True, stop=False)
                        pe.matmul(ps_h[b][:, :], win_match[:, :], match[b][:, :], start=False, stop=False)
                        pe.matmul(ps_h[b][:, :], win_hash[:, :], hash_act[b][:, :], start=False, stop=True).then_inc(S["in_ready"], 1)
                    for b in R:
                        pe.wait_ge(S["h1_ready"], n[b])
                        pe.matmul(ps_s[b][0:S_TOK, :], wg[:, :], h1[b][:, :], start=True, stop=True)
                        pe.matmul(ps_h[b][0:S_TOK, :], wi[:, :], h1[b][:, :], start=True, stop=True).then_inc(S["gates_ready"], 1)
                    for b in R:
                        pe.wait_ge(S["states_ready"], n[b])
                        pe.matmul(ps_h[b][:, :], centre[:, :], h1[b][:, :], start=True, stop=False)
                        pe.matmul(ps_h[b][:, :], wo_centred[:, :], states[b][:, :], start=False, stop=True).then_inc(S["centred_ready"], 1)
                    for b in R:
                        pe.wait_ge(S["squares_ready"], n[b])
                        pe.matmul(ps_s[b][:, :], mean_all[:, :], sq[b][:, :], start=True, stop=True).then_inc(S["var_ready"], 1)
                    for l in range(NR):
                        for b in R:
                            if l == 0:
                                pe.wait_ge(S["hid_ready"], n[b])
                            else:
                                pe.wait_ge(S["mlp_ready"], 2 * NR * i + 2 * (l - 1) + b + 1)
                            pe.matmul(ps_h[b][:, :], mlp_w[:, l, :], hid[b][:, :], start=True, stop=True).then_inc(S["mlp_lin"], 1)
                    for b in R:
                        pe.wait_ge(S["mlp_ready"], 2 * NR * i + 2 * (NR - 1) + b + 1)
                        for t in range(TT):
                            pe.matmul(ps_q[b][:, t, :], hid[b][:, t * P:(t + 1) * P], wout[:, :], start=True, stop=False)
                            mm = pe.matmul(ps_q[b][:, t, :], ones_row[:, :], bout[:, :], start=False, stop=True)
                        mm.then_inc(S["out_ready"], 1)

        clear_semaphores(nc, sems)


HEADS0, DH0 = 4, 16
SHIFTS = (0, 4, 8, 12)
NSH, PAD0, WINDOW = len(SHIFTS), max(SHIFTS), 64
FB = 2 * T - P
UNITS = TT * HEADS0
HIGH, MIDDLE, LOWER = range(3)
QPARTS = (HIGH, HIGH, HIGH, MIDDLE, MIDDLE, LOWER)
KPARTS = (HIGH, MIDDLE, LOWER, HIGH, MIDDLE, HIGH)
STACK = len(QPARTS) * DH0


def shifted_attention(nc, w, h_in, h_out):
    with ExitStack() as ctx:
        def sb(name, shape, dt=F32):
            return ctx.enter_context(nc.sbuf_tensor("at0_" + name, shape, dt))

        def ps(name, shape):
            return ctx.enter_context(nc.psum_tensor("at0_" + name, shape, F32))

        sems = []

        def sem(name):
            sems.append(ctx.enter_context(nc.semaphore("at0_" + name)))
            return sems[-1]

        wq_once, wk_once = (sb(f"w{n}_once", [D + 1, D]) for n in "qk")
        wq = sb("wq", [D + 1, HEADS0, len(QPARTS), DH0])
        wk = sb("wk", [D + 1, HEADS0, len(QPARTS), DH0])
        less_high = [sb(f"less_high{m}", [STACK, 1]) for m in range(2)]
        less_middle = [sb(f"less_middle{m}", [STACK, 1]) for m in range(2)]
        wv = sb("wv", [D + 1, D])
        wo = sb("wo", [D + 1, D])
        logits = sb("logits", [P, HEADS0, NSH])
        lmax = sb("lmax", [P, HEADS0])
        log_pi = sb("log_pi", [P, HEADS0, NSH])
        slope = sb("slope", [P, HEADS0])
        tiny = sb("tiny", [P, 1])
        eps = sb("eps", [P, 1])
        ident = sb("ident", [P, P])
        dist_i = sb("dist_i", [P, FB], I32)
        dist = sb("dist", [P, FB])
        mask = sb("mask", [P, FB])
        alibi = [sb(f"alibi{k}", [P, FB]) for k in range(2)]
        bias = sb("bias", [P, HEADS0, NSH, FB])
        loaded, gp_made, dve_made, act_made = sem("loaded"), sem("gp_made"), sem("dve_made"), sem("act_made")

        x = sb("x", [P, TT, D])
        xn = sb("xn", [P, TT, D])
        stats = sb("stats", [P, TT, 6])
        moments = sb("moments", [P, TT, 2])
        std = sb("std", [P, TT])
        xnT = sb("xnT", [D + 1, T])
        qS = [[sb(f"qS{b}_{h}", [STACK, T], BF16) for h in range(HEADS0)] for b in range(2)]
        kS = [[sb(f"kS{b}_{h}", [STACK, PAD0 + T], BF16) for h in range(HEADS0)] for b in range(2)]
        high = [sb(f"high{k}", [STACK, T], BF16) for k in range(2)]
        middle = [sb(f"middle{k}", [STACK, T], BF16) for k in range(2)]
        rest = [sb(f"rest{k}", [STACK, T]) for k in range(2)]
        vT = sb("vT", [D, PAD0 + T])
        vsumT = [sb(f"vsumT{k}", [D, T]) for k in range(2)]
        vsum = [sb(f"vsum{b}", [P, TT, D]) for b in range(2)]
        att = [sb(f"att{k}", [P, NSH, T]) for k in range(2)]
        prob = [sb(f"prob{k}", [P, NSH, T]) for k in range(2)]
        psum_p = [sb(f"psum_p{k}", [P, NSH // 2, T]) for k in range(3)]
        probT = [sb(f"probT{k}", [P, TT, P]) for k in range(2)]
        rowmax = [sb(f"rowmax{k}", [P, NSH // 2]) for k in range(2)]
        negmax = [sb(f"negmax{k}", [P, 1]) for k in range(2)]
        total = [sb(f"total{k}", [P, 1]) for k in range(6)]
        inv = [sb(f"inv{k}", [P, 1]) for k in range(6)]
        context = sb("context", [P, TT, D])
        contextT = sb("contextT", [D + 1, T])
        y = [sb(f"y{b}", [P, TT, D]) for b in range(2)]
        ps_att = [ps(f"ps_att{s}", [P, 2, T]) for s in range(NSH // 2)]
        ps_T = ps("ps_T", [P, T])
        ps_pT = ps("ps_pT", [P, T])
        ps_c = ps("ps_c", [P, T])
        ps_v = ps("ps_v", [P, T])

        x_in, x_used, stored = sem("x_in"), sem("x_used"), sem("stored")
        names = ("moments_ready std_ready xn_ready T_ps T_used high_ready middle_ready parts_ready vsum_made "
                 "scores_ready scores_used max_ready probs_ready summed pT_ps pT_ready "
                 "ctx_ps context_part context_ready y_ps y_ready")
        S = {n: sem(n) for n in names.split()}
        dve_steps, gp_steps = sem("dve_steps"), sem("gp_steps")
        dve_passed, pe_passed, sp_passed = sem("dve_passed"), sem("pe_passed"), sem("sp_passed")

        LOADS = 16 * 10

        with nc.Block() as block:
            @block.sync
            def _(sp):
                sp.dma_start(logits[:, :, :], w["shift_logits"].partition_broadcast(P)).then_inc(loaded, 16)
                sp.dma_start(slope[:, :], w["alibi_slope"].partition_broadcast(P)).then_inc(loaded, 16)
                for dst, name in ((wq_once, "q"), (wk_once, "k"), (wv, "v"), (wo, "o")):
                    sp.dma_start(dst[0:D, :], w[f"W{name}T"]).then_inc(loaded, 16)
                    sp.dma_start(dst[D:D + 1, :], w[f"b{name}"].unsqueeze(0)).then_inc(loaded, 16)
                sp.wait_ge(loaded, LOADS)

            @block.gpsimd
            def _(pool):
                pool.iota(dist_i[:, :], [[1, FB]], base=P - T, channel_multiplier=-1).then_inc(gp_made, 1)
                pool.memset(ident[:, :], 0.0).then_inc(gp_made, 1)
                pool.wait_ge(gp_made, 2)
                pool.affine_select(out=ident[:, :], in_=ident[:, :], compare_op=ALU.not_equal, fill=1.0, base=0,
                                   pattern=[[-1, P]], channel_multiplier=1).then_inc(gp_made, 1)
                count = 3
                for parts, high_sign, middle_sign in ((QPARTS, less_high[0], less_middle[0]), (KPARTS, less_high[1], less_middle[1])):
                    for tile, least in ((high_sign, MIDDLE), (middle_sign, LOWER)):
                        pool.memset(tile[:, :], 0.0).then_inc(gp_made, 1)
                        count += 1
                        for n, part in enumerate(parts):
                            if part >= least:
                                for first, sign in ((n * DH0, -1.0), ((n + 1) * DH0, 0.0)):
                                    pool.wait_ge(gp_made, count)
                                    if first < STACK:
                                        pool.affine_select(out=tile[:, :], in_=tile[:, :], compare_op=ALU.is_gt, fill=sign, base=first,
                                                           pattern=[[0, 1]], channel_multiplier=-1).then_inc(gp_made, 1)
                                        count += 1

            @block.scalar
            def _(act):
                act.wait_ge(dve_made, 1)
                act.activation(log_pi[:, :, :], logits[:, :, :], ACT.Exp).then_inc(act_made, 1)
                act.wait_ge(dve_made, 2)
                act.activation(log_pi[:, :, :], logits[:, :, :], ACT.Ln, bias=tiny[:, 0:1]).then_inc(act_made, 1)

            @block.vector
            def _(dve):
                s = Steps(dve, dve_steps)
                s.did(dve.memset(tiny[:, :], 1e-8))
                s.did(dve.memset(eps[:, :], EPS))
                for b in range(2):
                    for h in range(HEADS0):
                        s.did(dve.memset(kS[b][h][:, 0:PAD0], 0.0))
                s.did(dve.memset(vT[:, 0:PAD0], 0.0))
                s.did(dve.memset(xnT[D:D + 1, :], 1.0))
                s.did(dve.memset(contextT[D:D + 1, :], 1.0))
                dve.wait_ge(gp_made, 3)
                s.did(dve.tensor_copy(dist[:, :], dist_i[:, :]))
                s.wait()
                s.did(dve.tensor_scalar(mask[:, :], dist[:, :], float(WINDOW), 10000.0, ALU.is_lt, ALU.mult))
                s.wait()
                s.did(dve.scalar_tensor_tensor(mask[:, :], dist[:, :], 0.0, mask[:, :], ALU.is_ge, ALU.mult))
                s.wait()
                s.did(dve.tensor_scalar(mask[:, :], mask[:, :], -10000.0, None, ALU.add))
                s.did(dve.tensor_scalar(dist[:, :], dist[:, :], 0.0, None, ALU.max))
                dve.wait_ge(loaded, LOADS)
                s.did(dve.tensor_scalar(slope[:, :], slope[:, :], -1.0, None, ALU.mult))
                for h in range(HEADS0):
                    for dst, src, scale in ((wq, wq_once, float(DH0) ** -0.5), (wk, wk_once, 1.0)):
                        s.did(dve.tensor_scalar(dst[:, h, :, :], bc(src[:, h * DH0:(h + 1) * DH0], 1, len(QPARTS)), scale, None, ALU.mult))
                s.wait()
                s.did(dve.tensor_reduce(lmax[:, :], logits[:, :, :], AX.X, ALU.max))
                s.wait()
                dve.tensor_tensor(logits[:, :, :], logits[:, :, :], bc(lmax[:, :], 2, NSH), ALU.subtract).then_inc(dve_made, 1)
                dve.wait_ge(act_made, 1)
                s.did(dve.tensor_reduce(lmax[:, :], log_pi[:, :, :], AX.X, ALU.add))
                s.wait()
                s.did(dve.reciprocal(lmax[:, :], lmax[:, :]))
                s.wait()
                dve.tensor_tensor(logits[:, :, :], log_pi[:, :, :], bc(lmax[:, :], 2, NSH), ALU.mult).then_inc(dve_made, 1)
                dve.wait_ge(act_made, 2)
                for h in range(HEADS0):
                    s.did(dve.scalar_tensor_tensor(alibi[h % 2][:, :], dist[:, :], slope[:, h:h + 1], mask[:, :], ALU.mult, ALU.add))
                    s.wait()
                    for j in range(NSH):
                        s.did(dve.tensor_scalar(bias[:, h, j, :], alibi[h % 2][:, :], log_pi[:, h, j:j + 1], None, ALU.add))
                s.wait()

        TRANSPOSE, VALUE, PART, SUM = 0, 1, 2, 2 + 2 * HEADS0
        ITEMS = SUM + 1

        def use(k, n):
            return n if isinstance(k, int) and k == 0 else k * (ITEMS + 1) + (n - 1)

        def context_use(i):
            if isinstance(i, int) and i == B - 1:
                return i * (ITEMS + 1) + ITEMS
            return i * (ITEMS + 1) + 2 * ITEMS

        FIRST = 3

        def sequences(eng, prepare, body):
            prepare(0, 0)
            with eng.Fori(0, B // 2 - 1) as q:
                body(2 * q, 0, True)
                body(2 * q + 1, 1, True)
            body(B - 2, 0, True)
            body(B - 1, 1, False)

        with nc.Block() as block:
            @block.sync
            def _(sp):
                sp.sem_inc(stored, 32)

                def load(k, b):
                    if not (isinstance(k, int) and k == 0):
                        sp.wait_ge(x_used, k)
                    sp.dma_start(x[:, :, :], h_in[bass.ds(k * T, T), :].rearrange("(t p) d -> p t d", p=P)).then_inc(x_in, 16)

                def body(i, b, more):
                    if more:
                        load(i + 1, 1 - b)
                    held(sp, S["y_ready"], i + 1, sp_passed)
                    held(sp, stored, 16 * i + 32, sp_passed)
                    sp.dma_start(h_out[bass.ds(i * T, T), :].rearrange("(t p) d -> p t d", p=P), y[b][:, :, :]).then_inc(stored, 16)

                sequences(sp, load, body)
                sp.wait_ge(stored, 16 * (B + 2))

            @block.vector
            def _(dve):
                dve.sem_clear(dve_steps)
                s = Steps(dve, dve_steps)

                def moment(k):
                    held(dve, x_in, 16 * k + 16, dve_passed)
                    ln_moments(dve, s, x, stats, moments)
                    dve.sem_inc(S["moments_ready"], 1)

                def normalised(k, b):
                    dve.wait_ge(S["std_ready"], k + 1)
                    s.did(ln_apply(dve, s, xn, x, moments, std))
                    dve.wait_ge(stored, 16 * k + 16)
                    s.wait()
                    dve.sem_inc(S["xn_ready"], 1)
                    s.did(dve.tensor_copy(y[b][:, :, :], x[:, :, :]))
                    s.wait()
                    dve.sem_inc(x_used, 1)

                def rests(k, m):
                    dve.wait_ge(S["high_ready"], 2 * HEADS0 * k + m + 1)
                    if m >= 2:
                        dve.wait_ge(S["parts_ready"], 2 * HEADS0 * k + m - 1)
                    dve.scalar_tensor_tensor(rest[m % 2][:, :], high[m % 2][:, :], less_high[m % 2][:, 0:1], ps_T[0:STACK, :],
                                             ALU.mult, ALU.add).then_inc(S["T_used"], 1)

                def stacks(k, b, m):
                    dst = kS[b][m // 2][:, PAD0:] if m % 2 else qS[b][m // 2][:, :]
                    dve.wait_ge(S["middle_ready"], 2 * HEADS0 * k + m + 1)
                    dve.scalar_tensor_tensor(dst, middle[m % 2][:, :], less_middle[m % 2][:, 0:1], rest[m % 2][:, :],
                                             ALU.mult, ALU.add).then_inc(S["parts_ready"], 1)

                def prepare(k, b):
                    moment(k)
                    normalised(k, b)
                    for m in range(2 * HEADS0 + 1):
                        if m < 2 * HEADS0:
                            rests(k, m)
                        if m >= 1:
                            stacks(k, b, m - 1)
                    s.restart()

                def body(i, b, more):
                    def maxima(u):
                        qt, h, k = u // HEADS0, u % HEADS0, u % 2
                        off = T - P - qt * P
                        if u >= 2:
                            dve.wait_ge(S["probs_ready"], UNITS * i + u - 1)
                        for g in range(2):
                            held(dve, S["scores_ready"], 2 * UNITS * i + 2 * u + g + 1, dve_passed)
                            dve.tensor_tensor_reduce(att[k][:, 2 * g:2 * g + 2, :], ps_att[g][:, :, :], bias[:, h, 2 * g:2 * g + 2, off:off + T], 1.0, -3.0e38,
                                                     ALU.add, ALU.max, rowmax[k][:, g:g + 1]).then_inc(S["scores_used"], 1)
                        dve.wait_ge(S["scores_used"], 2 * UNITS * i + 2 * u + 2)
                        dve.tensor_reduce(negmax[k][:, :], rowmax[k][:, :], AX.X, ALU.max, negate=True).then_inc(S["max_ready"], 1)

                    def inverse(u):
                        dve.wait_ge(S["probs_ready"], UNITS * i + u + 1)
                        s.did(dve.reciprocal(inv[u % 6][:, :], total[u % 6][:, :]))

                    def normalise(u):
                        qt, h = u // HEADS0, u % HEADS0
                        dve.wait_ge(S["ctx_ps"], UNITS * i + u + 1)
                        s.wait()
                        dve.tensor_scalar(context[:, qt, h * DH0:(h + 1) * DH0], [ps_c, ps_v][u % 2][:, u * DH0:(u + 1) * DH0], inv[u % 6][:, 0:1], None,
                                          ALU.mult).then_inc(S["context_part"], 1)

                    for step in range(UNITS + 5):
                        m = step - FIRST - PART
                        if step < UNITS:
                            maxima(step)
                        if more and 0 <= m < 2 * HEADS0:
                            rests(i + 1, m)
                        if step >= 5:
                            normalise(step - 5)
                        if 2 <= step <= UNITS + 1:
                            inverse(step - 2)
                        if more and 1 <= m <= 2 * HEADS0:
                            stacks(i + 1, 1 - b, m - 1)
                        if more and step == FIRST - 2:
                            moment(i + 1)
                        if more and step == FIRST - 1:
                            normalised(i + 1, 1 - b)
                    dve.wait_ge(S["context_part"], UNITS * i + UNITS)
                    dve.sem_inc(S["context_ready"], 1)
                    dve.wait_ge(S["T_ps"], context_use(i) + 1)
                    dve.tensor_copy(contextT[0:D, :], ps_T[0:D, :]).then_inc(S["T_used"], 1)
                    dve.wait_ge(S["y_ps"], i + 1)
                    s.did(dve.tensor_tensor(y[b][:, :, :], ps_v[:, 0:TT * D].rearrange("p (t d) -> p t d", d=D), y[b][:, :, :], ALU.add))
                    s.wait()
                    dve.sem_inc(S["y_ready"], 1)
                    s.restart()

                sequences(dve, prepare, body)

            @block.scalar
            def _(act):
                def root(k):
                    act.wait_ge(S["moments_ready"], k + 1)
                    act.activation(std[:, :], moments[:, :, 1], ACT.Sqrt, bias=eps[:, 0:1]).then_inc(S["std_ready"], 1)

                def item(k, b, n):
                    act.wait_ge(S["T_ps"], use(k, n) + 1)
                    if n == TRANSPOSE:
                        act.activation(xnT[0:D, :], ps_T[0:D, :], ACT.Copy).then_inc(S["T_used"], 1)
                    elif n == VALUE:
                        act.activation(vT[:, PAD0:], ps_T[0:D, :], ACT.Copy).then_inc(S["T_used"], 1)
                    elif n < SUM:
                        act.activation(high[n % 2][:, :], ps_T[0:STACK, :], ACT.Copy).then_inc(S["high_ready"], 1)
                    else:
                        act.activation(vsum[b][:, :, :], ps_T[:, 0:TT * D].rearrange("p (t d) -> p t d", d=D), ACT.Copy).then_inc(S["T_used"], 1)

                def middles(k, m):
                    act.wait_ge(S["T_used"], use(k, PART + m) + 2)
                    if m >= 2:
                        act.wait_ge(S["parts_ready"], 2 * HEADS0 * k + m - 1)
                    act.activation(middle[m % 2][:, :], rest[m % 2][:, :], ACT.Copy).then_inc(S["middle_ready"], 1)

                def step_of(k, b, n):
                    if n < SUM:
                        item(k, b, n)
                    if PART < n <= SUM:
                        middles(k, n - PART - 1)
                    if n == SUM:
                        item(k, b, n)

                def prepare(k, b):
                    root(k)
                    for n in range(ITEMS):
                        step_of(k, b, n)

                def body(i, b, more):
                    def exponentials(u):
                        act.wait_ge(S["max_ready"], UNITS * i + u + 1)
                        if u >= 2:
                            act.wait_ge(S["summed"], UNITS * i + u - 1)
                        act.activation(prob[u % 2][:, :, :], att[u % 2][:, :, :], ACT.Exp, bias=negmax[u % 2][:, 0:1],
                                       accum_out=total[u % 6][:, 0:1]).then_inc(S["probs_ready"], 1)

                    def transposed(u):
                        act.wait_ge(S["pT_ps"], UNITS * i + u + 1)
                        if u >= 2:
                            act.wait_ge(S["ctx_ps"], UNITS * i + u - 1)
                        act.activation(probT[u % 2][:, :, :], ps_pT[:, :].rearrange("p (t q) -> p t q", t=TT), ACT.Copy).then_inc(S["pT_ready"], 1)

                    for step in range(UNITS + 3):
                        if more and step == FIRST - 1:
                            root(i + 1)
                        if more and 0 <= step - FIRST < ITEMS:
                            step_of(i + 1, 1 - b, step - FIRST)
                        if step >= 3:
                            transposed(step - 3)
                        if step < UNITS:
                            exponentials(step)

                sequences(act, prepare, body)

            @block.gpsimd
            def _(pool):
                pool.sem_clear(gp_steps)
                s = Steps(pool, gp_steps)

                def summed_values(k, part):
                    if part == 0:
                        pool.wait_ge(S["T_used"], use(k, VALUE) + 2)
                        s.did(pool.tensor_tensor(vsumT[0][:, :], vT[:, PAD0:PAD0 + T], vT[:, PAD0 - SHIFTS[1]:PAD0 - SHIFTS[1] + T], ALU.add))
                    elif part == 1:
                        s.did(pool.tensor_tensor(vsumT[1][:, :], vT[:, PAD0 - SHIFTS[2]:PAD0 - SHIFTS[2] + T], vT[:, PAD0 - SHIFTS[3]:PAD0 - SHIFTS[3] + T], ALU.add))
                    else:
                        s.wait()
                        pool.tensor_tensor(vsumT[0][:, :], vsumT[0][:, :], vsumT[1][:, :], ALU.add).then_inc(S["vsum_made"], 1)
                        s.restart()

                def prepare(k, b):
                    for part in range(3):
                        summed_values(k, part)

                def body(i, b, more):
                    for u in range(UNITS):
                        pool.wait_ge(S["probs_ready"], UNITS * i + u + 1)
                        if u >= 3:
                            pool.wait_ge(S["pT_ps"], UNITS * i + u - 2)
                        pool.tensor_tensor(psum_p[u % 3][:, :, :], prob[u % 2][:, 0:2, :], prob[u % 2][:, 2:4, :], ALU.add).then_inc(S["summed"], 1)
                        if more and 0 <= u - FIRST - 2 < 3:
                            summed_values(i + 1, u - FIRST - 2)

                sequences(pool, prepare, body)

            @block.tensor
            def _(pe):
                pe.sem_inc(S["T_used"], 1)

                def item(k, n):
                    if n == TRANSPOSE:
                        held(pe, S["xn_ready"], k + 1, pe_passed)
                    if n == SUM:
                        held(pe, S["vsum_made"], k + 1, pe_passed)
                    held(pe, S["T_used"], use(k, n) + 1, pe_passed)
                    if n == TRANSPOSE:
                        for t in range(TT):
                            mm = pe.transpose(ps_T[0:D, t * P:(t + 1) * P], xn[:, t, :], ident[:, :])
                    elif n == VALUE:
                        mm = pe.matmul(ps_T[0:D, :], wv[:, :], xnT[:, :], start=True, stop=True)
                    elif n < SUM:
                        m = n - PART
                        mm = pe.matmul(ps_T[0:STACK, :], [wq, wk][m % 2][:, m // 2, :, :].rearrange("i n d -> i (n d)"), xnT[:, :],
                                       start=True, stop=True)
                    else:
                        for t in range(TT):
                            mm = pe.transpose(ps_T[:, t * D:(t + 1) * D], vsumT[0][:, t * P:(t + 1) * P], ident[0:D, 0:D])
                    mm.then_inc(S["T_ps"], 1)

                def prepare(k, b):
                    for n in range(ITEMS):
                        item(k, n)

                def body(i, b, more):
                    def scores(u):
                        qt, h = u // HEADS0, u % HEADS0
                        for j, shift in enumerate(SHIFTS):
                            if u >= 1 and j % 2 == 0:
                                held(pe, S["scores_used"], 2 * UNITS * i + 2 * (u - 1) + j // 2 + 1, pe_passed)
                            mm = pe.matmul(ps_att[j // 2][:, j % 2, :], qS[b][h][:, qt * P:(qt + 1) * P], kS[b][h][:, PAD0 - shift:PAD0 - shift + T],
                                           start=True, stop=True)
                            if j % 2 == 1:
                                mm.then_inc(S["scores_ready"], 1)

                    def transposes(u):
                        pe.wait_ge(S["summed"], UNITS * i + u + 1)
                        if u >= 1:
                            pe.wait_ge(S["pT_ready"], UNITS * i + u)
                        for t in range(TT):
                            for j in range(NSH // 2):
                                mm = pe.matmul(ps_pT[:, t * P:(t + 1) * P], psum_p[u % 3][:, j, t * P:(t + 1) * P], ident[:, :],
                                               start=(j == 0), stop=(j == NSH // 2 - 1))
                        mm.then_inc(S["pT_ps"], 1)

                    def values(u):
                        h = u % HEADS0
                        pe.wait_ge(S["pT_ready"], UNITS * i + u + 1)
                        if u >= 2:
                            pe.wait_ge(S["context_part"], UNITS * i + u - 1)
                        for t in range(TT):
                            mm = pe.matmul([ps_c, ps_v][u % 2][:, u * DH0:(u + 1) * DH0], probT[u % 2][:, t, :], vsum[b][:, t, h * DH0:(h + 1) * DH0],
                                           start=(t == 0), stop=(t == TT - 1))
                        mm.then_inc(S["ctx_ps"], 1)

                    pe.wait_ge(S["T_used"], use(i, SUM) + 2)
                    pe.wait_ge(S["parts_ready"], 2 * HEADS0 * i + 2 * HEADS0)
                    for step in range(UNITS + 4):
                        if step < UNITS:
                            scores(step)
                        if more and 0 <= step - FIRST < ITEMS:
                            item(i + 1, step - FIRST)
                        if 3 <= step < UNITS + 3:
                            transposes(step - 3)
                        if step >= 4:
                            values(step - 4)
                    held(pe, S["context_ready"], i + 1, pe_passed)
                    held(pe, S["T_used"], context_use(i) + 1, pe_passed)
                    for t in range(TT):
                        mm = pe.transpose(ps_T[0:D, t * P:(t + 1) * P], context[:, t, :], ident[:, :])
                    mm.then_inc(S["T_ps"], 1)
                    pe.wait_ge(S["T_used"], context_use(i) + 2)
                    for t in range(TT):
                        mm = pe.matmul(ps_v[:, t * D:(t + 1) * D], contextT[:, t * P:(t + 1) * P], wo[:, :], start=True, stop=True)
                    mm.then_inc(S["y_ps"], 1)

                sequences(pe, prepare, body)

        clear_semaphores(nc, sems)


HID0, EXPERTS = 256, 8
HC0 = HID0 // P
HEADS1 = 8
PAIRS = HEADS1 // 2
ROWS3 = 3 * NTOK
BD_PARTS = 3


def experts_and_projection(nc, w, w_next, h_in, h_out, qkvT):
    with ExitStack() as ctx:
        def sb(name, shape, dt=F32):
            return ctx.enter_context(nc.sbuf_tensor("exp_" + name, shape, dt))

        def ps(name):
            return ctx.enter_context(nc.psum_tensor("exp_" + name, [P, 512], F32))

        sems = []

        def sem(name):
            sems.append(ctx.enter_context(nc.semaphore("exp_" + name)))
            return sems[-1]

        R = range(2)
        w1 = sb("w1", [D + 1, HID0])
        wg = sb("wg", [P, HC0, EXPERTS])
        bg = sb("bg", [1, EXPERTS])
        wd = sb("wd", [P, HC0, EXPERTS * D])
        bd = sb("bd", [BD_PARTS, EXPERTS * D])
        bd_rest = sb("bd_rest", [BD_PARTS, EXPERTS * D])
        bd_part = sb("bd_part", [BD_PARTS, EXPERTS * D], BF16)
        less = [sb(f"less{k}", [BD_PARTS, 1]) for k in R]
        ones_parts = sb("ones_parts", [BD_PARTS, P], BF16)
        ones_row = sb("ones_row", [1, P])
        wqkv = sb("wqkv", [D + 1, 3, PAIRS, P])
        eps = sb("eps", [P, 1])
        ident = sb("ident", [P, P])
        expert_id_i = sb("expert_id_i", [P, EXPERTS], I32)
        expert_id = sb("expert_id", [P, EXPERTS])
        x = [sb(f"x{b}", [P, TT, D]) for b in R]
        xn, stats, moments, std = ([sb(f"{n}{k}", shape) for k in R] for n, shape in
                                   (("xn", [P, TT, D]), ("stats", [P, TT, 6]), ("moments", [P, TT, 2]), ("std", [P, TT])))
        xnT = [sb(f"xnT{b}", [D + 1, T]) for b in R]
        ynT = sb("ynT", [D + 1, T])
        hidT = [sb(f"hidT{b}", [P, HC0, T]) for b in R]
        prob = sb("prob", [P, TT, EXPERTS])
        pmax = sb("pmax", [P, TT])
        psum_e = sb("psum_e", [P, TT])
        top8 = sb("top8", [P, TT, 8])
        top8_at = sb("top8_at", [P, TT, 8], U32)
        best = sb("best", [P, TT])
        pick = sb("pick", [P, TT, EXPERTS])
        picked = [sb(f"picked{b}", [P, EXPERTS, D]) for b in R]
        y = [sb(f"y{b}", [P, TT, D]) for b in R]
        rows = [sb(f"rows{f}", [P, T, 3]) for f in range(PAIRS)]
        ps_T = ps("ps_T")
        ps_hid = [ps(f"ps_hid{k}") for k in range(HC0)]
        ps_y = [ps(f"ps_y{k}") for k in R]
        ps_r = [ps(f"ps_r{k}") for k in range(3)]
        loaded, gp_made = sem("loaded"), sem("gp_made")
        stored = [sem(f"stored{f}") for f in range(PAIRS)]
        names = ("x_in x_used moments_ready std_ready xn_ready y_moments_ready y_std_ready yn_ready T_ps T_used hid_ps hid_ready "
                 "gates_exp y_ps y_used y_ready y_stored rows_ps rows_dve rows_act")
        S = {n: sem(n) for n in names.split()}
        dve_steps, dve_passed, pe_passed, sp_passed = sem("dve_steps"), sem("dve_passed"), sem("pe_passed"), sem("sp_passed")

        with nc.Block() as block:
            @block.sync
            def _(sp):
                for dst, src in ((w1[0:D, :], w["W1"]), (w1[D:D + 1, :], w["b1"].unsqueeze(0)),
                                 (wg[:, :, :], w["Wg"].rearrange("(c p) e -> p c e", p=P)), (bg[:, :], w["bg"].unsqueeze(0)),
                                 (bd[:, :], w["bd"].rearrange("e d -> (e d)").partition_broadcast(BD_PARTS)),
                                 (wqkv[0:D, :, :, :].rearrange("i c f m -> i (c f m)"), w_next["Wqkv_heads"]),
                                 (wqkv[D:D + 1, :, :, :].rearrange("i c f m -> i (c f m)"), w_next["bqkv_heads"].unsqueeze(0))):
                    sp.dma_start(dst, src).then_inc(loaded, 16)
                for c in range(HC0):
                    sp.dma_start(wd[:, c, :].rearrange("p (e d) -> p e d", e=EXPERTS),
                                 w["Wd"][:, c * P:(c + 1) * P, :].rearrange("e p d -> p e d")).then_inc(loaded, 16)
                sp.wait_ge(loaded, 16 * (7 + HC0))

            @block.gpsimd
            def _(pool):
                pool.iota(expert_id_i[:, :], [[1, EXPERTS]], base=0, channel_multiplier=0).then_inc(gp_made, 1)
                pool.memset(ident[:, :], 0.0).then_inc(gp_made, 1)
                for k in R:
                    pool.memset(less[k][:, :], 0.0).then_inc(gp_made, 1)
                pool.wait_ge(gp_made, 4)
                pool.affine_select(out=ident[:, :], in_=ident[:, :], compare_op=ALU.not_equal, fill=1.0, base=0,
                                   pattern=[[-1, P]], channel_multiplier=1).then_inc(gp_made, 1)
                for k in R:
                    pool.affine_select(out=less[k][:, :], in_=less[k][:, :], compare_op=ALU.is_gt, fill=-1.0, base=k + 1,
                                       pattern=[[0, 1]], channel_multiplier=-1).then_inc(gp_made, 1)

            @block.vector
            def _(dve):
                s = Steps(dve, dve_steps)
                s.did(dve.memset(ones_row[:, :], 1.0))
                s.did(dve.memset(ones_parts[:, :], 1.0))
                s.did(dve.memset(eps[:, :], EPS))
                for one in (*xnT, ynT):
                    s.did(dve.memset(one[D:D + 1, :], 1.0))
                dve.wait_ge(gp_made, 7)
                s.did(dve.tensor_copy(expert_id[:, :], expert_id_i[:, :]))
                dve.wait_ge(loaded, 16 * (7 + HC0))
                for k in R:
                    s.did(dve.tensor_copy(bd_part[:, :], bd[:, :]))
                    s.wait()
                    s.did(dve.scalar_tensor_tensor(bd_rest[:, :], bd_part[:, :], less[k][:, 0:1], bd[:, :], ALU.mult, ALU.add))
                    s.wait()
                    s.did(dve.tensor_copy(bd[:, :], bd_rest[:, :]))
                    s.wait()
                s.did(dve.tensor_copy(bd_part[:, :], bd[:, :]))
                s.restart()

        def pipeline(eng, first, body):
            first()
            body(0, 0, True, True, False)
            with eng.Fori(0, B // 2 - 1) as q:
                body(2 * q + 1, 1, True, True, True)
                body(2 * q + 2, 0, True, True, True)
            body(B - 1, 1, True, False, True)
            body(B, 0, False, False, True)

        def use_projected(k):
            return 3 * k - 1 if isinstance(k, int) and k == B else 3 * k

        def use_gates(k):
            return 3 * k + 1

        def use_next(k):
            return 3 * k + 2

        with nc.Block() as block:
            @block.sync
            def _(sp):
                for f in range(PAIRS):
                    sp.sem_inc(stored[f], 16)
                sp.sem_inc(S["y_stored"], 32)

                def load(k, b):
                    sp.dma_start(x[b][:, :, :], h_in[bass.ds(k * T, T), :].rearrange("(t p) d -> p t d", p=P)).then_inc(S["x_in"], 16)

                def store_rows(k, f):
                    held(sp, S["rows_act"], 8 * k + 2 * f + 4, sp_passed)
                    held(sp, S["rows_dve"], 4 * k + f + 2, sp_passed)
                    sp.dma_start(qkvT[f, :, bass.ds(k * 3 * T, 3 * T)], rows[f][:, :, :].rearrange("p t c -> p (t c)")).then_inc(stored[f], 16)

                def body(k, b, experts, more, project):
                    if more:
                        if project:
                            held(sp, S["x_used"], k, sp_passed)
                        held(sp, S["x_in"], 16 * k + 16, sp_passed)
                        load(k + 1, 1 - b)
                    if project:
                        store_rows(k - 1, 0)
                        store_rows(k - 1, 1)
                    if experts:
                        held(sp, S["y_ready"], k + 1, sp_passed)
                        held(sp, S["y_stored"], 16 * k + 32, sp_passed)
                        sp.dma_start(h_out[bass.ds(k * T, T), :].rearrange("(t p) d -> p t d", p=P), y[b][:, :, :]).then_inc(S["y_stored"], 16)
                    if project:
                        store_rows(k - 1, 2)
                        store_rows(k - 1, 3)

                pipeline(sp, lambda: load(0, 0), body)
                for f in range(PAIRS):
                    sp.wait_ge(stored[f], 16 * (B + 1))
                sp.wait_ge(S["y_stored"], 16 * (B + 2))

            @block.vector
            def _(dve):
                s = Steps(dve, dve_steps)

                def moment(k, b):
                    held(dve, S["x_in"], 16 * k + 16, dve_passed)
                    ln_moments(dve, s, x[b], stats[0], moments[0])
                    dve.sem_inc(S["moments_ready"], 1)

                def normalised(k, b):
                    dve.wait_ge(S["std_ready"], k + 1)
                    ln_apply(dve, s, xn[0], x[b], moments[0], std[0]).then_inc(S["xn_ready"], 1)

                def transposed(use, dst):
                    dve.wait_ge(S["T_ps"], use + 1)
                    dve.tensor_copy(dst[0:D, :], ps_T[0:D, :]).then_inc(S["T_used"], 1)

                def first():
                    dve.sem_clear(dve_steps)
                    moment(0, 0)
                    normalised(0, 0)
                    transposed(0, xnT[0])
                    s.restart()

                def copy_rows(k, f):
                    dve.wait_ge(stored[f], 16 * k + 16)
                    dve.wait_ge(S["rows_ps"], 12 * k + 3 * f + 1)
                    dve.tensor_copy(rows[f][:, :, 0], ps_r[0][:, :]).then_inc(S["rows_dve"], 1)

                def route(k):
                    dve.wait_ge(S["T_ps"], use_gates(k) + 1)
                    g = ps_T[:, 0:TT * EXPERTS].rearrange("p (t e) -> p t e", e=EXPERTS)
                    s.did(dve.tensor_reduce(pmax[:, :], g, AX.X, ALU.max))
                    s.wait()
                    dve.tensor_tensor(prob[:, :, :], g, bc(pmax[:, :], 2, EXPERTS), ALU.subtract).then_inc(S["T_used"], 1)
                    dve.wait_ge(S["gates_exp"], k + 1)
                    s.did(dve.tensor_reduce(psum_e[:, :], prob[:, :, :], AX.X, ALU.add))
                    s.wait()
                    s.did(dve.reciprocal(psum_e[:, :], psum_e[:, :]))
                    s.wait()
                    s.did(dve.tensor_tensor(prob[:, :, :], prob[:, :, :], bc(psum_e[:, :], 2, EXPERTS), ALU.mult))
                    s.wait()
                    for t in range(TT):
                        s.did(dve.max(top8[:, t, :], prob[:, t, :]))
                    s.wait()
                    for t in range(TT):
                        s.did(dve.max_index(top8_at[:, t, :], top8[:, t, :], prob[:, t, :]))
                    s.wait()
                    s.did(dve.tensor_copy(best[:, :], top8_at[:, :, 0]))
                    s.wait()
                    s.did(dve.tensor_tensor(pick[:, :, :], bc(expert_id[:, :], 1, TT), bc(best[:, :], 2, EXPERTS), ALU.is_equal))
                    s.wait()
                    s.did(dve.tensor_tensor(pick[:, :, :], pick[:, :, :], prob[:, :, :], ALU.mult))
                    s.wait()

                def weigh(k, b, t):
                    if t == 0:
                        dve.wait_ge(S["y_stored"], 16 * k + 16)
                    dve.wait_ge(S["y_ps"], TT * k + t + 1)
                    s.did(dve.tensor_tensor(picked[t % 2][:, :, :], ps_y[t % 2][:, :].rearrange("p (e d) -> p e d", e=EXPERTS),
                                            bc(pick[:, t, :], 2, D), ALU.mult))
                    s.wait()
                    dve.sem_inc(S["y_used"], 1)
                    s.did(dve.tensor_reduce(y[b][:, t, :], picked[t % 2][:, :, :].rearrange("p e d -> p d e"), AX.X, ALU.add))

                def body(k, b, experts, more, project):
                    if project:
                        transposed(use_projected(k), ynT)
                        copy_rows(k - 1, 0)
                        copy_rows(k - 1, 1)
                    if more:
                        moment(k + 1, 1 - b)
                        normalised(k + 1, 1 - b)
                    if experts:
                        route(k)
                        for t in range(TT):
                            weigh(k, b, t)
                    if more:
                        transposed(use_next(k), xnT[1 - b])
                    if experts:
                        s.wait()
                        s.did(dve.tensor_tensor(y[b][:, :, :], y[b][:, :, :], x[b][:, :, :], ALU.add))
                        s.wait()
                        dve.sem_inc(S["x_used"], 1)
                        dve.sem_inc(S["y_ready"], 1)
                        ln_moments(dve, s, y[b], stats[1], moments[1])
                        dve.sem_inc(S["y_moments_ready"], 1)
                    if project:
                        copy_rows(k - 1, 2)
                    if experts:
                        dve.wait_ge(S["y_std_ready"], k + 1)
                        ln_apply(dve, s, xn[1], y[b], moments[1], std[1]).then_inc(S["yn_ready"], 1)
                    if project:
                        copy_rows(k - 1, 3)
                    if experts:
                        s.restart()

                pipeline(dve, first, body)

            @block.scalar
            def _(act):
                def root(n, k, ready, done):
                    act.wait_ge(ready, k + 1)
                    act.activation(std[n][:, :], moments[n][:, :, 1], ACT.Sqrt, bias=eps[:, 0:1]).then_inc(done, 1)

                def copy_rows(k, f):
                    act.wait_ge(stored[f], 16 * k + 16)
                    for c in range(1, 3):
                        act.wait_ge(S["rows_ps"], 12 * k + 3 * f + c + 1)
                        act.activation(rows[f][:, :, c], ps_r[c][:, :], ACT.Copy).then_inc(S["rows_act"], 1)

                def body(k, b, experts, more, project):
                    if experts:
                        for c in range(HC0):
                            act.wait_ge(S["hid_ps"], HC0 * k + c + 1)
                            act.activation(hidT[b][:, c, :], ps_hid[c][:, :], ACT.Gelu).then_inc(S["hid_ready"], 1)
                    if project:
                        copy_rows(k - 1, 0)
                        copy_rows(k - 1, 1)
                    if more:
                        root(0, k + 1, S["moments_ready"], S["std_ready"])
                    if experts:
                        act.wait_ge(S["T_used"], use_gates(k) + 2)
                        act.activation(prob[:, :, :], prob[:, :, :], ACT.Exp).then_inc(S["gates_exp"], 1)
                    if project:
                        copy_rows(k - 1, 2)
                    if experts:
                        root(1, k, S["y_moments_ready"], S["y_std_ready"])
                    if project:
                        copy_rows(k - 1, 3)

                pipeline(act, lambda: root(0, 0, S["moments_ready"], S["std_ready"]), body)

            @block.tensor
            def _(pe):
                for name, banks in (("T_used", 1), ("hid_ready", HC0), ("y_used", 2), ("rows_dve", 1), ("rows_act", 2)):
                    pe.sem_inc(S[name], banks)

                def transposes(use, ready, n, src):
                    held(pe, ready, n, pe_passed)
                    held(pe, S["T_used"], use + 1, pe_passed)
                    for t in range(TT):
                        mm = pe.transpose(ps_T[0:D, t * P:(t + 1) * P], src[:, t, :], ident[:, :])
                    mm.then_inc(S["T_ps"], 1)

                def rows_of(k, f):
                    for c in range(3):
                        if c == 0:
                            pe.wait_ge(S["rows_dve"], 4 * k + f + 1)
                        else:
                            pe.wait_ge(S["rows_act"], 8 * k + 2 * f + c)
                        pe.matmul(ps_r[c][:, :], wqkv[:, c, f, :], ynT[:, :], start=True, stop=True).then_inc(S["rows_ps"], 1)

                def body(k, b, experts, more, project):
                    if experts:
                        pe.wait_ge(S["T_used"], 3 * k + 1 if project else 2)
                        for c in range(HC0):
                            pe.wait_ge(S["hid_ready"], HC0 * k + c + 1)
                            pe.matmul(ps_hid[c][:, :], w1[:, c * P:(c + 1) * P], xnT[b][:, :], start=True, stop=True).then_inc(S["hid_ps"], 1)
                    if project:
                        transposes(use_projected(k), S["yn_ready"], k, xn[1])
                        pe.wait_ge(S["T_used"], use_projected(k) + 2)
                        rows_of(k - 1, 0)
                        rows_of(k - 1, 1)
                    if experts:
                        pe.wait_ge(S["hid_ready"], HC0 * k + 2 * HC0)
                        pe.wait_ge(S["T_used"], use_gates(k) + 1)
                        for t in range(TT):
                            gates = ps_T[:, t * EXPERTS:(t + 1) * EXPERTS]
                            for c in range(HC0):
                                pe.matmul(gates, hidT[b][:, c, t * P:(t + 1) * P], wg[:, c, :], start=(c == 0), stop=False)
                            mm = pe.matmul(gates, ones_row[:, :], bg[:, :], start=False, stop=True)
                        mm.then_inc(S["T_ps"], 1)
                        for t in range(TT):
                            pe.wait_ge(S["y_used"], TT * k + t + 1)
                            for c in range(HC0):
                                pe.matmul(ps_y[t % 2][:, :], hidT[b][:, c, t * P:(t + 1) * P], wd[:, c, :], start=(c == 0), stop=False)
                            pe.matmul(ps_y[t % 2][:, :], ones_parts[:, :], bd_part[:, :], start=False, stop=True).then_inc(S["y_ps"], 1)
                    if more:
                        transposes(use_next(k), S["xn_ready"], k + 2, xn[0])
                    if project:
                        rows_of(k - 1, 2)
                        rows_of(k - 1, 3)

                pipeline(pe, lambda: transposes(0, S["xn_ready"], 1, xn[0]), body)

        clear_semaphores(nc, sems)


HEADS2, NKEYS, DKEY, TOPK = 8, 64, 32, 16
NKV = NKEYS * NKEYS
GROUPS = 2 * HEADS2
LOW = -3.0e38
MASKED = -1.0e30
RUNS, _a = [], 0
while _a < TOPK:
    _n = TOPK // (_a + 1)
    _e = _a
    while _e < TOPK and TOPK // (_e + 1) == _n:
        _e += 1
    RUNS.append((_a, _e, _n))
    _a = _e
CANDS = sum((e - a) * n for a, e, n in RUNS)
KV = 2 * D
GSLOTS = 4
UN = TT * HEADS2


class Round:

    def __init__(self, q, c):
        self.q, self.c = q, c
        self.par = c % 2
        loop = q is not None
        self.dia = loop or c < B - 1
        self.mix = loop or 0 <= c < B
        self.cau = loop or c >= 1
        self.early = int(not loop and c < 0)

    def at(self, each, offset):
        if self.q is None:
            return each * self.c + offset
        return 2 * each * self.q + (each * self.c + offset)

    def chosen(self, t):
        if self.early:
            return t == 2
        return self.q is not None or 4 * self.c + t + 1 < B * TT

    def compared(self, t):
        if self.early:
            return t in (1, 2)
        return self.q is not None or 4 * self.c + t + 2 < B * TT

    def front_uses(self, t):
        if self.early:
            return t + 3 * max(0, t - 1)
        each = 3 if not self.dia else 4
        return self.at(16, 10 + each * t)


def rounds(eng, body):
    body(Round(None, -1))
    body(Round(None, 0))
    with eng.Fori(0, B // 2 - 1) as q:
        body(Round(q, 1))
        body(Round(q, 2))
    body(Round(None, B - 1))
    body(Round(None, B))


def past(eng, sem, value):
    if not isinstance(value, int) or value > 0:
        eng.wait_ge(sem, value)


def idx_probs(u):
    return PAIRS + u + max(0, (u - 1) // HEADS2)


def idx_outs(t):
    return PAIRS + min(8 * t + 9, UN) + t


TUSES = PAIRS + UN + TT
OUSES = UN + TT


def idx_values(u):
    return u + u // HEADS2


def sequence_pipeline(nc, w1, w2, qkvT, h_in, h_mid, h_out):
    with ExitStack() as ctx:
        def sb(name, shape, dt=F32):
            return ctx.enter_context(nc.sbuf_tensor("sq_" + name, shape, dt))

        def ps(name):
            return ctx.enter_context(nc.psum_tensor("sq_" + name, [P, 512], F32))

        sems = []

        def sem(name):
            sems.append(ctx.enter_context(nc.semaphore("sq_" + name)))
            return sems[-1]

        R = range(2)
        SCALE = float(D) ** -0.5
        ident = sb("ident", [P, P])
        eps = sb("eps", [P, 1])
        w0 = sb("w0", [P, PAIRS, 2 * D])
        b0 = sb("b0", [P, D])
        d_q, d_k, d_v = (sb("d_" + n, [P, PAIRS, T]) for n in "qkv")
        d_x = sb("d_x", [P, TT, D])
        d_negmax, d_bias, d_diag, d_sums, d_attn = (sb("d_" + n, [P, UN]) for n in ("negmax", "bias", "diag", "sums", "attn"))
        diag_out = [sb(f"diag_out{k}", [P, P]) for k in R]
        exp_out = [sb(f"exp_out{k}", [P, T]) for k in R]
        weighted = sb("weighted", [P, HEADS1, D])
        mid = sb("mid", [P, TT, D])
        stats = sb("stats", [P, 6])
        moments = sb("moments", [P, 2])
        std = sb("std", [P, 1])
        xn = sb("xn", [P, D])
        xnT = sb("xnT", [D, TT, P])
        wpkT = sb("wpkT", [DKEY, GROUPS, D])
        keysT = sb("keysT", [DKEY, GROUPS, NKEYS])
        wsim = sb("wsim", [D, GROUPS * NKEYS])
        wq = sb("wq", [D, HEADS2 * D])
        head_base_i = sb("head_base_i", [P, HEADS2], I32)
        head_base = sb("head_base", [P, HEADS2])
        cand_id_i = sb("cand_id_i", [P, CANDS], I32)
        cand_id = sb("cand_id", [P, CANDS])
        sim = [sb(f"sim{b}", [P, GROUPS, NKEYS]) for b in R]
        sim_rest = sb("sim_rest", [P, GROUPS, NKEYS])
        top = sb("top", [P, GROUPS, TOPK])
        top_at = sb("top_at", [P, GROUPS, TOPK], U32)
        top_at_f = sb("top_at_f", [P, GROUPS, TOPK])
        cand = sb("cand", [P, HEADS2, CANDS])
        cand_rest = sb("cand_rest", [P, HEADS2, CANDS])
        cand_row = sb("cand_row", [P, HEADS2, CANDS])
        best = sb("best", [P, HEADS2, TOPK])
        best_at = sb("best_at", [P, HEADS2, TOPK], U32)
        best_at_f = sb("best_at_f", [P, HEADS2, TOPK])
        is_cand = [sb(f"is_cand{k}", [P, TOPK, CANDS]) for k in R]
        row_f = sb("row_f", [P, HEADS2, TOPK])
        row = [sb(f"row{b}", [P, HEADS2, TOPK], I32) for b in R]
        weight = [sb(f"weight{b}", [P, HEADS2, TOPK]) for b in R]
        wsum = sb("wsum", [P, HEADS2])
        rows = [sb(f"rows{k}", [P, TOPK, KV]) for k in range(GSLOTS)]
        qT = [sb(f"qT{b}", [P, PAIRS, T]) for b in R]
        kv = [sb(f"kv{b}", [P, TT, 2, HEADS2, D]) for b in R]
        future = sb("future", [P, P])
        wo = sb("wo", [P, PAIRS, D])
        c_x = sb("c_x", [P, TT, D])
        kT = sb("kT", [P, PAIRS, T])
        c_negmax, c_sums, c_inv = (sb("c_" + n, [P, UN]) for n in ("negmax", "sums", "inv"))
        prob = [sb(f"prob{k}", [P, T]) for k in R]
        probT = [sb(f"probT{k}", [P, T]) for k in R]
        out = [sb(f"out{k}", [P, HEADS2, D]) for k in R]
        outT = sb("outT", [P, PAIRS, P])
        y = sb("y", [P, TT, D])
        ps_d = [ps(f"ps_d{k}") for k in R]
        ps_v = ps("ps_v")
        ps_f = ps("ps_f")
        ps_c = [ps(f"ps_c{k}") for k in R]
        ps_t = ps("ps_t")
        ps_o = ps("ps_o")

        loaded, gp_made, dve_made, pe_made, zeroed = sem("loaded"), sem("gp_made"), sem("dve_made"), sem("pe_made"), sem("zeroed")
        names = ("d_in d_used d_scores d_bias d_exp d_pre d_attn d_vals d_vals_used mid_ready "
                 "moments_ready std_ready xn_ready f_ps f_used sim_ready sim_used best_centred weight_exp row_ready "
                 "rows_used q_ready kv_ready c_in c_used c_scores c_max c_probs t_ps t_used o_ps o_used y_ready y_stored")
        S = {n: sem(n) for n in names.split()}
        mid_stored = [sem(f"mid_stored{t}") for t in range(TT)]
        dve_steps, sp_passed, dve_passed, pe_passed, pool_passed = (sem(n) for n in ("dve_steps", "sp_passed", "dve_passed", "pe_passed", "pool_passed"))
        gathered = [nc.alloc_semaphore(f"sq_gathered{k}") for k in range(GSLOTS)]

        with nc.Block() as block:
            @block.sync
            def _(sp):
                for dst, src in ((wpkT, "Wq_pkT"), (keysT, "keysT")):
                    sp.dma_start(dst[:, :, :], w2[src]).then_inc(loaded, 16)
                sp.wait_ge(loaded, 32)
                sp.dma_start(wq[:, :], w2["Wq"]).then_inc(loaded, 16)
                sp.dma_start(wo[:, :, :], w2["Wo"].rearrange("(f p) o -> p f o", p=P)).then_inc(loaded, 16)
                sp.dma_start(b0[:, :], w1["b0"].partition_broadcast(P)).then_inc(loaded, 16)
                sp.wait_ge(zeroed, 1)
                for hh in range(2):
                    sp.dma_start(w0[hh * D:(hh + 1) * D, :, hh * D:(hh + 1) * D],
                                 w1["W0_heads"].rearrange("(f a) d o -> a d f o", a=2)[hh]).then_inc(loaded, 16)
                sp.wait_ge(loaded, 112)

            @block.gpsimd
            def _(pool):
                pool.iota(head_base_i[:, :], [[NKV, HEADS2]], base=0, channel_multiplier=0).then_inc(gp_made, 1)
                pool.iota(cand_id_i[:, :], [[1, CANDS]], base=0, channel_multiplier=0).then_inc(gp_made, 1)
                pool.memset(ident[:, :], 0.0).then_inc(gp_made, 1)
                pool.memset(future[:, :], 0.0).then_inc(gp_made, 1)
                pool.wait_ge(gp_made, 4)
                pool.affine_select(out=ident[:, :], in_=ident[:, :], compare_op=ALU.not_equal, fill=1.0, base=0,
                                   pattern=[[-1, P]], channel_multiplier=1).then_inc(gp_made, 1)
                pool.affine_select(out=future[:, :], in_=future[:, :], compare_op=ALU.is_ge, fill=MASKED, base=0,
                                   pattern=[[-1, P]], channel_multiplier=1).then_inc(gp_made, 1)

            @block.tensor
            def _(pe):
                pe.wait_ge(loaded, 32)
                for g in range(GROUPS):
                    if g == 8:
                        pe.wait_ge(dve_made, 1)
                    mm = pe.matmul(ps_f[0:D, (g % 8) * NKEYS:(g % 8 + 1) * NKEYS], wpkT[:, g, :], keysT[:, g, :], start=True, stop=True)
                    if g % 8 == 7:
                        mm.then_inc(pe_made, 1)

            @block.vector
            def _(dve):
                dve.memset(w0[:, :, :], 0.0).then_inc(zeroed, 1)
                dve.memset(eps[:, :], EPS)
                dve.wait_ge(gp_made, 4)
                dve.tensor_copy(head_base[:, :], head_base_i[:, :])
                dve.tensor_copy(cand_id[:, :], cand_id_i[:, :])
                for half in R:
                    dve.wait_ge(pe_made, half + 1)
                    dve.tensor_copy(wsim[:, half * 512:(half + 1) * 512], ps_f[0:D, :]).then_inc(dve_made, 1)

        with nc.Block() as block:
            @block.sync
            def _(sp):
                for name in ("d_used", "c_used"):
                    sp.sem_inc(S[name], 1)
                for t in range(TT):
                    sp.sem_inc(mid_stored[t], 16)
                sp.sem_inc(S["y_stored"], 16)

                def body(r):
                    if r.dia:
                        sp.wait_ge(S["d_used"], r.at(1, 2))
                        for m, dst in enumerate((d_q, d_k, d_v)):
                            src = qkvT[:, :, bass.ds(r.at(T, T + m * NTOK), T)].rearrange("f p t -> p f t")
                            sp.dma_start(dst[:, :, :], src).then_inc(S["d_in"], 16)
                        sp.dma_start(d_x[:, :, :], h_in[bass.ds(r.at(T, T), T), :].rearrange("(t p) d -> p t d", p=P)).then_inc(S["d_in"], 16)
                    if r.cau:
                        held(sp, S["c_used"], r.at(1, 0), sp_passed)
                        for t in range(TT):
                            sp.wait_ge(mid_stored[t], r.at(16, 16))
                        sp.dma_start(c_x[:, :, :], h_mid[bass.ds(r.at(T, -T), T), :].rearrange("(t p) d -> p t d", p=P)).then_inc(S["c_in"], 16)
                    if r.dia:
                        for t in range(TT):
                            sp.wait_ge(S["mid_ready"], r.at(TT, TT + t + 1))
                            sp.dma_start(h_mid[bass.ds(r.at(T, T + t * P), P), :], mid[:, t, :]).then_inc(mid_stored[t], 16)
                    if r.cau:
                        sp.wait_ge(S["y_ready"], r.at(1, 0))
                        sp.dma_start(h_out[bass.ds(r.at(T, -T), T), :].rearrange("(t p) d -> p t d", p=P), y[:, :, :]).then_inc(S["y_stored"], 16)

                rounds(sp, body)
                for t in range(TT):
                    sp.wait_ge(mid_stored[t], 16 * (B + 1))
                sp.wait_ge(S["y_stored"], 16 * (B + 1))

            @block.gpsimd
            def _(pool):
                pool.sem_inc(S["rows_used"], GSLOTS)

                def body(r):
                    for j in range(UN if r.mix else 0):
                        t, h = divmod(j, HEADS2)
                        if h == 0:
                            held(pool, S["row_ready"], r.at(TT, t + 1), pool_passed)
                        held(pool, S["rows_used"], r.at(UN, j + 1), pool_passed)
                        for k in range(TOPK):
                            pool.indirect_dma_start(rows[j % GSLOTS][:, k, :], None, w2["table"],
                                                    bass.IndirectOffsetOnAxis(row[t % 2][:, h, k:k + 1], 0)).then_inc(gathered[j % GSLOTS], 16)

                rounds(pool, body)

            @block.tensor
            def _(pe):
                pe.sem_inc(S["d_exp"], 2)
                pe.sem_inc(S["d_vals_used"], 1)
                pe.sem_inc(S["f_used"], 1)
                pe.sem_inc(S["c_scores"], 1)
                pe.sem_inc(S["c_probs"], 2)
                pe.sem_inc(S["t_used"], 1)
                pe.sem_inc(S["o_used"], 1)

                def body(r):
                    def t_at(n):
                        return r.at(TUSES, n - TUSES)

                    def o_at(n):
                        return r.at(OUSES, n - OUSES)

                    def diagonal_scores(u):
                        t, h = divmod(u, HEADS1)
                        f = slice((h % 2) * D, (h % 2 + 1) * D)
                        pe.wait_ge(S["d_exp"], r.at(UN, UN + u + 1))
                        pe.matmul(ps_d[u % 2][:, :], d_k[f, h // 2, t * P:(t + 1) * P], d_q[f, h // 2, :],
                                  start=True, stop=True).then_inc(S["d_scores"], 1)

                    def causal_scores(u):
                        t, h = divmod(u, HEADS2)
                        f = slice((h % 2) * D, (h % 2 + 1) * D)
                        pe.wait_ge(S["c_probs"], r.at(UN, u + 1 - UN))
                        q = qT[1 - r.par][f, h // 2, t * P:(t + 1) * P]
                        own = slice(t * P, (t + 1) * P)
                        if t:
                            pe.matmul(ps_c[u % 2][:, 0:t * P], q, kT[f, h // 2, 0:t * P], start=True, stop=True)
                        pe.matmul(ps_c[u % 2][:, own], q, kT[f, h // 2, own], start=True, stop=False)
                        pe.matmul(ps_c[u % 2][:, own], ident[:, :], future[:, :], start=False, stop=True).then_inc(S["c_scores"], 1)

                    def causal_transposes(u):
                        pe.wait_ge(S["c_probs"], r.at(UN, u + 3 - UN))
                        pe.wait_ge(S["t_used"], t_at(idx_probs(u) + 1))
                        for k in range(u // HEADS2 + 1):
                            mm = pe.transpose(ps_t[:, k * P:(k + 1) * P], prob[u % 2][:, k * P:(k + 1) * P], ident[:, :])
                        mm.then_inc(S["t_ps"], 1)

                    def causal_values(u):
                        t, h = divmod(u, HEADS2)
                        pe.wait_ge(S["t_used"], t_at(idx_probs(u) + 2))
                        pe.wait_ge(S["o_used"], o_at(idx_values(u) + 1))
                        for k in range(t + 1):
                            mm = pe.matmul(ps_o[:, 0:D], probT[u % 2][:, k * P:(k + 1) * P], kv[1 - r.par][:, k, 1, h, :],
                                           start=(k == 0), stop=(k == t))
                        mm.then_inc(S["o_ps"], 1)

                    def causal_projection(t):
                        pe.wait_ge(S["t_used"], t_at(idx_outs(t) + 1))
                        pe.wait_ge(S["o_used"], o_at(idx_values(8 * t + 7) + 2))
                        for f in range(PAIRS):
                            mm = pe.transpose(ps_t[:, f * P:(f + 1) * P], out[t % 2][:, 2 * f:2 * f + 2, :].rearrange("p h c -> p (h c)"), ident[:, :])
                        mm.then_inc(S["t_ps"], 1)
                        pe.wait_ge(S["t_used"], t_at(idx_outs(t) + 2))
                        for f in range(PAIRS):
                            mm = pe.matmul(ps_o[:, 0:D], outT[:, f, :], wo[:, f, :], start=(f == 0), stop=(f == PAIRS - 1))
                        mm.then_inc(S["o_ps"], 1)

                    if r.cau:
                        pe.wait_ge(S["q_ready"], r.at(TT, 0))
                        held(pe, S["kv_ready"], r.at(1, 0), pe_passed)
                        for f in range(PAIRS):
                            pe.wait_ge(S["t_used"], t_at(f + 1))
                            for t in range(TT):
                                mm = pe.transpose(ps_t[:, t * P:(t + 1) * P], kv[1 - r.par][:, t, 0, 2 * f:2 * f + 2, :].rearrange("p h c -> p (h c)"), ident[:, :])
                            mm.then_inc(S["t_ps"], 1)
                        pe.wait_ge(S["t_used"], t_at(PAIRS + 1))
                        causal_scores(0)
                    if r.dia:
                        pe.wait_ge(S["d_in"], r.at(64, 128))
                        diagonal_scores(0)
                    for j in range(UN + 2):
                        t, h = divmod(j, 8)
                        if r.dia and j + 1 < UN:
                            diagonal_scores(j + 1)
                        if r.cau:
                            if j + 1 < UN:
                                causal_scores(j + 1)
                            if 1 <= j <= UN:
                                causal_transposes(j - 1)
                            if j >= 2:
                                causal_values(j - 2)
                        if j < UN and 2 <= h <= 4 and r.compared(t):
                            x = xnT[:, (t + 2 + r.early) % TT, :]
                            pe.wait_ge(S["f_used"], r.front_uses(t) + h - 1)
                            if h < 4:
                                mm = pe.matmul(ps_f[:, :], x, wsim[:, (h - 2) * 512:(h - 1) * 512], start=True, stop=True)
                            else:
                                for f in range(PAIRS):
                                    mm = pe.matmul(ps_f[:, f * P:(f + 1) * P], wq[:, f * P:(f + 1) * P], x, start=True, stop=True)
                            mm.then_inc(S["f_ps"], 1)
                        if j < UN and h == 7 and r.dia:
                            pe.wait_ge(S["d_vals_used"], r.at(TT, TT + t + 1))
                            for f in range(PAIRS):
                                mm = pe.matmul(ps_v[:, f * P:(f + 1) * P], d_v[:, f, t * P:(t + 1) * P], w0[:, f, :], start=True, stop=True)
                            mm.then_inc(S["d_vals"], 1)
                            pe.wait_ge(S["f_used"], r.front_uses(t) + (3 if r.compared(t) else 0) + 1)
                            held(pe, S["xn_ready"], r.at(TT, TT + t + 1), pe_passed)
                            pe.transpose(ps_f[0:D, 0:P], xn[:, :], ident[:, :]).then_inc(S["f_ps"], 1)
                        if r.cau and j >= 9 and h == 1:
                            causal_projection(t - 1)

                rounds(pe, body)

            @block.scalar
            def _(act):
                def body(r):
                    def t_at(n):
                        return r.at(TUSES, n - TUSES)

                    if r.cau:
                        for f in range(PAIRS):
                            act.wait_ge(S["t_ps"], t_at(f + 1))
                            act.activation(kT[:, f, :], ps_t[:, :], ACT.Copy).then_inc(S["t_used"], 1)
                    for j in range(UN + 2):
                        t, h = divmod(j, 8)
                        if r.dia and j < UN:
                            act.wait_ge(S["d_bias"], r.at(UN, UN + j + 1))
                            act.wait_ge(S["d_exp"], r.at(UN, UN + j + 1))
                            act.activation(exp_out[j % 2][:, :], ps_d[j % 2][:, :], ACT.Exp, bias=d_bias[:, j:j + 1], scale=SCALE,
                                           accum_out=d_sums[:, j:j + 1]).then_inc(S["d_exp"], 1)
                        if r.cau:
                            if j < UN:
                                w_ = (t + 1) * P
                                act.wait_ge(S["c_max"], r.at(UN, j + 1 - UN))
                                act.activation(prob[j % 2][:, 0:w_], ps_c[j % 2][:, 0:w_], ACT.Exp, bias=c_negmax[:, j:j + 1],
                                               accum_out=c_sums[:, j:j + 1]).then_inc(S["c_probs"], 1)
                            if 1 <= j <= UN:
                                u = j - 1
                                w_ = (u // HEADS2 + 1) * P
                                if u >= 2:
                                    act.wait_ge(S["o_ps"], r.at(OUSES, idx_values(u - 2) + 1 - OUSES))
                                act.wait_ge(S["t_ps"], t_at(idx_probs(u) + 1))
                                act.activation(probT[u % 2][:, 0:w_], ps_t[:, 0:w_], ACT.Copy).then_inc(S["t_used"], 1)
                        if j < UN and 2 <= h <= 4 and r.compared(t):
                            n = (t + 2 + r.early) % TT
                            act.wait_ge(S["f_ps"], r.front_uses(t) + h - 1)
                            if h < 4:
                                if h == 2:
                                    act.wait_ge(S["sim_used"], r.at(TT, t + 3 + r.early))
                                ins = act.activation(sim[n % 2][:, (h - 2) * HEADS2:(h - 1) * HEADS2, :], ps_f[:, :].rearrange("p (g k) -> p g k", k=NKEYS), ACT.Copy)
                                ins.then_inc(S["f_used"], 1)
                                if h == 3:
                                    act.wait_ge(S["f_used"], r.front_uses(t) + 3)
                                    act.sem_inc(S["sim_ready"], 1)
                            else:
                                past(act, S["c_scores"], r.at(UN, (1 - UN) if t < 2 else (8 * (t - 1) + 1 - UN)))
                                half = r.par if t < 2 and not r.early else 1 - r.par
                                act.activation(qT[half][:, :, n * P:(n + 1) * P], ps_f[:, :].rearrange("p (f t) -> p f t", t=P), ACT.Copy,
                                               scale=float(D) ** -0.5).then_inc(S["f_used"], 1)
                                act.wait_ge(S["f_used"], r.front_uses(t) + 4)
                                act.sem_inc(S["q_ready"], 1)
                        if j < UN and h == 5 and r.chosen(t):
                            act.wait_ge(S["best_centred"], r.at(TT, t + 2 + r.early))
                            wt = weight[(t + 1 + r.early) % 2]
                            act.activation(wt[:, :, :], wt[:, :, :], ACT.Exp).then_inc(S["weight_exp"], 1)
                        if j < UN and h == 7 and r.dia:
                            a = d_attn[:, t * HEADS1:(t + 1) * HEADS1]
                            act.wait_ge(S["d_pre"], r.at(TT, TT + t + 1))
                            act.activation(a, a, ACT.Exp).then_inc(S["d_attn"], 1)
                            act.wait_ge(S["moments_ready"], r.at(TT, TT + t + 1))
                            act.activation(std[:, :], moments[:, 1:2], ACT.Sqrt, bias=eps[:, 0:1]).then_inc(S["std_ready"], 1)
                            act.wait_ge(S["f_ps"], r.front_uses(t) + (3 if r.compared(t) else 0) + 1)
                            act.activation(xnT[:, t, :], ps_f[0:D, 0:P], ACT.Copy).then_inc(S["f_used"], 1)
                        if r.cau and j >= 9 and h == 1:
                            act.wait_ge(S["t_ps"], t_at(idx_outs(t - 1) + 1))
                            act.activation(outT[:, :, :], ps_t[:, :].rearrange("p (f t) -> p f t", t=P), ACT.Copy).then_inc(S["t_used"], 1)

                rounds(act, body)

            @block.vector
            def _(dve):
                s = Steps(dve, dve_steps)
                dve.sem_inc(S["sim_used"], 2)

                def diagonal_unit(r, u):
                    t = u // HEADS1
                    dve.wait_ge(S["d_scores"], r.at(UN, UN + u + 1))
                    s.did(dve.tensor_tensor(diag_out[u % 2][:, :], ps_d[u % 2][:, t * P:(t + 1) * P], ident[:, :], ALU.mult))
                    s.did(dve.tensor_reduce(d_negmax[:, u:u + 1], ps_d[u % 2][:, :], AX.X, ALU.max, negate=True))
                    s.wait()
                    s.did(dve.tensor_reduce(d_diag[:, u:u + 1], diag_out[u % 2][:, :], AX.X, ALU.add))
                    dve.tensor_scalar(d_bias[:, u:u + 1], d_negmax[:, u:u + 1], SCALE, None, ALU.mult).then_inc(S["d_bias"], 1)
                    if u % HEADS1 == HEADS1 - 1:
                        units = slice(u + 1 - HEADS1, u + 1)
                        s.wait()
                        dve.wait_ge(S["d_bias"], r.at(UN, UN + u + 1))
                        dve.scalar_tensor_tensor(d_attn[:, units], d_diag[:, units], SCALE, d_bias[:, units], ALU.mult, ALU.add).then_inc(S["d_pre"], 1)

                def diagonal_tile(r, t):
                    units = slice(t * HEADS1, (t + 1) * HEADS1)
                    dve.wait_ge(S["d_attn"], r.at(TT, TT + t + 1))
                    s.did(dve.reciprocal(d_sums[:, units], d_sums[:, units]))
                    s.did(dve.tensor_tensor(d_x[:, t, :], d_x[:, t, :], b0[:, :], ALU.add))
                    s.wait()
                    s.did(dve.tensor_tensor(d_attn[:, units], d_attn[:, units], d_sums[:, units], ALU.mult))
                    s.wait()
                    dve.wait_ge(S["d_vals"], r.at(TT, TT + t + 1))
                    s.did(dve.tensor_tensor(weighted[:, :, :], ps_v[:, :].rearrange("p (h o) -> p h o", o=D), bc(d_attn[:, units], 2, D), ALU.mult))
                    s.wait()
                    dve.sem_inc(S["d_vals_used"], 1)
                    dve.wait_ge(mid_stored[t], r.at(16, 32))
                    s.did(dve.tensor_reduce(mid[:, t, :], weighted[:, :, :].rearrange("p h o -> p o h"), AX.X, ALU.add))
                    s.wait()
                    s.did(dve.tensor_tensor(mid[:, t, :], mid[:, t, :], d_x[:, t, :], ALU.add))
                    s.wait()
                    dve.sem_inc(S["mid_ready"], 1)
                    if t == TT - 1:
                        dve.sem_inc(S["d_used"], 1)
                    s.did(dve.bn_stats(stats[:, :], mid[:, t, :]))
                    s.wait()
                    s.did(dve.bn_aggr(moments[:, :], stats[:, :]))
                    s.wait()
                    dve.sem_inc(S["moments_ready"], 1)
                    dve.wait_ge(S["std_ready"], r.at(TT, TT + t + 1))
                    s.did(dve.reciprocal(std[:, :], std[:, :]))
                    past(dve, S["f_ps"], r.front_uses(t))
                    s.wait()
                    s.did(dve.tensor_scalar(xn[:, :], mid[:, t, :], moments[:, 0:1], std[:, 0:1], ALU.subtract, ALU.mult))
                    s.wait()
                    dve.sem_inc(S["xn_ready"], 1)

                def best8(groups, values, at, source, rest):
                    for g in range(groups):
                        s.did(dve.max(values[:, g, 0:8], source[:, g, :]))
                    s.wait()
                    for g in range(groups):
                        s.did(dve.match_replace(rest[:, g, :], values[:, g, 0:8], source[:, g, :], LOW))
                        s.did(dve.max_index(at[:, g, 0:8], values[:, g, 0:8], source[:, g, :]))
                    s.wait()

                def next8(groups, values, at, rest):
                    for g in range(groups):
                        s.did(dve.max(values[:, g, 8:16], rest[:, g, :]))
                    s.wait()
                    for g in range(groups):
                        s.did(dve.max_index(at[:, g, 8:16], values[:, g, 8:16], rest[:, g, :]))
                    s.wait()

                def candidates():
                    s.did(dve.tensor_copy(top_at_f[:, :, :], top_at[:, :, :]))
                    s.wait()
                    second = top_at_f[:, HEADS2:GROUPS, :]
                    s.did(dve.tensor_scalar(second, second, float(NKEYS), None, ALU.mult))
                    s.wait()
                    s.did(dve.tensor_tensor(second, second, bc(head_base[:, :], 2, TOPK), ALU.add))
                    s.wait()
                    at = 0
                    for a0, a1, nb in RUNS:
                        na = a1 - a0
                        for src, dst in ((top, cand), (top_at_f, cand_row)):
                            s.did(dve.tensor_tensor(
                                dst[:, :, at:at + na * nb].rearrange("p h (a b) -> p h a b", b=nb),
                                bc(src[:, 0:HEADS2, a0:a1], 3, nb), bc(src[:, HEADS2:GROUPS, 0:nb], 2, na), ALU.add))
                        at += na * nb
                    s.wait()

                def table_rows(heads):
                    for h in heads:
                        eq = is_cand[h % 2][:, :, :]
                        s.did(dve.tensor_tensor(eq, bc(cand_id[:, :], 1, TOPK), bc(best_at_f[:, h, :], 2, CANDS), ALU.is_equal))
                        s.wait()
                        s.did(dve.tensor_tensor(eq, eq, bc(cand_row[:, h, :], 1, TOPK), ALU.mult))
                        s.wait()
                        s.did(dve.tensor_reduce(row_f[:, h, :], eq, AX.X, ALU.add))
                    s.wait()

                def choose(r, t, piece):
                    b = (t + 1 + r.early) % 2
                    if piece == 0:
                        held(dve, S["sim_ready"], r.at(TT, t + 2 + r.early), dve_passed)
                        best8(GROUPS, top, top_at, sim[b], sim_rest)
                        dve.sem_inc(S["sim_used"], 1)
                    elif piece == 1:
                        next8(GROUPS, top, top_at, sim_rest)
                    elif piece == 2:
                        candidates()
                    elif piece == 3:
                        best8(HEADS2, best, best_at, cand, cand_rest)
                    elif piece == 4:
                        next8(HEADS2, best, best_at, cand_rest)
                        dve.tensor_tensor(weight[b][:, :, :], best[:, :, :], best[:, :, 0:1].broadcast_to([P, HEADS2, TOPK]), ALU.subtract).then_inc(S["best_centred"], 1)
                        s.did(dve.tensor_copy(best_at_f[:, :, :], best_at[:, :, :]))
                        s.wait()
                    elif piece == 5:
                        table_rows(range(HEADS2 // 2))
                    elif piece == 6:
                        table_rows(range(HEADS2 // 2, HEADS2))
                        s.did(dve.tensor_copy(row[b][:, :, :], row_f[:, :, :]))
                        s.wait()
                        dve.sem_inc(S["row_ready"], 1)
                        dve.wait_ge(S["weight_exp"], r.at(TT, t + 2 + r.early))
                        s.did(dve.tensor_reduce(wsum[:, :], weight[b][:, :, :], AX.X, ALU.add))
                        s.wait()
                        s.did(dve.reciprocal(wsum[:, :], wsum[:, :]))
                        s.wait()
                        s.did(dve.tensor_tensor(weight[b][:, :, :], weight[b][:, :, :], bc(wsum[:, :], 2, TOPK), ALU.mult))
                        s.wait()

                def mix(r, u):
                    t, h = divmod(u, HEADS2)
                    slot = rows[u % GSLOTS]
                    dve.wait_ge(gathered[u % GSLOTS], r.at(16 * TOPK * UN // GSLOTS, 16 * TOPK * (u // GSLOTS + 1)))
                    s.did(dve.tensor_tensor(slot[:, :, :], slot[:, :, :], bc(weight[t % 2][:, h, :], 2, KV), ALU.mult))
                    s.wait()
                    s.did(dve.tensor_reduce(kv[r.par][:, t, :, h, :], slot[:, :, :].rearrange("p j (m c) -> p m c j", m=2), AX.X, ALU.add))
                    s.wait()
                    dve.sem_inc(S["rows_used"], 1)
                    if u == UN - 1:
                        dve.sem_inc(S["kv_ready"], 1)

                def causal_max(r, u):
                    w_ = (u // HEADS2 + 1) * P
                    dve.wait_ge(S["c_scores"], r.at(UN, u + 2 - UN))
                    dve.tensor_reduce(c_negmax[:, u:u + 1], ps_c[u % 2][:, 0:w_], AX.X, ALU.max, negate=True).then_inc(S["c_max"], 1)

                def causal_normalise(r, u):
                    t, h = divmod(u, HEADS2)
                    dve.wait_ge(S["o_ps"], r.at(OUSES, idx_values(u) + 1 - OUSES))
                    s.did(dve.reciprocal(c_inv[:, u:u + 1], c_sums[:, u:u + 1]))
                    s.wait()
                    dve.tensor_scalar(out[t % 2][:, h, :], ps_o[:, 0:D], c_inv[:, u:u + 1], None, ALU.mult).then_inc(S["o_used"], 1)

                def causal_tile(r, t):
                    if t == 0:
                        dve.wait_ge(S["c_in"], r.at(16, 0))
                        dve.wait_ge(S["y_stored"], r.at(16, 0))
                    dve.wait_ge(S["o_ps"], r.at(OUSES, idx_values(8 * t + 7) + 2 - OUSES))
                    dve.tensor_tensor(y[:, t, :], ps_o[:, 0:D], c_x[:, t, :], ALU.add).then_inc(S["o_used"], 1)
                    if t == TT - 1:
                        dve.wait_ge(S["o_used"], r.at(OUSES, 1))
                        dve.sem_inc(S["y_ready"], 1)
                        dve.sem_inc(S["c_used"], 1)

                def body(r):
                    if r.dia:
                        held(dve, S["d_in"], r.at(64, 128), dve_passed)
                    for j in range(UN + 2):
                        t, h = divmod(j, 8)
                        if r.dia and j < UN:
                            diagonal_unit(r, j)
                        if j < UN and r.chosen(t):
                            choose(r, t, h)
                        if r.cau and j < UN:
                            causal_max(r, j)
                        if r.cau and j >= 2:
                            causal_normalise(r, j - 2)
                        if r.mix and j < UN:
                            mix(r, j)
                        if r.cau and j >= 9 and h == 1:
                            causal_tile(r, t - 1)
                        if r.dia and j < UN and h == 7:
                            diagonal_tile(r, t)
                    s.restart()

                rounds(dve, body)

        clear_semaphores(nc, sems)


LAID = (["x"] + ["L0_tok_" + n for n in (
    "emb_byteT hash_rows Wq bq conv_w conv_b Win b_in Wg bg Wi bi WoT bo ln_g ln_b mlp_w mlp_bT Wout bout").split()]
        + ["L0_attn_" + n for n in "WqT bq WkT bk WvT bv WoT bo shift_logits alibi_slope".split()]
        + ["L0_ffn_" + n for n in "W1 b1 Wg bg Wd bd".split()]
        + ["L1_attn_" + n for n in "Wqkv_heads bqkv_heads W0_heads b0".split()]
        + ["L1_ffn_" + n for n in "Wq_pkT keysT Wq table Wo".split()])
def build(nc, a, out):
    outs = [nc.dram_tensor(f"h{n}", (NTOK, D), F32, kind="Internal").ap() for n in range(4)] + [out]
    tok = {k[7:]: v for k, v in a.items() if k.startswith("L0_tok_")}
    xpad = nc.dram_tensor("chars_padded", (B, WMAX + T), I32, kind="Internal").ap()
    pad_chars(nc, a["x"], xpad)
    tower_tok(nc, tok, a["x"], xpad, outs[0])
    shifted_attention(nc, {k[8:]: v for k, v in a.items() if k.startswith("L0_attn_")}, outs[0], outs[1])
    at1 = {k[8:]: v for k, v in a.items() if k.startswith("L1_attn_")}
    qkvT = nc.dram_tensor("qkvT", (PAIRS, P, ROWS3), F32, kind="Internal").ap()
    experts_and_projection(nc, {k[7:]: v for k, v in a.items() if k.startswith("L0_ffn_")}, at1, outs[1], outs[2], qkvT)
    ff1 = {k[7:]: v for k, v in a.items() if k.startswith("L1_ffn_")}
    sequence_pipeline(nc, at1, ff1, qkvT, outs[2], outs[3], outs[4])


def kernel(**inputs):
    import numpy as np
    import concourse.bacc as bacc
    from concourse.bass_utils import run_bass_kernel_spmd

    laid = {k: np.asarray(v) for k, v in inputs.items()}
    t = {}
    t["L0_tok_emb_byteT"] = laid["L0_tok_emb_byte"].T
    t["L0_tok_WoT"] = laid["L0_tok_Wo"].T
    t["L0_tok_mlp_bT"] = laid["L0_tok_mlp_b"].T
    t["L0_tok_hash_rows"] = laid["L0_tok_hash_tables"].reshape(NW * HASH_MOD, E_TOK)
    for n in "qkvo":
        t[f"L0_attn_W{n}T"] = laid[f"L0_attn_W{n}"].T
    t["L1_attn_Wqkv_heads"] = laid["L1_attn_Wqkv"].reshape(D, 3, D, HEADS1).transpose(0, 1, 3, 2).reshape(D, -1)
    t["L1_attn_bqkv_heads"] = laid["L1_attn_bqkv"].reshape(3, D, HEADS1).transpose(0, 2, 1).reshape(-1)
    t["L1_attn_W0_heads"] = laid["L1_attn_W0"].reshape(D, HEADS1, D).transpose(1, 0, 2)
    t["L1_ffn_Wq_pkT"] = laid["L1_ffn_Wq_pk"].reshape(D, GROUPS, DKEY).transpose(2, 1, 0)
    t["L1_ffn_keysT"] = laid["L1_ffn_pk_keys"].transpose(3, 0, 2, 1).reshape(DKEY, GROUPS, NKEYS)
    t["L1_ffn_table"] = np.concatenate([laid["L1_ffn_keys_table"], laid["L1_ffn_values_table"]], axis=1)
    laid.update(t)
    nc = bacc.Bacc("TRN2", target_bir_lowering=False, num_devices=1)
    arrays, aps = {}, {}
    for name in LAID:
        v = np.ascontiguousarray(laid[name])
        arrays["in_" + name] = v
        aps[name] = nc.dram_tensor("in_" + name, v.shape, mybir.dt.from_np(v.dtype), kind="ExternalInput").ap()
    out = nc.dram_tensor("out_0", (NTOK, D), F32, kind="ExternalOutput").ap()
    build(nc, aps, out)
    r = run_bass_kernel_spmd(nc, [arrays], core_ids=[0]).results[0]
    return r["out_0"].reshape(B, T, D)
```
